# Optimizing a Trainium2 kernel written in Bass

```python
import numpy as np
import jax
import jax.numpy as jnp

def _softmax(x, axis=-1):
    return jax.nn.softmax(x, axis=axis)

def _gelu(x):
    return jax.nn.gelu(x, approximate=True)

def _silu(x):
    return jax.nn.silu(x)

def _sigmoid(x):
    return jax.nn.sigmoid(x)

def _layernorm(x, axis=-1, eps=1e-05):
    m = jnp.mean(x, axis=axis, keepdims=True)
    v = jnp.var(x, axis=axis, keepdims=True)
    return (x - m) / jnp.sqrt(v + eps)

def _scatter_add(tgt, idx, src, axis=0):
    return tgt.at[idx].add(src)

def _segment_sum(src, seg, n):
    return jax.ops.segment_sum(src, seg, n)
kernel_name = 'mk_gnn_preln_d2_gnn_r16_5cc7c0'

def setup_inputs(seed: int=0):
    np.random.seed(seed)
    _w = jnp.asarray

    def _rec_inputs():
        import jax
        import jax.numpy as jnp
        _gk = jax.random.key(seed)
        x = -0.0001394 + 0.9999 * jax.random.normal(jax.random.fold_in(_gk, 1), (3125, 768), jnp.float32)
        src = jax.random.randint(jax.random.fold_in(_gk, 2), (50000,), 0, 3125, jnp.int32)
        dst = jax.random.randint(jax.random.fold_in(_gk, 3), (50000,), 0, 3125, jnp.int32)
        _o = jnp.argsort(dst, stable=True)
        src = src[_o]
        dst = dst[_o]
        return (x, src, dst)
    x, src, dst = _rec_inputs()

    def _L0_gnn_setup():
        import jax, jax.numpy as jnp
        import numpy as np
        N_NODES = 3125

        def gcn_conv(x, edge_index, W, b, n_nodes):
            src = edge_index[0]
            dst = edge_index[1]
            loop = jnp.arange(n_nodes, dtype=src.dtype)
            src = jnp.concatenate([src, loop])
            dst = jnp.concatenate([dst, loop])
            deg = jax.ops.segment_sum(jnp.ones(src.shape, x.dtype), dst, num_segments=n_nodes)
            dinv = jnp.where(deg > 0, jax.lax.rsqrt(deg), jnp.zeros_like(deg))
            norm = dinv[src] * dinv[dst]
            h = x @ W.T
            msg = h[src] * norm[:, None]
            out = jax.ops.segment_sum(msg, dst, num_segments=n_nodes)
            return out + b
        key = jax.random.key(seed)
        k1, k2, k3, k4 = jax.random.split(key, 4)
        d = 768
        n_edges = 12500
        s = 1.0 / np.sqrt(d)
        return {'x': jax.random.normal(k1, (N_NODES, d), dtype=jnp.float32), 'edge_index': jax.random.randint(k2, (2, n_edges), 0, N_NODES, dtype=jnp.int64), 'W1': jax.random.normal(k3, (d, d), dtype=jnp.float32) * s, 'b1': jnp.zeros((d,), jnp.float32), 'W2': jax.random.normal(k4, (d, d), dtype=jnp.float32) * s, 'b2': jnp.zeros((d,), jnp.float32)}
    _L0_gnn_all = _L0_gnn_setup()
    _L0_gnn_in = {k: v for k, v in _L0_gnn_all.items() if k in ('W1', 'b1', 'W2', 'b2')}
    del _L0_gnn_all

    def _L1_gnn_setup():
        import jax, jax.numpy as jnp
        import numpy as np
        N = 3125
        E = 15625
        H = 12
        D = 64
        NEG_SLOPE = 0.2
        key = jax.random.key(seed)
        k1, k2, k3, k4, k5, k6, k7 = jax.random.split(key, 7)
        h = jax.random.normal(k1, (N, H * D), dtype=jnp.float32)
        src = jnp.concatenate([jnp.arange(N, dtype=jnp.int32), jax.random.randint(k2, (E - N,), 0, N, dtype=jnp.int32)])
        dst = jnp.concatenate([jnp.arange(N, dtype=jnp.int32), jax.random.randint(k3, (E - N,), 0, N, dtype=jnp.int32)])
        xav = 1.414 / np.sqrt(D)
        W_fc = jax.random.normal(k4, (D, D), dtype=jnp.float32) * xav
        attn_l = jax.random.normal(k5, (H, D), dtype=jnp.float32) * 0.15
        attn_r = jax.random.normal(k6, (H, D), dtype=jnp.float32) * 0.15
        W_res = jax.random.normal(k7, (D, D), dtype=jnp.float32) * xav
        return {'h': h, 'W_fc': W_fc, 'attn_l': attn_l, 'attn_r': attn_r, 'W_res': W_res, 'src': src, 'dst': dst}
    _L1_gnn_all = _L1_gnn_setup()
    _L1_gnn_in = {k: v for k, v in _L1_gnn_all.items() if k in ('W_fc', 'attn_l', 'attn_r', 'W_res')}
    del _L1_gnn_all
    return {'x': x, 'src': src, 'dst': dst, 'L0_gnn_W1': _L0_gnn_in['W1'], 'L0_gnn_b1': _L0_gnn_in['b1'], 'L0_gnn_W2': _L0_gnn_in['W2'], 'L0_gnn_b2': _L0_gnn_in['b2'], 'L1_gnn_W_fc': _L1_gnn_in['W_fc'], 'L1_gnn_attn_l': _L1_gnn_in['attn_l'], 'L1_gnn_attn_r': _L1_gnn_in['attn_r'], 'L1_gnn_W_res': _L1_gnn_in['W_res']}

def reference(x, src, dst, L0_gnn_W1, L0_gnn_b1, L0_gnn_W2, L0_gnn_b2, L1_gnn_W_fc, L1_gnn_attn_l, L1_gnn_attn_r, L1_gnn_W_res):
    import jax
    import jax.numpy as jnp

    def _L0_gnn_ref(x, edge_index, W1, b1, W2, b2):
        import jax, jax.numpy as jnp
        import numpy as np
        N_NODES = 3125

        def gcn_conv(x, edge_index, W, b, n_nodes):
            src = edge_index[0]
            dst = edge_index[1]
            loop = jnp.arange(n_nodes, dtype=src.dtype)
            src = jnp.concatenate([src, loop])
            dst = jnp.concatenate([dst, loop])
            deg = jax.ops.segment_sum(jnp.ones(src.shape, x.dtype), dst, num_segments=n_nodes)
            dinv = jnp.where(deg > 0, jax.lax.rsqrt(deg), jnp.zeros_like(deg))
            norm = dinv[src] * dinv[dst]
            h = x @ W.T
            msg = h[src] * norm[:, None]
            out = jax.ops.segment_sum(msg, dst, num_segments=n_nodes)
            return out + b
        h = gcn_conv(x, edge_index, W1, b1, N_NODES)
        h = jax.nn.relu(h)
        out = gcn_conv(h, edge_index, W2, b2, N_NODES)
        return out

    def _L1_gnn_ref(h, W_fc, attn_l, attn_r, W_res, src, dst):
        import jax, jax.numpy as jnp
        import numpy as np
        N = 3125
        E = 15625
        H = 12
        D = 64
        NEG_SLOPE = 0.2
        n = h.shape[0]
        hh = h.reshape(n, H, D)
        ft = jnp.einsum('nhd,ed->nhe', hh, W_fc)
        a1 = jnp.einsum('nhd,hd->nh', ft, attn_l)
        a2 = jnp.einsum('nhd,hd->nh', ft, attn_r)
        e = jax.nn.leaky_relu(a1[src] + a2[dst], negative_slope=NEG_SLOPE)
        m = jax.ops.segment_max(e, dst, num_segments=n)
        ee = jnp.exp(e - m[dst])
        denom = jax.ops.segment_sum(ee, dst, num_segments=n)
        alpha = ee / denom[dst]
        agg = jax.ops.segment_sum(alpha[:, :, None] * ft[src], dst, num_segments=n)
        res = jnp.einsum('nhd,ed->nhe', hh, W_res)
        return jax.nn.relu((res + agg).reshape(n, H * D))
    edge_index = jnp.stack([src, dst])
    h = jnp.maximum(_layernorm(x, axis=-1), 0.0)
    x = x + _L0_gnn_ref(h, edge_index, L0_gnn_W1, L0_gnn_b1, L0_gnn_W2, L0_gnn_b2)
    h = jnp.maximum(_layernorm(x, axis=-1), 0.0)
    x = x + _L1_gnn_ref(h, L1_gnn_W_fc, L1_gnn_attn_l, L1_gnn_attn_r, L1_gnn_W_res, src, dst)
    return x

_drawn_inputs = setup_inputs


def setup_inputs(seed=0):
    import zlib

    import numpy as np

    out = dict(_drawn_inputs(seed))
    spreads = {'L0_gnn_b1': (0.0, 0.1), 'L0_gnn_b2': (0.0, 0.1)}
    factors = {}
    for name, (base, spread) in spreads.items():
        noise = np.random.default_rng([zlib.crc32(name.encode()), seed]).standard_normal(out[name].shape)
        drawn = base * np.exp(spread * noise) if base else spread * noise
        out[name] = jnp.asarray(drawn.astype(out[name].dtype))
    for name, factor in factors.items():
        out[name] = (out[name] * factor).astype(out[name].dtype)
    return out
```

```python
from contextlib import ExitStack

import concourse.bass as bass
from concourse import mybir

F32 = mybir.dt.float32
BF16 = mybir.dt.bfloat16
I32 = mybir.dt.int32
ALU = mybir.AluOpType
ACT = mybir.ActivationFunctionType
ds = bass.ds

P = 128
N = 3125
D = 768
E = 50000
H = 12
DH = D // H
NT = -(-N // P)
LAST = N - (NT - 1) * P
NCH = -(-E // P)
V = NCH + NT
RING = 8
PAIR = 2 * RING
AHEAD = 4
NPS = 4
KB = D // P
HALVES = [(0, 512), (512, D - 512)]
CB = -(-NCH // P)
EB = E // P // P
EPS = 1e-5
SLOPE = 0.2
BIG = 3.0e38
HCOLS = NCH
HSTEP = 17
HFULL = E // P
HREST = E - HFULL * P
XG = 5
GRP = V // RING
SG = 8
SW = V // SG
SPT = SG * H
SL = SW * P
assert V % PAIR == 0 and HCOLS % HSTEP == 0 and NT % XG == 0 and V % SG == 0 and SW % 4 == 0


def gnn_kernel(nc, x, src, dst, w1t, b1, w2t, b2, wfc, wfct, attn_lt, attn_rt, wrest, out):
    ctx = ExitStack()


    def sb(stack, name, shape, dt=F32):
        return stack.enter_context(nc.sbuf_tensor(name, shape, dt))

    def pb(stack, name, cols=512, dt=F32):
        return stack.enter_context(nc.psum_tensor(name, [P, cols], dt))

    def sem(stack, name):
        return stack.enter_context(nc.semaphore(name))

    def chained(eng, s):
        n = [0]

        def link(ins):
            n[0] += 1
            ins.then_inc(s, 1)
            eng.wait_ge(s, n[0])
        return link

    with ctx:
        table1 = nc.dram_tensor("table1", (NT * P, D), F32).ap()
        table2 = nc.dram_tensor("table2", (NT * P, D), F32).ap()
        table3 = nc.dram_tensor("table3", (NT * P, D), F32).ap()
        a1_table = nc.dram_tensor("a1_table", (NT * P, H), F32).ap()
        x1_table = nc.dram_tensor("x1_table", (NT * P, D), F32).ap()
        res_table = nc.dram_tensor("res_table", (NT * P, D), F32).ap()

        def by_tile(t):
            return t.rearrange("(t p) d -> p t d", p=P)

        nodes = sb(ctx, "nodes", [P, NT, D])
        ident = sb(ctx, "ident", [P, P])
        iota1 = sb(ctx, "iota1", [P, P])
        dl1 = sb(ctx, "dl1", [P, V + RING])
        d1v = sb(ctx, "d1v", [P, V])
        idx = sb(ctx, "idx", [P, V], I32)
        tile_of = sb(ctx, "tile_of", [1, V], I32)
        dinv = sb(ctx, "dinv", [P, NT])
        idx_slot = [sb(ctx, f"idx_slot{h}", [P, RING], I32) for h in range(2)]




        with ExitStack() as st:
            hist_dst = sb(st, "hist_dst", [P, HCOLS], I32)
            lo_i = sb(st, "lo_i", [P, HCOLS], I32)
            hi_i = sb(st, "hi_i", [P, HCOLS], I32)
            lo = sb(st, "lo", [P, HCOLS])
            hi = sb(st, "hi", [P, HCOLS])
            hi_hot = sb(st, "hi_hot", [P, HCOLS, NT], BF16)
            lo_hot = sb(st, "lo_hot", [P, 2, HSTEP, P], BF16)
            iota0b = sb(st, "iota0b", [P, P], BF16)
            iota_nt = sb(st, "iota_nt", [P, NT])
            iota_v = sb(st, "iota_v", [P, V])
            rowno = sb(st, "rowno", [P, CB])
            zeros_b = sb(st, "zeros_b", [P, P], BF16)
            ones = sb(st, "ones", [P, P])
            tri = sb(st, "tri", [NT, NT])
            src_i = sb(st, "src_i", [P, CB, P], I32)
            dst_i = sb(st, "dst_i", [P, CB, P], I32)
            src_f = sb(st, "src_f", [P, CB, P])
            dst_f = sb(st, "dst_f", [P, CB, P])
            counts = sb(st, "counts", [P, NT])
            c = sb(st, "c", [NT, 16])
            ci = sb(st, "ci", [NT, 4], I32)
            at_least = sb(st, "at_least", [NT, V])
            sel = sb(st, "sel", [NT, V])
            off_b = sb(st, "off_b", [NT, P])
            tile_b = sb(st, "tile_b", [NT, P])
            chunk_v = sb(st, "chunk_v", [P, V])
            chunk_hot = sb(st, "chunk_hot", [P, CB, V])
            stats = sb(st, "stats", [P, NT, 2, 6])
            mv = sb(st, "mv", [P, NT, 2])
            std = sb(st, "std", [P, NT])
            sc = sb(st, "sc", [P, NT])
            bi = sb(st, "bi", [P, NT])
            ps_h = pb(st, "ps_h", NT)
            ps_c = pb(st, "ps_c")
            ps_off = pb(st, "ps_off")
            ps_tile = pb(st, "ps_tile")
            ps_d = pb(st, "ps_d")
            ps_s = pb(st, "ps_s")
            s_fill = sem(st, "s_fill")
            s_hd = sem(st, "s_hd")
            s_ed = sem(st, "s_ed")
            s_x = [sem(st, f"s_x{g}") for g in range(NT // XG)]
            s_pool = sem(st, "s_pool")
            s_dve = sem(st, "s_dve")
            s_lo = sem(st, "s_lo")
            s_hdone = sem(st, "s_hdone")
            s_counts = sem(st, "s_counts")
            s_pe = sem(st, "s_pe")
            s_step = sem(st, "s_step")
            s_sqrt = sem(st, "s_sqrt")
            s_var = sem(st, "s_var")
            s_scale = sem(st, "s_scale")
            s_row = sem(st, "s_row")
            s_st = sem(st, "s_st")
            FILL = 5
            POOL = 10
            with nc.Block() as block:

                @block.sync
                def _(eng):
                    eng.wait_ge(s_fill, FILL)
                    eng.dma_start(hist_dst[:, 0:HFULL], dst[0:HFULL * P].rearrange("(p c) -> p c", p=P)).then_inc(s_hd, 16)
                    eng.dma_start(hist_dst[0:HREST, HFULL:HCOLS], dst[HFULL * P:E].rearrange("(p c) -> p c", c=1)).then_inc(s_hd, 16)
                    whole = EB * P * P
                    rows = (E - whole) // P
                    for v, t in ((src, src_i), (dst, dst_i)):
                        eng.dma_start(t[:, 0:EB, :], v[0:whole].rearrange("(b q e) -> q b e", q=P, e=P)).then_inc(s_ed, 16)
                        eng.dma_start(t[0:rows, EB, :], v[whole:whole + rows * P].rearrange("(q e) -> q e", e=P)).then_inc(s_ed, 16)
                        eng.dma_start(t[rows:rows + 1, EB, 0:E - whole - rows * P], v[whole + rows * P:E].rearrange("(a e) -> a e", a=1)).then_inc(s_ed, 16)
                    for g in range(NT // XG):
                        r0, r1 = g * XG * P, min((g + 1) * XG * P, N)
                        full = (r1 - r0) // P
                        eng.dma_start(nodes[:, g * XG:g * XG + full, :], x[r0:r0 + full * P, :].rearrange("(t p) d -> p t d", p=P)).then_inc(s_x[g], 16)
                        if r0 + full * P < r1:
                            eng.dma_start(nodes[0:r1 - r0 - full * P, g * XG + full, :], x[r0 + full * P:r1, :]).then_inc(s_x[g], 16)

                @block.gpsimd
                def _(eng):
                    eng.memset(hist_dst[:, HFULL:HCOLS], -1).then_inc(s_fill, 1)
                    eng.memset(src_i[:, EB, :], 0).then_inc(s_fill, 1)
                    eng.memset(dst_i[:, EB, :], -1).then_inc(s_fill, 1)
                    eng.memset(nodes[:, NT - 1, :], 0.0).then_inc(s_fill, 1)
                    eng.memset(zeros_b[:, :], 0.0).then_inc(s_fill, 1)
                    eng.iota(iota0b[:, :], pattern=[[1, P]], base=0, channel_multiplier=0, allow_small_or_imprecise_dtypes=True).then_inc(s_pool, 1)
                    eng.iota(iota_nt[:, :], pattern=[[1, NT]], base=0, channel_multiplier=0, allow_small_or_imprecise_dtypes=True).then_inc(s_pool, 1)
                    eng.iota(iota_v[:, :], pattern=[[1, V]], base=0, channel_multiplier=0, allow_small_or_imprecise_dtypes=True).then_inc(s_pool, 1)
                    eng.iota(rowno[:, :], pattern=[[P, CB]], base=0, channel_multiplier=1, allow_small_or_imprecise_dtypes=True).then_inc(s_pool, 1)
                    eng.iota(iota1[:, :], pattern=[[1, P]], base=1, channel_multiplier=0, allow_small_or_imprecise_dtypes=True).then_inc(s_pool, 1)
                    eng.memset(ones[:, :], 1.0).then_inc(s_pool, 1)
                    eng.memset(ident[:, :], 0.0).then_inc(s_pool, 1)
                    eng.memset(tri[:, :], 1.0).then_inc(s_pool, 1)
                    eng.wait_ge(s_pool, 8)
                    eng.affine_select(out=ident[:, :], in_=ident[:, :], compare_op=ALU.not_equal, fill=1.0, base=0,
                                      pattern=[[-1, P]], channel_multiplier=1).then_inc(s_pool, 1)
                    eng.affine_select(out=tri[:, :], in_=tri[:, :], compare_op=ALU.is_gt, fill=0.0, base=0,
                                      pattern=[[1, NT]], channel_multiplier=-1).then_inc(s_pool, 1)

                @block.vector
                def _(eng):
                    link = chained(eng, s_dve)
                    eng.wait_ge(s_pool, POOL)
                    link(eng.memset(dl1[:, V:V + RING], 0.0))
                    eng.wait_ge(s_hd, 32)
                    link(eng.tensor_single_scalar(lo_i[:, :], hist_dst[:, :], P - 1, ALU.bitwise_and))
                    link(eng.tensor_single_scalar(hi_i[:, :], hist_dst[:, :], P.bit_length() - 1, ALU.arith_shift_right))
                    link(eng.tensor_copy(lo[:, :], lo_i[:, :]))
                    link(eng.tensor_copy(hi[:, :], hi_i[:, :]))
                    link(eng.tensor_tensor(hi_hot[:, :, :], hi[:, :].unsqueeze(2).to_broadcast([P, HCOLS, NT]),
                                           iota_nt[:, :].unsqueeze(1).to_broadcast([P, HCOLS, NT]), ALU.is_equal))
                    with eng.Fori(0, HCOLS // HSTEP) as i:
                        eng.wait_ge(s_hdone, i + 1)
                        for k in range(HSTEP):
                            last = eng.tensor_scalar(lo_hot[:, ds(i % 2, 1), k, :], iota0b[:, :], lo[:, ds(i * HSTEP + k, 1)], None, ALU.is_equal)
                        last.then_inc(s_lo, 1)
                    for j in range(NT):
                        if j % XG == 0:
                            eng.wait_ge(s_x[j // XG], 32 if j == NT - XG else 16)
                        for h in range(2):
                            last = eng.bn_stats(stats[:, j, h, :], nodes[:, j, h * D // 2:(h + 1) * D // 2])
                    link(last)
                    for j in range(NT):
                        last = eng.bn_aggr(mv[:, j, :], stats[:, j, :, :])
                    link(last)
                    eng.tensor_scalar(std[:, :], mv[:, :, 1], EPS, None, ALU.add).then_inc(s_var, 1)
                    eng.wait_ge(s_hdone, 3 + HCOLS // HSTEP)
                    link(eng.tensor_copy(counts[:, :], ps_h[:, 0:NT]))
                    eng.tensor_scalar(dinv[:, :], counts[:, :], 1.0, None, ALU.add).then_inc(s_var, 1)
                    eng.sem_inc(s_counts, 1)
                    eng.wait_ge(s_sqrt, 2)
                    link(eng.reciprocal(dinv[:, :], dinv[:, :]))
                    link(eng.reciprocal(std[:, :], std[:, :]))
                    link(eng.tensor_tensor(sc[:, :], std[:, :], dinv[:, :], ALU.mult))
                    link(eng.scalar_tensor_tensor(out=bi[:, :], in0=mv[:, :, 0], scalar=-1.0, in1=sc[:, :], op0=ALU.mult, op1=ALU.mult))
                    eng.sem_inc(s_scale, 1)
                    CNT, T0, T1, CS, CE, NV, M0, M1, LASTV, OFF = range(10)

                    def col(k):
                        return c[:, k:k + 1]
                    eng.wait_ge(s_pe, 1)
                    link(eng.tensor_copy(col(CNT), ps_c[0:NT, 0:1]))
                    eng.sem_inc(s_step, 1)
                    eng.wait_ge(s_pe, 2)
                    link(eng.tensor_copy(col(T0), ps_c[0:NT, 1:2]))
                    link(eng.tensor_tensor(col(T1), col(T0), col(CNT), ALU.add))
                    link(eng.tensor_scalar(col(T1), col(T1), float(P - 1), None, ALU.add))
                    link(eng.tensor_copy(ci[:, 0:2], c[:, T0:T1 + 1]))
                    link(eng.tensor_single_scalar(ci[:, 2:4], ci[:, 0:2], P.bit_length() - 1, ALU.arith_shift_right))
                    link(eng.tensor_copy(c[:, CS:CE + 1], ci[:, 2:4]))
                    link(eng.tensor_tensor(col(NV), col(CE), col(CS), ALU.subtract))
                    link(eng.tensor_scalar(col(NV), col(NV), 1.0, None, ALU.max))
                    eng.sem_inc(s_step, 1)
                    eng.wait_ge(s_pe, 3)
                    link(eng.tensor_copy(col(M0), ps_c[0:NT, 2:3]))
                    link(eng.tensor_tensor(col(M1), col(M0), col(NV), ALU.add))
                    link(eng.tensor_scalar(col(LASTV), rowno[0:NT, 0:1], float(NT - 1), float(V), ALU.is_equal, ALU.mult))
                    link(eng.tensor_tensor(col(M1), col(M1), col(LASTV), ALU.max))
                    link(eng.tensor_tensor(col(OFF), col(CS), col(M0), ALU.subtract))
                    link(eng.tensor_scalar(at_least[:, :], iota_v[0:NT, :], col(M0), None, ALU.is_ge))
                    link(eng.scalar_tensor_tensor(out=sel[:, :], in0=iota_v[0:NT, :], scalar=col(M1), in1=at_least[:, :],
                                                  op0=ALU.is_lt, op1=ALU.mult))
                    link(eng.tensor_scalar(off_b[:, :], ones[0:NT, :], col(OFF), None, ALU.mult))
                    link(eng.tensor_scalar(tile_b[:, :], ones[0:NT, :], rowno[0:NT, 0:1], float(P), ALU.mult, ALU.mult))
                    eng.sem_inc(s_step, 1)
                    eng.wait_ge(s_pe, 4)
                    link(eng.tensor_tensor(chunk_v[:, :], ps_off[:, 0:V], iota_v[:, :], ALU.add))
                    for b in range(CB):
                        link(eng.tensor_scalar(chunk_hot[:, b, :], chunk_v[:, :], rowno[:, b:b + 1], None, ALU.is_equal))
                    eng.wait_ge(s_ed, 6 * 16)
                    link(eng.tensor_scalar(dst_f[:, :, :], dst_i[:, :, :], 1.0, None, ALU.add))
                    link(eng.tensor_copy(src_f[:, :, :], src_i[:, :, :]))
                    eng.sem_inc(s_step, 1)
                    eng.wait_ge(s_pe, 5)
                    link(eng.tensor_copy(d1v[:, :], ps_d[:, 0:V]))
                    link(eng.tensor_tensor(dl1[:, 0:V], d1v[:, :], ps_tile[:, 0:V], ALU.subtract))
                    link(eng.tensor_copy(idx[:, :], ps_s[:, 0:V]))
                    link(eng.tensor_scalar(tile_of[:, :], ps_tile[0:1, 0:V], 1.0 / P, None, ALU.mult))

                @block.tensor
                def _(eng):
                    eng.wait_ge(s_pool, POOL)
                    eng.wait_ge(s_fill, FILL)
                    eng.sem_inc(s_hdone, 1)
                    eng.matmul(ps_h[:, 0:NT], zeros_b[:, :], zeros_b[:, 0:NT], start=True, stop=True).then_inc(s_hdone, 1)
                    with eng.Fori(0, HCOLS // HSTEP) as i:
                        eng.wait_ge(s_lo, i + 1)
                        for k in range(HSTEP):
                            last = eng.matmul(ps_h[:, 0:NT], lo_hot[:, ds(i % 2, 1), k, :], hi_hot[:, ds(i * HSTEP + k, 1), :],
                                              start=False, stop=True, skip_group_check=True)
                        last.then_inc(s_hdone, 1)
                    eng.matmul(ps_h[:, 0:NT], zeros_b[:, :], zeros_b[:, 0:NT], start=False, stop=True,
                               skip_group_check=True).then_inc(s_hdone, 1)
                    eng.wait_ge(s_counts, 1)
                    eng.matmul(ps_c[0:NT, 0:1], counts[:, :], ones[:, 0:1], start=True, stop=True).then_inc(s_pe, 1)
                    eng.wait_ge(s_step, 1)
                    eng.matmul(ps_c[0:NT, 1:2], tri[:, :], c[:, 0:1], start=True, stop=True).then_inc(s_pe, 1)
                    eng.wait_ge(s_step, 2)
                    eng.matmul(ps_c[0:NT, 2:3], tri[:, :], c[:, 5:6], start=True, stop=True).then_inc(s_pe, 1)
                    eng.wait_ge(s_step, 3)
                    eng.matmul(ps_off[:, 0:V], off_b[:, :], sel[:, :], start=True, stop=True)
                    eng.matmul(ps_tile[:, 0:V], tile_b[:, :], sel[:, :], start=True, stop=True).then_inc(s_pe, 1)
                    eng.wait_ge(s_step, 4)
                    for t, ps in ((dst_f, ps_d), (src_f, ps_s)):
                        for b in range(CB):
                            last = eng.matmul(ps[:, 0:V], t[:, b, :], chunk_hot[:, b, :], start=(b == 0), stop=(b == CB - 1))
                    last.then_inc(s_pe, 1)

                @block.scalar
                def _(eng):
                    eng.wait_ge(s_var, 1)
                    eng.activation(std[:, :], std[:, :], ACT.Sqrt).then_inc(s_sqrt, 1)
                    eng.wait_ge(s_var, 2)
                    eng.activation(dinv[:, :], dinv[:, :], ACT.Sqrt).then_inc(s_sqrt, 1)
                    eng.wait_ge(s_scale, 1)
                    with eng.Fori(0, NT) as j:
                        eng.activation(nodes[:, ds(j, 1), :], nodes[:, ds(j, 1), :], ACT.Relu, bias=bi[:, ds(j, 1)],
                                       scale=sc[:, ds(j, 1)]).then_inc(s_row, 1)
                        eng.wait_ge(s_row, j + 1)
                        eng.dma_start(by_tile(table1)[:, ds(j, 1), :], nodes[:, ds(j, 1), :]).then_inc(s_st, 16)
                    eng.wait_ge(s_st, NT * 16)

        def gather_rows(eng, table, landed, rows_free, idx_ready, asked, dest):
            with eng.Fori(0, V // PAIR) as i:
                for h in range(2):
                    eng.wait_ge(rows_free, i * PAIR + h * RING + 1)
                    eng.tensor_copy(idx_slot[h][:, :], idx[:, ds(i * PAIR + h * RING, RING)]).then_inc(idx_ready, 1)
                    eng.wait_ge(idx_ready, i * 2 + h + 1)
                    for k in range(RING):
                        eng.wait_ge(rows_free, i * PAIR + h * RING + k + 1)
                        eng.sem_inc(asked, 1)
                        eng.indirect_dma_start(out=dest(k), out_offset=None, in_=table,
                                               in_offset=bass.IndirectOffsetOnAxis(ap=idx_slot[h][:, k:k + 1], axis=0)).then_inc(landed[k], 16)

        def sum_pass(tag, table):
            with ExitStack() as st:
                ring = sb(st, f"ring{tag}", [P, RING, D])
                onehot = sb(st, f"onehot{tag}", [P, RING, P])
                ps = [pb(st, f"ps_sum{tag}{k}", 1024) for k in range(NPS)]
                landed = [sem(st, f"landed{tag}{k}") for k in range(RING)]
                rows_free = sem(st, f"rows_free{tag}")
                idx_ready = sem(st, f"idx_ready{tag}")
                asked = sem(st, f"asked{tag}")
                hot_ready = sem(st, f"hot_ready{tag}")
                summed = sem(st, f"summed{tag}")
                added = sem(st, f"added{tag}")
                with nc.Block() as block:

                    @block.gpsimd
                    def _(eng):
                        gather_rows(eng, table, landed, rows_free, idx_ready, asked, lambda k: ring[:, k, :])

                    @block.tensor
                    def _(eng):
                        eng.sem_inc(rows_free, RING)
                        with eng.Fori(0, GRP) as i:
                            for k in range(RING):
                                eng.wait_ge(landed[k], i * 16 + 16)
                                eng.wait_ge(hot_ready, i * RING + k + 1)
                                eng.wait_ge(added, i * RING + k + 1)
                                eng.matmul(ps[k % NPS][:, 0:512], onehot[:, k, :], ring[:, k, 0:512], start=True, stop=True).then_inc(summed, 1)
                                eng.matmul(ps[k % NPS][:, 512:D], onehot[:, k, :], ring[:, k, 512:D], start=True, stop=True).then_inc(rows_free, 1)

                    @block.vector
                    def _(eng):
                        eng.sem_inc(added, NPS)

                        def hot(v, k):
                            eng.tensor_scalar(onehot[:, k, :], iota1[:, :], dl1[:, ds(v, 1)], None, ALU.is_equal).then_inc(hot_ready, 1)
                        for k in range(AHEAD):
                            hot(k, k)
                        with eng.Fori(0, GRP) as i:
                            for k in range(RING):
                                v = i * RING + k
                                tile = eng.value_load(tile_of[0:1, ds(v, 1)], min_val=0, max_val=NT - 1)
                                eng.wait_ge(rows_free, v + RING + 1)
                                acc = nodes[:, ds(tile, 1), :]
                                eng.wait_ge(added, v + NPS)
                                eng.tensor_tensor(acc, acc, ps[k % NPS][:, 0:D].unsqueeze(1), ALU.add).then_inc(added, 1)
                                hot(v + AHEAD, (k + AHEAD) % RING)

        def linear_pass(tag, wt, bias, first):
            with ExitStack() as st:
                w = sb(st, f"w{tag}", [P, KB, D])
                bias_b = sb(st, f"bias_b{tag}", [P, D])
                scaled = sb(st, f"scaled{tag}", [P, D])
                sum_t = sb(st, f"sum_t{tag}", [P, D])
                tmp = sb(st, f"tmp{tag}", [P, 2, D])
                xt = sb(st, f"xt{tag}", [P, 2, D])
                ps_t = pb(st, f"ps_t{tag}", 1024)
                ps_y = [pb(st, f"ps_y{tag}{k}", 1024) for k in range(2)]
                s_w = sem(st, f"s_w{tag}")
                s_scaled = sem(st, f"s_scaled{tag}")
                s_t = sem(st, f"s_t{tag}")
                s_tc = sem(st, f"s_tc{tag}")
                s_y = sem(st, f"s_y{tag}")
                s_b = sem(st, f"s_b{tag}")
                s_o = sem(st, f"s_o{tag}")
                s_st = sem(st, f"s_st{tag}")
                s_xl = [sem(st, f"s_xl{tag}{k}") for k in range(2)]
                def tcols(k):
                    return slice(k * P, (k + 1) * P)
                with nc.Block() as block:

                    @block.sync
                    def _(eng):
                        eng.dma_start(w[:, :, :], wt.rearrange("(k p) n -> p k n", p=P)).then_inc(s_w, 16)
                        eng.dma_start(bias_b[:, :], bias.rearrange("(a n) -> a n", a=1).to_broadcast([P, D])).then_inc(s_w, 16)
                        if not first:
                            for j in range(NT):
                                rows = P if j < NT - 1 else LAST
                                if j >= 2:
                                    eng.wait_ge(s_o, j)
                                eng.dma_start(xt[0:rows, j % 2, :], x[j * P:j * P + rows, :]).then_inc(s_xl[j % 2], 16)

                    @block.scalar
                    def _(eng):
                        if first:
                            eng.sem_inc(s_o, 1)
                        with eng.Fori(0, NT) as j:
                            eng.wait_ge(s_t, j + 1)
                            eng.activation(scaled[:, :], nodes[:, ds(j, 1), :].rearrange("p a d -> p (a d)"), ACT.Copy, scale=dinv[:, ds(j, 1)]).then_inc(s_scaled, 1)
                            if first:
                                eng.wait_ge(s_b, j + 2)
                                eng.activation(nodes[:, ds(j, 1), :], tmp[:, ds(j % 2, 1), :], ACT.Relu, scale=dinv[:, ds(j, 1)]).then_inc(s_o, 1)
                                eng.wait_ge(s_o, j + 2)
                                eng.dma_start(by_tile(table2)[:, ds(j, 1), :], nodes[:, ds(j, 1), :]).then_inc(s_st, 16)
                        if first:
                            eng.wait_ge(s_st, NT * 16)

                    @block.tensor
                    def _(eng):
                        eng.sem_inc(s_t, 1)
                        eng.sem_inc(s_y, 1)
                        eng.wait_ge(s_w, 32)

                        def step(j, par):
                            eng.wait_ge(s_scaled, j + 1)
                            for k in range(KB):
                                last = eng.transpose(ps_t[:, tcols(k)], scaled[:, tcols(k)], ident[:, :])
                            last.then_inc(s_t, 1)
                            eng.wait_ge(s_tc, j + 1)
                            for c0, n in HALVES:
                                for k in range(KB):
                                    last = eng.matmul(ps_y[par][:, c0:c0 + n], sum_t[:, tcols(k)], w[:, k, c0:c0 + n],
                                                      start=(k == 0), stop=(k == KB - 1))
                            last.then_inc(s_y, 1)
                        step(0, 0)
                        with eng.Fori(0, (NT - 1) // 2) as i:
                            for par in (1, 0):
                                j = i * 2 + (1 if par else 2)
                                eng.wait_ge(s_b, j)
                                step(j, par)

                    @block.vector
                    def _(eng):
                        def step(j, par):
                            eng.wait_ge(s_t, j + 2)
                            eng.wait_ge(s_y, j + 1)
                            eng.tensor_copy(sum_t[:, :], ps_t[:, 0:D]).then_inc(s_tc, 1)
                            eng.wait_ge(s_y, j + 2)
                            eng.wait_ge(s_o, max(j, 1) if isinstance(j, int) else j)
                            eng.tensor_tensor(tmp[:, par, :], ps_y[par][:, 0:D], bias_b[:, :], ALU.add).then_inc(s_b, 1)
                            if not first:
                                eng.wait_ge(s_b, j + 2)

                        def residual(j, par, need, rows=P):
                            eng.wait_ge(s_xl[par], need)
                            eng.tensor_tensor(nodes[0:rows, ds(j, 1), :], tmp[0:rows, ds(par, 1), :], xt[0:rows, ds(par, 1), :], ALU.add).then_inc(s_o, 1)
                        eng.sem_inc(s_b, 1)
                        if not first:
                            eng.sem_inc(s_o, 1)
                        eng.wait_ge(s_w, 32)
                        step(0, 0)
                        if not first:
                            residual(0, 0, 16)
                        with eng.Fori(0, (NT - 1) // 2 - 1) as i:
                            for par in (1, 0):
                                j = i * 2 + (1 if par else 2)
                                step(j, par)
                                if not first:
                                    residual(j, par, i * 16 + (16 if par else 32))
                        for j in (NT - 2, NT - 1):
                            step(j, j % 2)
                            if not first:
                                residual(j, j % 2, 16 * (j // 2 + 1), P if j < NT - 1 else LAST)

        sum_pass("a", table1)
        linear_pass("a", w1t, b1, True)
        sum_pass("b", table2)
        linear_pass("b", w2t, b2, False)

        a2 = sb(ctx, "a2", [P, NT, H])
        with ExitStack() as st:
            stats = sb(st, "stats2", [P, NT, 2, 6])
            mv = sb(st, "mv2", [P, NT, 2])
            std = sb(st, "std2", [P, NT])
            bi = sb(st, "bi2", [P, NT])
            wfc2 = sb(st, "wfc2", [DH, 2, DH])
            attn_t = sb(st, "attn_t", [DH, 2 * H])
            blk = sb(st, "blk", [P, 4, DH])
            att_w = sb(st, "att_w", [P, KB, 4])
            h2 = sb(st, "h2", [P, 2, D])
            h2_t = sb(st, "h2_t", [P, D])
            ft = sb(st, "ft", [P, 2, KB, P])
            res = sb(st, "res", [P, 2, KB, P])
            a1 = sb(st, "a1", [P, 2, H])
            ps_t = pb(st, "ps_t2", 1024)
            ps_f = pb(st, "ps_f", KB * 2 * P)
            ps_a = pb(st, "ps_a")
            s_w = sem(st, "s_w2")
            s_z = sem(st, "s_z2")
            s_var = sem(st, "s_var2")
            s_sqrt = sem(st, "s_sqrt2")
            s_dve = sem(st, "s_dve2")
            s_blk = sem(st, "s_blk2")
            s_fold = sem(st, "s_fold2")
            s_ready = sem(st, "s_ready2")
            s_h2 = sem(st, "s_h2")
            s_t = sem(st, "s_t2")
            s_tc = sem(st, "s_tc2")
            s_f = sem(st, "s_f2")
            s_fc = sem(st, "s_fc2")
            s_rc = sem(st, "s_rc2")
            s_fst = [sem(st, f"s_fst2{k}") for k in range(2)]
            s_rst = [sem(st, f"s_rst2{k}") for k in range(2)]
            s_x1 = sem(st, "s_x1")
            with nc.Block() as block:

                @block.sync
                def _(eng):
                    eng.dma_start(wfc2[:, 0, :], wfc).then_inc(s_w, 16)
                    eng.dma_start(wfc2[:, 1, :], wfc).then_inc(s_w, 16)
                    eng.dma_start(attn_t[:, 0:H], attn_lt).then_inc(s_w, 16)
                    eng.dma_start(attn_t[:, H:2 * H], attn_rt).then_inc(s_w, 16)
                    eng.wait_ge(s_z, 1)
                    for q, w in ((0, wfct), (2, wrest)):
                        eng.dma_start(blk[0:DH, q, :], w).then_inc(s_blk, 16)
                        eng.dma_start(blk[DH:P, q + 1, :], w).then_inc(s_blk, 16)
                    eng.dma_start(by_tile(x1_table), nodes[:, :, :]).then_inc(s_x1, 16)
                    with eng.Fori(0, NT // 2) as i:
                        for par in range(2):
                            eng.wait_ge(s_rc, i * 2 + par + 2)
                            eng.dma_start(by_tile(res_table)[:, ds(i * 2 + par, 1), :], res[:, par:par + 1, :, :].rearrange("p a k c -> p a (k c)")).then_inc(s_rst[par], 16)
                            eng.dma_start(by_tile(a1_table)[:, ds(i * 2 + par, 1), :], a1[:, par:par + 1, :]).then_inc(s_rst[par], 16)
                    eng.wait_ge(s_rc, NT + 1)
                    eng.dma_start(by_tile(res_table)[:, NT - 1:NT, :], res[:, 0:1, :, :].rearrange("p a k c -> p a (k c)")).then_inc(s_rst[0], 16)
                    eng.dma_start(by_tile(a1_table)[:, NT - 1:NT, :], a1[:, 0:1, :]).then_inc(s_rst[0], 16)
                    eng.wait_ge(s_rst[0], 32 * (NT // 2 + 1))
                    eng.wait_ge(s_rst[1], 32 * (NT // 2))
                    eng.wait_ge(s_x1, 16)

                @block.vector
                def _(eng):
                    link = chained(eng, s_dve)
                    eng.memset(att_w[:, :, :], 0.0)
                    eng.memset(blk[:, :, :], 0.0).then_inc(s_z, 1)
                    eng.wait_ge(s_z, 1)
                    for j in range(NT):
                        for h in range(2):
                            last = eng.bn_stats(stats[:, j, h, :], nodes[:, j, h * D // 2:(h + 1) * D // 2])
                    link(last)
                    for j in range(NT):
                        last = eng.bn_aggr(mv[:, j, :], stats[:, j, :, :])
                    link(last)
                    eng.tensor_scalar(std[:, :], mv[:, :, 1], EPS, None, ALU.add).then_inc(s_var, 1)
                    eng.wait_ge(s_fold, 1)
                    for half, which in ((0, 0), (1, 1)):
                        rows = slice(half * DH, half * DH + DH)
                        for side in range(2):
                            v = ps_a[rows, side * H:(side + 1) * H].rearrange("p (k t) -> p k t", t=2)
                            last = eng.tensor_copy(att_w[rows, :, 2 * side + which], v[:, :, which])
                    link(last)
                    eng.wait_ge(s_sqrt, 1)
                    link(eng.reciprocal(std[:, :], std[:, :]))
                    link(eng.scalar_tensor_tensor(out=bi[:, :], in0=mv[:, :, 0], scalar=-1.0, in1=std[:, :], op0=ALU.mult, op1=ALU.mult))
                    eng.sem_inc(s_ready, 1)

                    def step(j, par, stored):
                        eng.wait_ge(s_t, j + 2)
                        eng.wait_ge(s_f, j + 1)
                        eng.tensor_copy(h2_t[:, :], ps_t[:, 0:D]).then_inc(s_tc, 1)
                        eng.wait_ge(s_f, j + 2)
                        eng.wait_ge(s_fc, j + 2)
                        if stored is not None:
                            eng.wait_ge(s_rst[par], stored)
                        eng.tensor_copy(res[:, par, :, :], ps_f[:, :].rearrange("p (k c) -> p k c", c=2 * P)[:, :, P:2 * P])
                        eng.tensor_copy(a1[:, par, :].rearrange("p (k t) -> p k t", t=2), ps_a[:, 0:4 * KB].rearrange("p (k t) -> p k t", t=4)[:, :, 0:2])
                        eng.tensor_copy(a2[:, ds(j, 1), :].rearrange("p a (k t) -> p (a k) t", t=2), ps_a[:, 0:4 * KB].rearrange("p (k t) -> p k t", t=4)[:, :, 2:4]).then_inc(s_rc, 1)
                    eng.sem_inc(s_rc, 1)
                    step(0, 0, None)
                    step(1, 1, None)
                    with eng.Fori(1, NT // 2) as i:
                        for par in range(2):
                            step(i * 2 + par, par, i * 32)
                    step(NT - 1, 0, 32 * (NT // 2))

                @block.scalar
                def _(eng):
                    eng.wait_ge(s_var, 1)
                    eng.activation(std[:, :], std[:, :], ACT.Sqrt).then_inc(s_sqrt, 1)
                    eng.wait_ge(s_ready, 1)

                    def norm(j, par):
                        eng.activation(h2[:, par, :], nodes[:, ds(j, 1), :].rearrange("p a d -> p (a d)"), ACT.Relu, bias=bi[:, ds(j, 1)], scale=std[:, ds(j, 1)]).then_inc(s_h2, 1)

                    def features(j, par, stored):
                        eng.wait_ge(s_f, j + 2)
                        if stored is not None:
                            eng.wait_ge(s_fst[par], stored)
                        eng.activation(ft[:, par, :, :], ps_f[:, :].rearrange("p (k c) -> p k c", c=2 * P)[:, :, 0:P], ACT.Copy).then_inc(s_fc, 1)
                        eng.wait_ge(s_fc, j + 2)
                        eng.dma_start(by_tile(table3)[:, ds(j, 1), :], ft[:, par:par + 1, :, :].rearrange("p a k c -> p a (k c)")).then_inc(s_fst[par], 16)
                    eng.sem_inc(s_fc, 1)
                    norm(0, 0)
                    norm(1, 1)
                    features(0, 0, None)
                    eng.wait_ge(s_t, 2)
                    norm(2, 0)
                    features(1, 1, None)
                    with eng.Fori(1, NT // 2) as i:
                        for par in range(2):
                            eng.wait_ge(s_t, i * 2 + par + 1)
                            norm(i * 2 + par + 1, 1 - par)
                            features(i * 2 + par, par, i * 16)
                    features(NT - 1, 0, 16 * (NT // 2))
                    eng.wait_ge(s_fst[0], 16 * (NT // 2 + 1))
                    eng.wait_ge(s_fst[1], 16 * (NT // 2))

                @block.tensor
                def _(eng):
                    eng.sem_inc(s_t, 1)
                    eng.sem_inc(s_f, 1)
                    eng.wait_ge(s_w, 64)
                    eng.matmul(ps_a[:, 0:2 * H], wfc2[:, :, :].rearrange("p a d -> p (a d)"), attn_t[:, :], start=True, stop=True).then_inc(s_fold, 1)
                    eng.wait_ge(s_blk, 64)
                    eng.wait_ge(s_ready, 1)

                    def step(j, par):
                        eng.wait_ge(s_h2, j + 1)
                        for k in range(KB):
                            last = eng.transpose(ps_t[:, k * P:(k + 1) * P], h2[:, par, k * P:(k + 1) * P], ident[:, :])
                        last.then_inc(s_t, 1)
                        eng.wait_ge(s_tc, j + 1)
                        eng.wait_ge(s_fc, j + 1)
                        eng.wait_ge(s_rc, j + 1)
                        for k in range(KB):
                            eng.matmul(ps_f[:, k * 2 * P:(k + 1) * 2 * P], h2_t[:, k * P:(k + 1) * P], blk[:, :, :].rearrange("p a c -> p (a c)"), start=True, stop=True)
                            last = eng.matmul(ps_a[:, 4 * k:4 * k + 4], h2_t[:, k * P:(k + 1) * P], att_w[:, k, :], start=True, stop=True)
                        last.then_inc(s_f, 1)
                    with eng.Fori(0, NT // 2) as i:
                        for par in range(2):
                            step(i * 2 + par, par)
                    step(NT - 1, 0)

        weights = sb(ctx, "weights", [P, V, H])
        with ExitStack() as st:
            a2e = sb(st, "a2e", [P, V, H])
            cont = sb(st, "cont", [SPT, SL], BF16)
            ends = sb(st, "ends", [SPT, 3])
            perm = sb(st, "perm", [P, SW, SG, H])

            with ExitStack() as st1:
                a1_slot = sb(st1, "a1_slot", [P, RING, H])
                hot8 = sb(st1, "hot8", [P, 2, RING, P])
                hot8_t = sb(st1, "hot8_t", [P, 2, RING * P])
                ps_ht = [pb(st1, f"ps_ht{k}", RING * P) for k in range(2)]
                ps_e = [pb(st1, f"ps_e{k}") for k in range(2)]
                landed = [sem(st1, f"landed_s{k}") for k in range(RING)]
                rows_free = sem(st1, "rows_free_s")
                idx_ready = sem(st1, "idx_ready_s")
                asked = sem(st1, "asked_s")
                s_hot = sem(st1, "s_hot8")
                s_ht = sem(st1, "s_ht")
                s_htc = sem(st1, "s_htc")
                s_e = sem(st1, "s_e")
                s_ec = sem(st1, "s_ec")
                with nc.Block() as block:

                    @block.gpsimd
                    def _(eng):
                        gather_rows(eng, a1_table, landed, rows_free, idx_ready, asked, lambda k: a1_slot[:, k, :])

                    @block.vector
                    def _(eng):
                        with eng.Fori(0, GRP // 2) as i:
                            for par in range(2):
                                g = i * 2 + par

                                eng.wait_ge(s_ht, g + 1)
                                eng.tensor_tensor(hot8[:, par, :, :], iota1[:, :].unsqueeze(1).to_broadcast([P, RING, P]),
                                                  dl1[:, ds(g * RING, RING)].unsqueeze(2).to_broadcast([P, RING, P]), ALU.is_equal).then_inc(s_hot, 1)
                                eng.wait_ge(s_e, g + 1)
                                eng.tensor_copy(a2e[:, ds(g * RING, RING), :].rearrange("p v h -> p (v h)"), ps_e[par][:, 0:RING * H]).then_inc(s_ec, 1)

                    @block.tensor
                    def _(eng):
                        eng.sem_inc(s_ht, 2)
                        with eng.Fori(0, GRP // 2) as i:
                            for par in range(2):
                                g = i * 2 + par
                                eng.wait_ge(s_hot, g + 1)
                                for k in range(RING):
                                    last = eng.transpose(ps_ht[par][:, k * P:(k + 1) * P], hot8[:, par, k, :], ident[:, :])
                                last.then_inc(s_ht, 1)
                                eng.wait_ge(s_htc, g + 1)
                                for k in range(RING):
                                    tile = eng.value_load(tile_of[0:1, ds(g * RING + k, 1)], min_val=0, max_val=NT - 1)
                                    last = eng.matmul(ps_e[par][:, k * H:(k + 1) * H], hot8_t[:, par, k * P:(k + 1) * P], a2[:, ds(tile, 1), :], start=True, stop=True)
                                last.then_inc(s_e, 1)

                    @block.scalar
                    def _(eng):
                        eng.sem_inc(rows_free, RING)
                        with eng.Fori(0, GRP // 2) as i:
                            for par in range(2):
                                g = i * 2 + par
                                eng.wait_ge(s_ht, g + 3)
                                eng.activation(hot8_t[:, par, :], ps_ht[par][:, :], ACT.Copy).then_inc(s_htc, 1)
                                for k in range(RING):
                                    eng.wait_ge(landed[k], g * 16 + 16)
                                    eng.activation(weights[:, ds(g * RING + k, 1), :], a1_slot[:, k:k + 1, :], ACT.Copy).then_inc(rows_free, 1)

            with ExitStack() as st1:
                key = sb(st1, "key", [P, V])
                keys = sb(st1, "keys", [SPT, SL])
                ps_k = [pb(st1, f"ps_k{k}") for k in range(4)]
                s_dve = sem(st1, "s_dve_k")
                s_perm = sem(st1, "s_perm_k")
                s_t = sem(st1, "s_t_k")
                s_c = sem(st1, "s_c_k")
                with nc.Block() as block:

                    @block.vector
                    def _(eng):
                        link = chained(eng, s_dve)
                        link(eng.tensor_scalar(key[:, :], dl1[:, 0:V], 1.0, None, ALU.is_ge))
                        link(eng.scalar_tensor_tensor(out=key[:, :], in0=dl1[:, 0:V], scalar=float(P), in1=key[:, :], op0=ALU.is_le, op1=ALU.mult))
                        link(eng.tensor_tensor(key[:, :], key[:, :], d1v[:, :], ALU.mult))
                        eng.tensor_copy(perm[:, :, :, :], key[:, :].rearrange("p (g w) -> p w g", w=SW).unsqueeze(3).to_broadcast([P, SW, SG, H])).then_inc(s_perm, 1)
                        eng.wait_ge(s_c, SW // 4)
                        link(eng.tensor_tensor(cont[:, 1:SL], keys[:, 1:SL], keys[:, 0:SL - 1], ALU.is_equal))
                        link(eng.tensor_scalar(cont[:, 1:SL], cont[:, 1:SL], -1.0, BIG, ALU.add, ALU.mult))
                        link(eng.memset(cont[:, 0:1], -BIG))
                        link(eng.tensor_copy(ends[:, 0:1], keys[:, 0:1]))
                        link(eng.tensor_copy(ends[:, 1:2], keys[:, SL - 1:SL]))

                    @block.tensor
                    def _(eng):
                        eng.wait_ge(s_perm, 1)
                        for q in range(SW // 4):
                            if q >= 4:
                                eng.wait_ge(s_c, q - 3)
                            for k in range(4):
                                last = eng.transpose(ps_k[q % 4][0:SPT, k * P:(k + 1) * P], perm[:, q * 4 + k, :, :].rearrange("p g h -> p (g h)"), ident[:, :])
                            last.then_inc(s_t, 1)

                    @block.scalar
                    def _(eng):
                        for q in range(SW // 4):
                            eng.wait_ge(s_t, q + 1)
                            eng.activation(keys[:, q * 4 * P:(q + 1) * 4 * P], ps_k[q % 4][0:SPT, :], ACT.Copy).then_inc(s_c, 1)

            with ExitStack() as st1:
                run = sb(st1, "run", [SPT, SL])
                row = sb(st1, "row", [1, 14, SPT])
                carry = sb(st1, "carry", [SPT, 2])
                one1 = sb(st1, "one1", [1, 1])
                ps_a = [pb(st1, f"ps_a{k}") for k in range(4)]
                ps_r = pb(st1, "ps_r")
                ps_m = pb(st1, "ps_m")
                s_dve = sem(st1, "s_dve_m")
                s_perm = sem(st1, "s_perm_m")
                s_t = sem(st1, "s_t_m")
                s_c = sem(st1, "s_c_m")
                s_scan = sem(st1, "s_scan")
                s_row = sem(st1, "s_row_m")
                s_car = sem(st1, "s_car")
                s_cc = sem(st1, "s_cc")
                s_mt = sem(st1, "s_mt")
                s_mc = sem(st1, "s_mc")
                s_z = sem(st1, "s_z_m")
                s_d = sem(st1, "s_d_m")
                R_FIRST, R_LAST, R_MAX, R_LINK, R_WHOLE, R_GO, R_ACC, R_IN, R_T = range(9)

                def by_head(r):
                    return row[:, r, :].rearrange("a (h g) -> a h g", g=SG)
                with nc.Block() as block:

                    @block.vector
                    def _(eng):
                        link = chained(eng, s_dve)
                        link(eng.memset(one1[:, :], 1.0))
                        eng.tensor_copy(perm[:, :, :, :], weights[:, :, :].rearrange("p (g w) h -> p w g h", w=SW)).then_inc(s_perm, 1)
                        eng.wait_ge(s_c, SW // 4)
                        fwd, bwd = slice(None), slice(None, None, -1)

                        def carries(back):
                            lo_, hi_ = (slice(1, SG), slice(0, SG - 1))
                            cur, prev = (hi_, lo_) if back else (lo_, hi_)
                            head_end = slice(SG - 1, SG) if back else slice(0, 1)
                            a, b = (R_LAST, R_FIRST) if back else (R_FIRST, R_LAST)
                            link(eng.memset(row[:, R_LINK, :], -BIG))
                            link(eng.tensor_tensor(by_head(R_LINK)[:, :, cur], by_head(a)[:, :, cur], by_head(b)[:, :, prev], ALU.is_equal))
                            link(eng.tensor_scalar(by_head(R_LINK)[:, :, cur], by_head(R_LINK)[:, :, cur], -1.0, BIG, ALU.add, ALU.mult))
                            link(eng.tensor_tensor(row[:, R_WHOLE, :], row[:, R_FIRST, :], row[:, R_LAST, :], ALU.is_equal))
                            link(eng.tensor_scalar(row[:, R_WHOLE, :], row[:, R_WHOLE, :], -1.0, BIG, ALU.add, ALU.mult))
                            link(eng.tensor_tensor(row[:, R_GO, :], row[:, R_LINK, :], row[:, R_WHOLE, :], ALU.min))
                            d = bwd if back else fwd
                            link(eng.tensor_tensor_scan(row[:, R_ACC, :][:, d], row[:, R_GO, :][:, d], row[:, R_MAX, :][:, d], -BIG, ALU.add, ALU.max))
                            link(eng.memset(row[:, R_IN, :], -BIG))
                            link(eng.tensor_tensor(by_head(R_IN)[:, :, cur], by_head(R_ACC)[:, :, prev], by_head(R_LINK)[:, :, cur], ALU.add))
                            link(eng.tensor_scalar(row[:, R_IN, :], row[:, R_IN, :], -BIG, None, ALU.max))
                            link(eng.tensor_copy(row[:, R_T, :].rearrange("a (g h) -> a g h", h=H), by_head(R_IN).rearrange("a h g -> a g h")))

                        link(eng.tensor_tensor_scan(run[:, :], cont[:, :], run[:, :], -BIG, ALU.add, ALU.max))
                        link(eng.tensor_copy(ends[:, 2:3], run[:, SL - 1:SL]))
                        eng.sem_inc(s_scan, 1)
                        eng.wait_ge(s_row, 1)
                        for r in (R_FIRST, R_LAST, R_MAX):
                            link(eng.tensor_copy(by_head(r).rearrange("a h g -> a g h"), ps_r[0:1, r * P:r * P + SPT].rearrange("a (g h) -> a g h", h=H)))
                        carries(False)
                        eng.sem_inc(s_scan, 1)
                        eng.wait_ge(s_row, 2)
                        link(eng.tensor_copy(carry[:, 0:1], ps_m[0:SPT, 0:1]))
                        link(eng.memset(cont[:, 0:1], 0.0))
                        link(eng.tensor_tensor_scan(run[:, :], cont[:, :], run[:, :], carry[:, 0:1], ALU.add, ALU.max))
                        link(eng.memset(cont[:, 0:1], -BIG))
                        eb = run[:, 0:SL - 1][:, bwd]
                        cb = cont[:, 1:SL][:, bwd]
                        link(eng.tensor_tensor_scan(eb, cb, eb, run[:, SL - 1:SL], ALU.add, ALU.max))
                        link(eng.tensor_copy(ends[:, 2:3], run[:, 0:1]))
                        eng.sem_inc(s_scan, 1)
                        eng.wait_ge(s_row, 3)
                        link(eng.tensor_copy(by_head(R_MAX).rearrange("a h g -> a g h"), ps_r[0:1, R_MAX * P:R_MAX * P + SPT].rearrange("a (g h) -> a g h", h=H)))
                        carries(True)
                        eng.sem_inc(s_scan, 1)
                        eng.wait_ge(s_row, 4)
                        link(eng.tensor_copy(carry[:, 1:2], ps_m[0:SPT, 1:2]))
                        link(eng.tensor_tensor(run[:, SL - 1:SL], run[:, SL - 1:SL], carry[:, 1:2], ALU.max))
                        link(eng.tensor_tensor_scan(eb, cb, eb, run[:, SL - 1:SL], ALU.add, ALU.max))
                        eng.sem_inc(s_scan, 1)
                        def flat(t):
                            return t.rearrange("p v h -> p (v h)")
                        w_, e_ = flat(weights[:, :, :]), flat(a2e[:, :, :])
                        m_ = perm[:, :, :, :].rearrange("p w g h -> p (w g h)")
                        link(eng.tensor_tensor(w_, w_, e_, ALU.add))
                        link(eng.scalar_tensor_tensor(out=w_, in0=w_, scalar=SLOPE, in1=w_, op0=ALU.mult, op1=ALU.max))
                        eng.wait_ge(s_mc, SW // 4)
                        link(eng.tensor_tensor(m_, m_, e_, ALU.add))
                        link(eng.scalar_tensor_tensor(out=m_, in0=m_, scalar=SLOPE, in1=m_, op0=ALU.mult, op1=ALU.max))
                        eng.tensor_tensor(w_, w_, m_, ALU.subtract).then_inc(s_d, 1)

                    @block.tensor
                    def _(eng):
                        eng.wait_ge(s_perm, 1)
                        for q in range(SW // 4):
                            if q >= 4:
                                eng.wait_ge(s_c, q - 3)
                            for k in range(4):
                                last = eng.transpose(ps_a[q % 4][0:SPT, k * P:(k + 1) * P], perm[:, q * 4 + k, :, :].rearrange("p g h -> p (g h)"), ident[:, :])
                            last.then_inc(s_t, 1)
                        for back in range(2):
                            eng.wait_ge(s_scan, 2 * back + 1)
                            for r in range(3) if not back else (2,):
                                last = eng.transpose(ps_r[0:1, r * P:r * P + SPT], ends[:, r:r + 1], ident[0:SPT, 0:SPT])
                            last.then_inc(s_row, 1)
                            eng.wait_ge(s_scan, 2 * back + 2)
                            eng.matmul(ps_m[0:SPT, back:back + 1], row[:, R_T, :], one1[:, :], start=True, stop=True).then_inc(s_row, 1)
                        eng.wait_ge(s_scan, 5)
                        for q in range(SW // 4):
                            eng.wait_ge(s_c, SW // 4) if q < 4 else eng.wait_ge(s_mc, q - 3)
                            for k in range(4):
                                last = eng.transpose(ps_a[q % 4][:, k * P:k * P + SPT], run[:, (q * 4 + k) * P:(q * 4 + k + 1) * P], ident[0:SPT, 0:SPT])
                            last.then_inc(s_mt, 1)

                    @block.scalar
                    def _(eng):
                        for q in range(SW // 4):
                            eng.wait_ge(s_t, q + 1)
                            eng.activation(run[:, q * 4 * P:(q + 1) * 4 * P], ps_a[q % 4][0:SPT, :], ACT.Copy).then_inc(s_c, 1)
                        back = perm[:, :, :, :].rearrange("p w g h -> p (w g h)").rearrange("p (g w h) -> p w g h", g=SG, h=H)
                        for q in range(SW // 4):
                            eng.wait_ge(s_mt, q + 1)
                            for k in range(4):
                                last = eng.activation(back[:, q * 4 + k, :, :], ps_a[q % 4][:, k * P:k * P + SPT].rearrange("p (g h) -> p g h", h=H), ACT.Copy)
                            last.then_inc(s_mc, 1)
                        eng.wait_ge(s_d, 1)
                        w_ = weights[:, :, :].rearrange("p v h -> p (v h)")
                        eng.activation(w_, w_, ACT.Exp).then_inc(s_z, 1)

        den = sb(ctx, "den", [P, NT, H])
        with ExitStack() as st:
            ring = sb(st, "ring_g", [P, RING, D])
            onehot = sb(st, "onehot_g", [P, RING, P])
            msg = sb(st, "msg", [P, NPS, D + H])
            ps = [pb(st, f"ps_sum_g{k}", 1024) for k in range(NPS)]
            landed = [sem(st, f"landed_g{k}") for k in range(RING)]
            rows_free = sem(st, "rows_free_g")
            idx_ready = sem(st, "idx_ready_g")
            asked = sem(st, "asked_g")
            hot_ready = sem(st, "hot_ready_g")
            s_act = sem(st, "s_act_g")
            summed = sem(st, "summed_g")
            added = sem(st, "added_g")
            s_zero = sem(st, "s_zero_g")
            HA = 5
            with nc.Block() as block:

                @block.gpsimd
                def _(eng):
                    gather_rows(eng, table3, landed, rows_free, idx_ready, asked, lambda k: ring[:, k, :])

                @block.scalar
                def _(eng):
                    with eng.Fori(0, GRP) as i:
                        for k in range(RING):
                            v = i * RING + k
                            eng.wait_ge(landed[k], i * 16 + 16)
                            eng.wait_ge(summed, v + 1)
                            for h in range(HA):
                                eng.activation(msg[:, k % NPS, h * DH:(h + 1) * DH], ring[:, k, h * DH:(h + 1) * DH], ACT.Copy, scale=weights[:, ds(v, 1), h:h + 1].rearrange("p a h -> p (a h)"))
                            eng.activation(msg[:, k % NPS, D:D + H].unsqueeze(1), weights[:, ds(v, 1), :], ACT.Copy).then_inc(s_act, 1)

                @block.tensor
                def _(eng):
                    eng.sem_inc(summed, NPS)
                    with eng.Fori(0, GRP) as i:
                        for k in range(RING):
                            v = i * RING + k
                            eng.wait_ge(s_act, v + 1)
                            eng.wait_ge(hot_ready, v + 1)
                            eng.wait_ge(added, v + 1)
                            eng.matmul(ps[k % NPS][:, 0:512], onehot[:, k, :], msg[:, k % NPS, 0:512], start=True, stop=True)
                            eng.matmul(ps[k % NPS][:, 512:D + H], onehot[:, k, :], msg[:, k % NPS, 512:D + H], start=True, stop=True).then_inc(summed, 1)

                @block.vector
                def _(eng):
                    eng.memset(nodes[:, :, :], 0.0)
                    eng.memset(den[:, :, :], 0.0).then_inc(s_zero, 1)
                    eng.sem_inc(added, NPS)
                    eng.sem_inc(rows_free, RING)
                    eng.wait_ge(s_zero, 1)

                    def prepare(v, k, first=False, need=16):
                        eng.tensor_scalar(onehot[:, k, :], iota1[:, :], dl1[:, ds(v, 1)], None, ALU.is_equal)
                        eng.wait_ge(landed[k], need)
                        eng.wait_ge(s_act, v + 1)
                        n = H - HA
                        eng.tensor_tensor(msg[:, k % NPS, HA * DH:D].rearrange("p (h d) -> p h d", d=DH), ring[:, k, HA * DH:D].rearrange("p (h d) -> p h d", d=DH),
                                          weights[:, ds(v, 1), HA:H].rearrange("p a h -> p (a h)").unsqueeze(2).to_broadcast([P, n, DH]), ALU.mult).then_inc(hot_ready, 1)
                        eng.wait_ge(hot_ready, v + 1)
                        eng.sem_inc(rows_free, 1)

                    def add(v, k):
                        tile = eng.value_load(tile_of[0:1, ds(v, 1)], min_val=0, max_val=NT - 1)
                        eng.wait_ge(summed, v + NPS + 1)
                        eng.wait_ge(added, v + NPS)
                        eng.tensor_tensor(nodes[:, ds(tile, 1), :], nodes[:, ds(tile, 1), :], ps[k % NPS][:, 0:D].unsqueeze(1), ALU.add)
                        eng.tensor_tensor(den[:, ds(tile, 1), :], den[:, ds(tile, 1), :], ps[k % NPS][:, D:D + H].unsqueeze(1), ALU.add).then_inc(added, 1)
                    for k in range(2):
                        prepare(k, k)
                    with eng.Fori(0, GRP - 1) as i:
                        for k in range(RING):
                            v = i * RING + k
                            add(v, k)
                            prepare(v + 2, (k + 2) % RING, need=i * 16 + (16 if k + 2 < RING else 32))
                    for k in range(RING):
                        v = V - RING + k
                        add(v, k)
                        if k + 2 < RING:
                            prepare(v + 2, k + 2, need=16 * GRP)

        with ExitStack() as st:
            res = sb(st, "res_l", [P, 2, D])
            x1 = sb(st, "x1_l", [P, 2, D])
            o = sb(st, "o", [P, 2, D])
            s_r = [sem(st, f"s_r{k}") for k in range(2)]
            s_dve = sem(st, "s_dve_o")
            s_use = sem(st, "s_use")
            s_o = [sem(st, f"s_o{k}") for k in range(2)]
            with nc.Block() as block:

                @block.sync
                def _(eng):
                    for j in range(NT):
                        if j >= 2:
                            eng.wait_ge(s_use, j - 1)
                        eng.dma_start(res[:, j % 2, :], res_table[j * P:(j + 1) * P, :]).then_inc(s_r[j % 2], 16)
                        eng.dma_start(x1[:, j % 2, :], x1_table[j * P:(j + 1) * P, :]).then_inc(s_r[j % 2], 16)

                @block.vector
                def _(eng):
                    link = chained(eng, s_dve)
                    link(eng.tensor_scalar(den[:, :, :], den[:, :, :], 0.5, None, ALU.max))
                    link(eng.reciprocal(den[:, :, :], den[:, :, :]))
                    for j in range(NT):
                        par = j % 2
                        link(eng.tensor_tensor(nodes[:, j, :].rearrange("p (h d) -> p h d", d=DH), nodes[:, j, :].rearrange("p (h d) -> p h d", d=DH),
                                               den[:, j, :].unsqueeze(2).to_broadcast([P, H, DH]), ALU.mult))
                        eng.wait_ge(s_r[par], 32 * (j // 2 + 1))
                        link(eng.tensor_tensor(nodes[:, j, :], nodes[:, j, :], res[:, par, :], ALU.add))
                        if j >= 2:
                            eng.wait_ge(s_o[par], 16 * (j // 2))
                        eng.scalar_tensor_tensor(out=o[:, par, :], in0=nodes[:, j, :], scalar=0.0, in1=x1[:, par, :], op0=ALU.max, op1=ALU.add).then_inc(s_use, 1)

                @block.scalar
                def _(eng):
                    for j in range(NT):
                        rows = P if j < NT - 1 else LAST
                        eng.wait_ge(s_use, j + 1)
                        eng.dma_start(out[j * P:j * P + rows, :], o[0:rows, j % 2, :]).then_inc(s_o[j % 2], 16)
                    eng.wait_ge(s_o[0], 16 * (NT // 2 + 1))
                    eng.wait_ge(s_o[1], 16 * (NT // 2))


def kernel(**inputs):
    import numpy as np
    import concourse.bacc as bacc
    from concourse.bass_utils import run_bass_kernel_spmd

    nc = bacc.Bacc("TRN2", target_bir_lowering=False, num_devices=1)
    given = {k: np.asarray(v) for k, v in inputs.items()}
    laid = {
        "x": given["x"], "src": given["src"], "dst": given["dst"],
        "w1t": given["L0_gnn_W1"].T, "b1": given["L0_gnn_b1"],
        "w2t": given["L0_gnn_W2"].T, "b2": given["L0_gnn_b2"],
        "wfc": given["L1_gnn_W_fc"], "wfct": given["L1_gnn_W_fc"].T,
        "attn_lt": given["L1_gnn_attn_l"].T, "attn_rt": given["L1_gnn_attn_r"].T,
        "wrest": given["L1_gnn_W_res"].T,
    }
    arrays, args = {}, []
    for name, a in laid.items():
        a = np.ascontiguousarray(a)
        arrays[f"in_{name}"] = a
        args.append(nc.dram_tensor(f"in_{name}", a.shape, mybir.dt.from_np(a.dtype), kind="ExternalInput").ap())
    args.append(nc.dram_tensor("out_x", (N, D), F32, kind="ExternalOutput").ap())
    gnn_kernel(nc, *args)
    r = run_bass_kernel_spmd(nc, [arrays], core_ids=[0])
    return r.results[0]["out_x"]
```

```python
from contextlib import ExitStack

import concourse.bass as bass
from concourse import mybir

F32 = mybir.dt.float32
F32R = mybir.dt.float32r
BF16 = mybir.dt.bfloat16
I32 = mybir.dt.int32
ALU = mybir.AluOpType
ACT = mybir.ActivationFunctionType
ds = bass.ds

P = 128
N = 3125
D = 768
E = 50000
H = 12
DH = D // H
NT = -(-N // P)
LAST = N - (NT - 1) * P
NCH = -(-E // P)
V = (NCH + NT + NT) // 2 * 2
RING = 10
SMALL = 20
AHEAD = 2
GROUP = 10
HOTS = 4
KB = D // P
HALVES = [(0, 512), (512, D - 512)]
CB = -(-NCH // P)
EB = E // P // P
EPS = 1e-5
SLOPE = 0.2
BIG = 3.0e38
HCOLS = NCH
HSTEP = 17
HFULL = E // P
HREST = E - HFULL * P
XG = 5
SG = 10
SW = V // SG
SPT = SG * H
SL = SW * P
assert V % (2 * SMALL) == 0 and SMALL == 2 * GROUP and RING % 2 == 0 and HCOLS % HSTEP == 0 and NT % XG == 0 and V % SG == 0 and SW % 4 == 0


def gnn_kernel(nc, x, src, dst, w1t, b1, w2t, b2, wfc, wfct, attn_lt, attn_rt, wrest, out):
    ctx = ExitStack()


    def sb(stack, name, shape, dt=F32):
        return stack.enter_context(nc.sbuf_tensor(name, shape, dt))

    def pb(stack, name, cols=512, dt=F32):
        return stack.enter_context(nc.psum_tensor(name, [P, cols], dt))

    def sem(stack, name):
        return stack.enter_context(nc.semaphore(name))

    def chained(eng, s):
        n = [0]

        def link(ins):
            n[0] += 1
            ins.then_inc(s, 1)
            eng.wait_ge(s, n[0])
        return link

    with ctx:
        table1 = nc.dram_tensor("table1", (NT * P, D), F32).ap()
        table2 = nc.dram_tensor("table2", (NT * P, D), F32).ap()
        table3 = nc.dram_tensor("table3", (NT * P, D), F32).ap()
        a1_table = nc.dram_tensor("a1_table", (NT * P, H), F32).ap()
        res_table = nc.dram_tensor("res_table", (NT * P, D), F32).ap()

        def by_tile(t):
            return t.rearrange("(t p) d -> p t d", p=P)

        nodes = sb(ctx, "nodes", [P, NT, D])
        ident = sb(ctx, "ident", [P, P])
        iota1 = sb(ctx, "iota1", [P, P])
        dl1 = sb(ctx, "dl1", [P, V])
        d1v = sb(ctx, "d1v", [P, V])
        idx = sb(ctx, "idx", [P, V], I32)
        tile_of = sb(ctx, "tile_of", [1, V], I32)
        pair0 = sb(ctx, "pair0", [1, NT + 1], I32)
        dinv = sb(ctx, "dinv", [P, NT])
        landed = [sem(ctx, f"landed{k}") for k in range(RING)]
        idx_slot = [sb(ctx, f"idx_slot{h}", [P, max(RING, SMALL)], I32) for h in range(2)]




        with ExitStack() as st:
            hist_dst = sb(st, "hist_dst", [P, HCOLS], I32)
            lo_i = sb(st, "lo_i", [P, HCOLS], I32)
            hi_i = sb(st, "hi_i", [P, HCOLS], I32)
            lo = sb(st, "lo", [P, HCOLS])
            hi = sb(st, "hi", [P, HCOLS])
            hi_hot = sb(st, "hi_hot", [P, HCOLS, NT], BF16)
            lo_hot = sb(st, "lo_hot", [P, 2, HSTEP, P], BF16)
            iota0b = sb(st, "iota0b", [P, P], BF16)
            iota_nt = sb(st, "iota_nt", [P, NT])
            iota_v = sb(st, "iota_v", [P, V])
            rowno = sb(st, "rowno", [P, CB])
            zeros_b = sb(st, "zeros_b", [P, P], BF16)
            ones = sb(st, "ones", [P, P])
            tri = sb(st, "tri", [NT, NT])
            src_i = sb(st, "src_i", [P, CB, P], I32)
            dst_i = sb(st, "dst_i", [P, CB, P], I32)
            src_f = sb(st, "src_f", [P, CB, P])
            dst_f = sb(st, "dst_f", [P, CB, P])
            counts = sb(st, "counts", [P, NT])
            c = sb(st, "c", [NT, 16])
            ci = sb(st, "ci", [NT, 4], I32)
            at_least = sb(st, "at_least", [NT, V])
            sel = sb(st, "sel", [NT, V])
            off_b = sb(st, "off_b", [NT, P])
            tile_b = sb(st, "tile_b", [NT, P])
            chunk_v = sb(st, "chunk_v", [P, V])
            chunk_hot = sb(st, "chunk_hot", [P, CB, V])
            stats = sb(st, "stats", [P, NT, 2, 6])
            mv = sb(st, "mv", [P, NT, 2])
            std = sb(st, "std", [P, NT])
            sc = sb(st, "sc", [P, NT])
            bi = sb(st, "bi", [P, NT])
            ps_h = pb(st, "ps_h", NT)
            ps_c = pb(st, "ps_c")
            ps_off = pb(st, "ps_off")
            ps_tile = pb(st, "ps_tile")
            ps_d = pb(st, "ps_d")
            ps_s = pb(st, "ps_s")
            s_fill = sem(st, "s_fill")
            s_hd = sem(st, "s_hd")
            s_ed = sem(st, "s_ed")
            s_x = [sem(st, f"s_x{g}") for g in range(NT // XG)]
            s_pool = sem(st, "s_pool")
            s_dve = sem(st, "s_dve")
            s_lo = sem(st, "s_lo")
            s_hdone = sem(st, "s_hdone")
            s_counts = sem(st, "s_counts")
            s_pe = sem(st, "s_pe")
            s_step = sem(st, "s_step")
            s_sqrt = sem(st, "s_sqrt")
            s_var = sem(st, "s_var")
            s_scale = sem(st, "s_scale")
            s_row = sem(st, "s_row")
            s_st = sem(st, "s_st")
            FILL = 5
            POOL = 10
            with nc.Block() as block:

                @block.sync
                def _(eng):
                    eng.wait_ge(s_fill, FILL)
                    eng.dma_start(hist_dst[:, 0:HFULL], dst[0:HFULL * P].rearrange("(p c) -> p c", p=P)).then_inc(s_hd, 16)
                    eng.dma_start(hist_dst[0:HREST, HFULL:HCOLS], dst[HFULL * P:E].rearrange("(p c) -> p c", c=1)).then_inc(s_hd, 16)
                    whole = EB * P * P
                    rows = (E - whole) // P
                    for v, t in ((src, src_i), (dst, dst_i)):
                        eng.dma_start(t[:, 0:EB, :], v[0:whole].rearrange("(b q e) -> q b e", q=P, e=P)).then_inc(s_ed, 16)
                        eng.dma_start(t[0:rows, EB, :], v[whole:whole + rows * P].rearrange("(q e) -> q e", e=P)).then_inc(s_ed, 16)
                        eng.dma_start(t[rows:rows + 1, EB, 0:E - whole - rows * P], v[whole + rows * P:E].rearrange("(a e) -> a e", a=1)).then_inc(s_ed, 16)
                    for g in range(NT // XG):
                        r0, r1 = g * XG * P, min((g + 1) * XG * P, N)
                        full = (r1 - r0) // P
                        eng.dma_start(nodes[:, g * XG:g * XG + full, :], x[r0:r0 + full * P, :].rearrange("(t p) d -> p t d", p=P)).then_inc(s_x[g], 16)
                        if r0 + full * P < r1:
                            eng.dma_start(nodes[0:r1 - r0 - full * P, g * XG + full, :], x[r0 + full * P:r1, :]).then_inc(s_x[g], 16)

                @block.gpsimd
                def _(eng):
                    eng.memset(hist_dst[:, HFULL:HCOLS], -1).then_inc(s_fill, 1)
                    eng.memset(src_i[:, EB, :], 0).then_inc(s_fill, 1)
                    eng.memset(dst_i[:, EB, :], -1).then_inc(s_fill, 1)
                    eng.memset(nodes[:, NT - 1, :], 0.0).then_inc(s_fill, 1)
                    eng.memset(zeros_b[:, :], 0.0).then_inc(s_fill, 1)
                    eng.iota(iota0b[:, :], pattern=[[1, P]], base=0, channel_multiplier=0, allow_small_or_imprecise_dtypes=True).then_inc(s_pool, 1)
                    eng.iota(iota_nt[:, :], pattern=[[1, NT]], base=0, channel_multiplier=0, allow_small_or_imprecise_dtypes=True).then_inc(s_pool, 1)
                    eng.iota(iota_v[:, :], pattern=[[1, V]], base=0, channel_multiplier=0, allow_small_or_imprecise_dtypes=True).then_inc(s_pool, 1)
                    eng.iota(rowno[:, :], pattern=[[P, CB]], base=0, channel_multiplier=1, allow_small_or_imprecise_dtypes=True).then_inc(s_pool, 1)
                    eng.iota(iota1[:, :], pattern=[[1, P]], base=1, channel_multiplier=0, allow_small_or_imprecise_dtypes=True).then_inc(s_pool, 1)
                    eng.memset(ones[:, :], 1.0).then_inc(s_pool, 1)
                    eng.memset(ident[:, :], 0.0).then_inc(s_pool, 1)
                    eng.memset(tri[:, :], 1.0).then_inc(s_pool, 1)
                    eng.wait_ge(s_pool, 8)
                    eng.affine_select(out=ident[:, :], in_=ident[:, :], compare_op=ALU.not_equal, fill=1.0, base=0,
                                      pattern=[[-1, P]], channel_multiplier=1).then_inc(s_pool, 1)
                    eng.affine_select(out=tri[:, :], in_=tri[:, :], compare_op=ALU.is_gt, fill=0.0, base=0,
                                      pattern=[[1, NT]], channel_multiplier=-1).then_inc(s_pool, 1)

                @block.vector
                def _(eng):
                    link = chained(eng, s_dve)
                    eng.wait_ge(s_pool, POOL)
                    eng.wait_ge(s_hd, 32)
                    link(eng.tensor_single_scalar(lo_i[:, :], hist_dst[:, :], P - 1, ALU.bitwise_and))
                    link(eng.tensor_single_scalar(hi_i[:, :], hist_dst[:, :], P.bit_length() - 1, ALU.arith_shift_right))
                    link(eng.tensor_copy(lo[:, :], lo_i[:, :]))
                    link(eng.tensor_copy(hi[:, :], hi_i[:, :]))
                    link(eng.tensor_tensor(hi_hot[:, :, :], hi[:, :].unsqueeze(2).to_broadcast([P, HCOLS, NT]),
                                           iota_nt[:, :].unsqueeze(1).to_broadcast([P, HCOLS, NT]), ALU.is_equal))
                    with eng.Fori(0, HCOLS // HSTEP) as i:
                        eng.wait_ge(s_hdone, i + 1)
                        for k in range(HSTEP):
                            last = eng.tensor_scalar(lo_hot[:, ds(i % 2, 1), k, :], iota0b[:, :], lo[:, ds(i * HSTEP + k, 1)], None, ALU.is_equal)
                        last.then_inc(s_lo, 1)
                    for j in range(NT):
                        if j % XG == 0:
                            eng.wait_ge(s_x[j // XG], 32 if j == NT - XG else 16)
                        for h in range(2):
                            last = eng.bn_stats(stats[:, j, h, :], nodes[:, j, h * D // 2:(h + 1) * D // 2])
                    link(last)
                    for j in range(NT):
                        last = eng.bn_aggr(mv[:, j, :], stats[:, j, :, :])
                    link(last)
                    eng.tensor_scalar(std[:, :], mv[:, :, 1], EPS, None, ALU.add).then_inc(s_var, 1)
                    eng.wait_ge(s_hdone, 3 + HCOLS // HSTEP)
                    link(eng.tensor_copy(counts[:, :], ps_h[:, 0:NT]))
                    eng.tensor_scalar(dinv[:, :], counts[:, :], 1.0, None, ALU.add).then_inc(s_var, 1)
                    eng.sem_inc(s_counts, 1)
                    eng.wait_ge(s_sqrt, 2)
                    link(eng.reciprocal(dinv[:, :], dinv[:, :]))
                    link(eng.reciprocal(std[:, :], std[:, :]))
                    link(eng.tensor_tensor(sc[:, :], std[:, :], dinv[:, :], ALU.mult))
                    link(eng.scalar_tensor_tensor(out=bi[:, :], in0=mv[:, :, 0], scalar=-1.0, in1=sc[:, :], op0=ALU.mult, op1=ALU.mult))
                    eng.sem_inc(s_scale, 1)
                    CNT, T0, T1, CS, CE, NV, M0, M1, LASTV, OFF, V0, V1 = range(12)

                    def col(k):
                        return c[:, k:k + 1]
                    eng.wait_ge(s_pe, 1)
                    link(eng.tensor_copy(col(CNT), ps_c[0:NT, 0:1]))
                    eng.sem_inc(s_step, 1)
                    eng.wait_ge(s_pe, 2)
                    link(eng.tensor_copy(col(T0), ps_c[0:NT, 1:2]))
                    link(eng.tensor_tensor(col(T1), col(T0), col(CNT), ALU.add))
                    link(eng.tensor_scalar(col(T1), col(T1), float(P - 1), None, ALU.add))
                    link(eng.tensor_copy(ci[:, 0:2], c[:, T0:T1 + 1]))
                    link(eng.tensor_single_scalar(ci[:, 2:4], ci[:, 0:2], P.bit_length() - 1, ALU.arith_shift_right))
                    link(eng.tensor_copy(c[:, CS:CE + 1], ci[:, 2:4]))
                    link(eng.tensor_tensor(col(NV), col(CE), col(CS), ALU.subtract))
                    link(eng.tensor_scalar(ci[:, 0:1], col(NV), 1.0, 1.0, ALU.max, ALU.add))
                    link(eng.tensor_single_scalar(ci[:, 1:2], ci[:, 0:1], 1, ALU.arith_shift_right))
                    link(eng.tensor_copy(col(NV), ci[:, 1:2]))
                    eng.sem_inc(s_step, 1)
                    eng.wait_ge(s_pe, 3)
                    link(eng.tensor_copy(col(M0), ps_c[0:NT, 2:3]))
                    link(eng.tensor_tensor(col(M1), col(M0), col(NV), ALU.add))
                    link(eng.tensor_scalar(col(LASTV), rowno[0:NT, 0:1], float(NT - 1), float(V // 2), ALU.is_equal, ALU.mult))
                    link(eng.tensor_tensor(col(M1), col(M1), col(LASTV), ALU.max))
                    link(eng.tensor_scalar(c[:, V0:V1 + 1], c[:, M0:M1 + 1], 2.0, None, ALU.mult))
                    link(eng.tensor_tensor(col(OFF), col(CS), col(V0), ALU.subtract))
                    link(eng.tensor_scalar(at_least[:, :], iota_v[0:NT, :], col(V0), None, ALU.is_ge))
                    link(eng.scalar_tensor_tensor(out=sel[:, :], in0=iota_v[0:NT, :], scalar=col(V1), in1=at_least[:, :],
                                                  op0=ALU.is_lt, op1=ALU.mult))
                    link(eng.tensor_scalar(off_b[:, :], ones[0:NT, :], col(OFF), None, ALU.mult))
                    link(eng.tensor_scalar(tile_b[:, :], ones[0:NT, :], rowno[0:NT, 0:1], float(P), ALU.mult, ALU.mult))
                    eng.sem_inc(s_step, 1)
                    eng.wait_ge(s_pe, 4)
                    link(eng.tensor_tensor(chunk_v[:, :], ps_off[:, 0:V], iota_v[:, :], ALU.add))
                    for b in range(CB):
                        link(eng.tensor_scalar(chunk_hot[:, b, :], chunk_v[:, :], rowno[:, b:b + 1], None, ALU.is_equal))
                    eng.wait_ge(s_ed, 6 * 16)
                    link(eng.tensor_scalar(dst_f[:, :, :], dst_i[:, :, :], 1.0, None, ALU.add))
                    link(eng.tensor_copy(src_f[:, :, :], src_i[:, :, :]))
                    eng.sem_inc(s_step, 1)
                    eng.wait_ge(s_pe, 5)
                    link(eng.tensor_copy(pair0[:, 0:NT], ps_c[0:1, 4:4 + NT]))
                    link(eng.memset(pair0[:, NT:NT + 1], V // 2))
                    link(eng.tensor_copy(d1v[:, :], ps_d[:, 0:V]))
                    link(eng.tensor_tensor(dl1[:, 0:V], d1v[:, :], ps_tile[:, 0:V], ALU.subtract))
                    link(eng.tensor_copy(idx[:, :], ps_s[:, 0:V]))
                    link(eng.tensor_scalar(tile_of[:, :], ps_tile[0:1, 0:V], 1.0 / P, None, ALU.mult))

                @block.tensor
                def _(eng):
                    eng.wait_ge(s_pool, POOL)
                    eng.wait_ge(s_fill, FILL)
                    eng.sem_inc(s_hdone, 1)
                    eng.matmul(ps_h[:, 0:NT], zeros_b[:, :], zeros_b[:, 0:NT], start=True, stop=True).then_inc(s_hdone, 1)
                    with eng.Fori(0, HCOLS // HSTEP) as i:
                        eng.wait_ge(s_lo, i + 1)
                        for k in range(HSTEP):
                            last = eng.matmul(ps_h[:, 0:NT], lo_hot[:, ds(i % 2, 1), k, :], hi_hot[:, ds(i * HSTEP + k, 1), :],
                                              start=False, stop=True, skip_group_check=True)
                        last.then_inc(s_hdone, 1)
                    eng.matmul(ps_h[:, 0:NT], zeros_b[:, :], zeros_b[:, 0:NT], start=False, stop=True,
                               skip_group_check=True).then_inc(s_hdone, 1)
                    eng.wait_ge(s_counts, 1)
                    eng.matmul(ps_c[0:NT, 0:1], counts[:, :], ones[:, 0:1], start=True, stop=True).then_inc(s_pe, 1)
                    eng.wait_ge(s_step, 1)
                    eng.matmul(ps_c[0:NT, 1:2], tri[:, :], c[:, 0:1], start=True, stop=True).then_inc(s_pe, 1)
                    eng.wait_ge(s_step, 2)
                    eng.matmul(ps_c[0:NT, 2:3], tri[:, :], c[:, 5:6], start=True, stop=True).then_inc(s_pe, 1)
                    eng.wait_ge(s_step, 3)
                    eng.transpose(ps_c[0:1, 4:4 + NT], c[:, 6:7], ident[0:NT, 0:NT])
                    eng.matmul(ps_off[:, 0:V], off_b[:, :], sel[:, :], start=True, stop=True)
                    eng.matmul(ps_tile[:, 0:V], tile_b[:, :], sel[:, :], start=True, stop=True).then_inc(s_pe, 1)
                    eng.wait_ge(s_step, 4)
                    for t, ps in ((dst_f, ps_d), (src_f, ps_s)):
                        for b in range(CB):
                            last = eng.matmul(ps[:, 0:V], t[:, b, :], chunk_hot[:, b, :], start=(b == 0), stop=(b == CB - 1))
                    last.then_inc(s_pe, 1)

                @block.scalar
                def _(eng):
                    eng.wait_ge(s_var, 1)
                    eng.activation(std[:, :], std[:, :], ACT.Sqrt).then_inc(s_sqrt, 1)
                    eng.wait_ge(s_var, 2)
                    eng.activation(dinv[:, :], dinv[:, :], ACT.Sqrt).then_inc(s_sqrt, 1)
                    eng.wait_ge(s_scale, 1)
                    with eng.Fori(0, NT) as j:
                        eng.activation(nodes[:, ds(j, 1), :], nodes[:, ds(j, 1), :], ACT.Relu, bias=bi[:, ds(j, 1)],
                                       scale=sc[:, ds(j, 1)]).then_inc(s_row, 1)
                        eng.wait_ge(s_row, j + 1)
                        eng.dma_start(by_tile(table1)[:, ds(j, 1), :], nodes[:, ds(j, 1), :]).then_inc(s_st, 16)
                    eng.wait_ge(s_st, NT * 16)

        def gather_rows(eng, table, freed, idx_ready, asked, dest):
            def half(n, h, count):
                eng.wait_ge(freed[0], n * (RING // 2) + 1)
                eng.tensor_copy(idx_slot[h][:, 0:count], idx[:, ds(n * RING, count)]).then_inc(idx_ready, 1)
                eng.wait_ge(idx_ready, n + 1)
                for k in range(count):
                    if k % 2 == 0:
                        for f in freed:
                            eng.wait_ge(f, n * (RING // 2) + k // 2 + 1)
                        eng.sem_inc(asked, 1)
                    eng.indirect_dma_start(out=dest(k), out_offset=None, in_=table,
                                           in_offset=bass.IndirectOffsetOnAxis(ap=idx_slot[h][:, k:k + 1], axis=0)).then_inc(landed[k], 16)
            with eng.Fori(0, V // RING // 2) as i:
                for h in range(2):
                    half(i * 2 + h, h, RING)
            for n in range(V // RING // 2 * 2, -(-V // RING)):
                half(n, n % 2, min(RING, V - n * RING))

        def slot_uses(k):
            return -(-(V - k) // RING)

        def relay_landed(eng, earlier, rows_landed):
            with eng.Fori(0, V // RING) as i:
                for k in range(RING):
                    eng.wait_ge(landed[k], i * 16 + (slot_uses(k) * earlier + 1) * 16)
                    eng.sem_inc(rows_landed, 1)
            for k in range(V % RING):
                eng.wait_ge(landed[k], slot_uses(k) * (earlier + 1) * 16)
                eng.sem_inc(rows_landed, 1)
            eng.sem_inc(rows_landed, 2 * AHEAD)

        def visits_of(eng, j, body):
            first = eng.value_load(pair0[0:1, ds(j, 1)], min_val=0, max_val=V // 2 - 1)
            end = eng.value_load(pair0[0:1, ds(j + 1, 1)], min_val=1, max_val=V // 2)
            with eng.Fori(first, end) as g:
                body(g)

        def one_hots(eng, g, hot):
            return eng.tensor_tensor(hot[:, ds((g * 2) % (2 * HOTS), 2), :], iota1[:, :].unsqueeze(1).to_broadcast([P, 2, P]),
                                     dl1[:, ds(g * 2, 2)].unsqueeze(2).to_broadcast([P, 2, P]), ALU.is_equal)

        def by_pair(eng, g, body):
            which = eng.snap(g % HOTS)

            def choose(lo_, hi_):
                if hi_ - lo_ == 1:
                    body(lo_)
                    return
                mid = (lo_ + hi_) // 2
                with eng.If(which < mid):
                    choose(lo_, mid)
                with eng.Else():
                    choose(mid, hi_)
            choose(0, HOTS)

        def staged(eng, lag, step):
            assert (NT - lag) % 2 == 0
            for j in range(lag):
                step(j, j % 2)
            with eng.Fori(0, (NT - lag) // 2) as i:
                for b in range(2):
                    step(i * 2 + lag + b, (lag + b) % 2)
            for j in range(NT, NT + lag):
                step(j, j % 2)

        def has(j, back):
            return not isinstance(j, int) or 0 <= j - back < NT

        def convolution(tag, table, wt, bias, first):
            with ExitStack() as st:
                ring = sb(st, f"ring{tag}", [P, RING, D])
                hot = sb(st, f"hot{tag}", [P, 2 * HOTS, P], F32R)
                parts = sb(st, f"parts{tag}", [P, 2, 2 * HOTS, D], F32R)
                w = sb(st, f"w{tag}", [P, KB, D])
                bias_b = sb(st, f"bias_b{tag}", [P, D])
                scaled = sb(st, f"scaled{tag}", [P, 2, D])
                sum_t = sb(st, f"sum_t{tag}", [P, D])
                tmp = sb(st, f"tmp{tag}", [P, D])
                xt = sb(st, f"xt{tag}", [P, 2, D])
                ps_sum = pb(st, f"ps_sum{tag}", 2048)
                ps_t = pb(st, f"ps_t{tag}", 1024)
                ps_y = pb(st, f"ps_y{tag}", 1024)
                rows_landed = sem(st, f"rows_landed{tag}")
                visited = sem(st, f"visited{tag}")
                idx_ready = sem(st, f"idx_ready{tag}")
                asked = sem(st, f"asked{tag}")
                high = sem(st, f"high{tag}")
                low = sem(st, f"low{tag}")
                hot_ready = sem(st, f"hot_ready{tag}")
                s_w = sem(st, f"s_w{tag}")
                s_scaled = sem(st, f"s_scaled{tag}")
                s_t = sem(st, f"s_t{tag}")
                s_tc = sem(st, f"s_tc{tag}")
                s_y = sem(st, f"s_y{tag}")
                s_b = sem(st, f"s_b{tag}")
                s_o = sem(st, f"s_o{tag}")
                s_st = sem(st, f"s_st{tag}")
                s_xl = sem(st, f"s_xl{tag}")

                def sums(par, c0, n):
                    return ps_sum[:, par * 1024 + c0:par * 1024 + c0 + n]

                def pair_of(t, g, slots):
                    return t[:, ds((g * 2) % slots, 2), :]
                with nc.Block() as block:

                    @block.gpsimd
                    def _(eng):
                        gather_rows(eng, table, [low], idx_ready, asked, lambda k: ring[:, k, :])

                    @block.sync
                    def _(eng):
                        eng.dma_start(w[:, :, :], wt.rearrange("(k p) n -> p k n", p=P)).then_inc(s_w, 16)
                        eng.dma_start(bias_b[:, :], bias.rearrange("(a n) -> a n", a=1).to_broadcast([P, D])).then_inc(s_w, 16)
                        relay_landed(eng, 0 if first else 1, rows_landed)

                    @block.scalar
                    def _(eng):
                        if first:
                            eng.sem_inc(s_o, 1)

                        def round_high(g):
                            eng.wait_ge(rows_landed, g * 2 + 2)
                            eng.wait_ge(visited, g + 1)
                            eng.activation(pair_of(parts[:, 0, :, :], g, 2 * HOTS), pair_of(ring, g, RING), ACT.Copy).then_inc(high, 1)

                        def step(j, par):
                            if not first and has(j, 3):
                                jj = j - 3
                                if not isinstance(j, int) or jj >= 1:
                                    eng.wait_ge(s_xl, jj * 16)
                                    eng.wait_ge(s_o, jj)
                                if isinstance(j, int) and jj == NT - 1:
                                    eng.dma_start(xt[0:LAST, 1 - par, :], x[jj * P:N, :]).then_inc(s_xl, 16)
                                else:
                                    whole = x[0:(NT - 1) * P, :].rearrange("(t p) d -> p t d", p=P)
                                    eng.dma_start(xt[:, 1 - par:2 - par, :], whole[:, ds(jj, 1), :]).then_inc(s_xl, 16)
                            if has(j, 0):
                                visits_of(eng, j, lambda g: round_high(g + AHEAD))
                            if has(j, 2):
                                eng.wait_ge(s_y, j - 2 + 1)
                                eng.wait_ge(s_t, j - 2 + 2)
                                eng.activation(sum_t[:, :], ps_t[:, 0:D], ACT.Copy).then_inc(s_tc, 1)
                            if has(j, 0):
                                end = eng.value_load(pair0[0:1, ds(j + 1, 1)], min_val=1, max_val=V // 2)
                                eng.wait_ge(visited, end + HOTS)
                                if not isinstance(j, int) or j >= 1:
                                    eng.wait_ge(s_t, j)
                                eng.activation(scaled[:, par, :], sums(par, 0, D), ACT.Copy, scale=dinv[:, ds(j, 1)]).then_inc(s_scaled, 1)
                            if first and has(j, 3):
                                jj = j - 3
                                eng.wait_ge(s_b, jj + 2)
                                eng.activation(nodes[:, ds(jj, 1), :].rearrange("p a d -> p (a d)"), tmp[:, :], ACT.Relu, scale=dinv[:, ds(jj, 1)]).then_inc(s_o, 1)
                                eng.wait_ge(s_o, jj + 2)
                                eng.dma_start(by_tile(table2)[:, ds(jj, 1), :], nodes[:, ds(jj, 1), :]).then_inc(s_st, 16)
                        for g in range(AHEAD):
                            round_high(g)
                        staged(eng, 5, step)
                        if first:
                            eng.wait_ge(s_st, NT * 16)

                    @block.tensor
                    def _(eng):
                        eng.sem_inc(visited, HOTS)
                        eng.sem_inc(s_t, 1)
                        eng.sem_inc(s_y, 1)
                        eng.wait_ge(s_w, 32)

                        def step(j, par):
                            if has(j, 0):
                                if not isinstance(j, int) or j >= 2:
                                    eng.wait_ge(s_scaled, j - 1)
                                for c0, n in HALVES:
                                    eng.matmul(sums(par, c0, n), ident[:, :], nodes[:, ds(j, 1), c0:c0 + n].rearrange("p a c -> p (a c)"), start=True, stop=True)

                                def visit(g):
                                    eng.wait_ge(low, g + RING // 2 + 1)
                                    eng.wait_ge(hot_ready, g + 1)

                                    def products(at):
                                        for k in range(at * 2, at * 2 + 2):
                                            for c0, n in HALVES:
                                                for t in range(2):
                                                    last = eng.matmul(sums(par, c0, n), hot[:, k, :], parts[:, t, k, c0:c0 + n],
                                                                      start=False, stop=True, skip_group_check=True)
                                        last.then_inc(visited, 1)
                                    by_pair(eng, g, products)
                                visits_of(eng, j, visit)
                            if has(j, 2):
                                jj = j - 2
                                eng.wait_ge(s_tc, jj + 1)
                                eng.wait_ge(s_b, jj + 1)
                                for c0, n in HALVES:
                                    for k in range(KB):
                                        last = eng.matmul(ps_y[:, c0:c0 + n], sum_t[:, k * P:(k + 1) * P], w[:, k, c0:c0 + n],
                                                          start=(k == 0), stop=(k == KB - 1))
                                last.then_inc(s_y, 1)
                            if has(j, 1):
                                eng.wait_ge(s_scaled, j)
                                for k in range(KB):
                                    last = eng.transpose(ps_t[:, k * P:(k + 1) * P], scaled[:, 1 - par, k * P:(k + 1) * P], ident[:, :])
                                last.then_inc(s_t, 1)
                        staged(eng, 3, step)

                    @block.vector
                    def _(eng):
                        eng.sem_inc(low, RING // 2)
                        eng.sem_inc(s_b, 1)
                        if not first:
                            eng.sem_inc(s_o, 1)
                        eng.wait_ge(s_w, 32)

                        def low_and_hot(g):
                            eng.wait_ge(high, g + 1)
                            eng.tensor_tensor(pair_of(parts[:, 1, :, :], g, 2 * HOTS), pair_of(ring, g, RING),
                                              pair_of(parts[:, 0, :, :], g, 2 * HOTS).bitcast(F32), ALU.subtract).then_inc(low, 1)
                            one_hots(eng, g, hot).then_inc(hot_ready, 1)

                        def step(j, par):
                            if has(j, 0):
                                visits_of(eng, j, low_and_hot)
                            if has(j, 3):
                                jj = j - 3
                                eng.wait_ge(s_y, jj + 2)
                                eng.wait_ge(s_o, jj + 1)
                                eng.tensor_tensor(tmp[:, :], ps_y[:, 0:D], bias_b[:, :], ALU.add).then_inc(s_b, 1)
                                if not first:
                                    eng.wait_ge(s_b, jj + 2)
                                    eng.wait_ge(s_xl, jj * 16 + 16)
                                    rows = LAST if isinstance(j, int) and jj == NT - 1 else P
                                    eng.tensor_tensor(nodes[0:rows, ds(jj, 1), :], tmp[0:rows, :].unsqueeze(1), xt[0:rows, 1 - par:2 - par, :], ALU.add).then_inc(s_o, 1)
                        staged(eng, 3, step)

        convolution("a", table1, w1t, b1, True)
        convolution("b", table2, w2t, b2, False)

        a2 = sb(ctx, "a2", [P, NT, H])
        with ExitStack() as st:
            stats = sb(st, "stats2", [P, NT, 2, 6])
            mv = sb(st, "mv2", [P, NT, 2])
            std = sb(st, "std2", [P, NT])
            bi = sb(st, "bi2", [P, NT])
            wfc2 = sb(st, "wfc2", [DH, 2, DH])
            attn_t = sb(st, "attn_t", [DH, 2 * H])
            blk = sb(st, "blk", [P, 4, DH])
            att_w = sb(st, "att_w", [P, KB, 4])
            h2 = sb(st, "h2", [P, 2, D])
            h2_t = sb(st, "h2_t", [P, D])
            ft = sb(st, "ft", [P, 2, KB, P])
            res = sb(st, "res", [P, 2, KB, P])
            a1 = sb(st, "a1", [P, 2, H])
            ps_t = pb(st, "ps_t2", 1024)
            ps_f = pb(st, "ps_f", KB * 2 * P)
            ps_a = pb(st, "ps_a")
            s_w = sem(st, "s_w2")
            s_z = sem(st, "s_z2")
            s_var = sem(st, "s_var2")
            s_sqrt = sem(st, "s_sqrt2")
            s_dve = sem(st, "s_dve2")
            s_blk = sem(st, "s_blk2")
            s_fold = sem(st, "s_fold2")
            s_ready = sem(st, "s_ready2")
            s_h2 = sem(st, "s_h2")
            s_t = sem(st, "s_t2")
            s_tc = sem(st, "s_tc2")
            s_f = sem(st, "s_f2")
            s_fc = sem(st, "s_fc2")
            s_rc = sem(st, "s_rc2")
            s_fst = [sem(st, f"s_fst2{k}") for k in range(2)]
            s_rst = [sem(st, f"s_rst2{k}") for k in range(2)]
            with nc.Block() as block:

                @block.sync
                def _(eng):
                    eng.dma_start(wfc2[:, 0, :], wfc).then_inc(s_w, 16)
                    eng.dma_start(wfc2[:, 1, :], wfc).then_inc(s_w, 16)
                    eng.dma_start(attn_t[:, 0:H], attn_lt).then_inc(s_w, 16)
                    eng.dma_start(attn_t[:, H:2 * H], attn_rt).then_inc(s_w, 16)
                    eng.wait_ge(s_z, 1)
                    for q, w in ((0, wfct), (2, wrest)):
                        eng.dma_start(blk[0:DH, q, :], w).then_inc(s_blk, 16)
                        eng.dma_start(blk[DH:P, q + 1, :], w).then_inc(s_blk, 16)
                    with eng.Fori(0, NT // 2) as i:
                        for par in range(2):
                            eng.wait_ge(s_rc, i * 2 + par + 2)
                            eng.dma_start(by_tile(res_table)[:, ds(i * 2 + par, 1), :], res[:, par:par + 1, :, :].rearrange("p a k c -> p a (k c)")).then_inc(s_rst[par], 16)
                            eng.dma_start(by_tile(a1_table)[:, ds(i * 2 + par, 1), :], a1[:, par:par + 1, :]).then_inc(s_rst[par], 16)
                    eng.wait_ge(s_rc, NT + 1)
                    eng.dma_start(by_tile(res_table)[:, NT - 1:NT, :], res[:, 0:1, :, :].rearrange("p a k c -> p a (k c)")).then_inc(s_rst[0], 16)
                    eng.dma_start(by_tile(a1_table)[:, NT - 1:NT, :], a1[:, 0:1, :]).then_inc(s_rst[0], 16)
                    eng.wait_ge(s_rst[0], 32 * (NT // 2 + 1))
                    eng.wait_ge(s_rst[1], 32 * (NT // 2))

                @block.vector
                def _(eng):
                    link = chained(eng, s_dve)
                    eng.memset(att_w[:, :, :], 0.0)
                    eng.memset(blk[:, :, :], 0.0).then_inc(s_z, 1)
                    eng.wait_ge(s_z, 1)
                    for j in range(NT):
                        for h in range(2):
                            last = eng.bn_stats(stats[:, j, h, :], nodes[:, j, h * D // 2:(h + 1) * D // 2])
                    link(last)
                    for j in range(NT):
                        last = eng.bn_aggr(mv[:, j, :], stats[:, j, :, :])
                    link(last)
                    eng.tensor_scalar(std[:, :], mv[:, :, 1], EPS, None, ALU.add).then_inc(s_var, 1)
                    eng.wait_ge(s_fold, 1)
                    for half, which in ((0, 0), (1, 1)):
                        rows = slice(half * DH, half * DH + DH)
                        for side in range(2):
                            v = ps_a[rows, side * H:(side + 1) * H].rearrange("p (k t) -> p k t", t=2)
                            last = eng.tensor_copy(att_w[rows, :, 2 * side + which], v[:, :, which])
                    link(last)
                    eng.wait_ge(s_sqrt, 1)
                    link(eng.reciprocal(std[:, :], std[:, :]))
                    link(eng.scalar_tensor_tensor(out=bi[:, :], in0=mv[:, :, 0], scalar=-1.0, in1=std[:, :], op0=ALU.mult, op1=ALU.mult))
                    eng.sem_inc(s_ready, 1)

                    def step(j, par, stored):
                        eng.wait_ge(s_t, j + 2)
                        eng.wait_ge(s_f, j + 1)
                        eng.tensor_copy(h2_t[:, :], ps_t[:, 0:D]).then_inc(s_tc, 1)
                        eng.wait_ge(s_f, j + 2)
                        eng.wait_ge(s_fc, j + 2)
                        if stored is not None:
                            eng.wait_ge(s_rst[par], stored)
                        eng.tensor_copy(res[:, par, :, :], ps_f[:, :].rearrange("p (k c) -> p k c", c=2 * P)[:, :, P:2 * P])
                        eng.tensor_copy(a1[:, par, :].rearrange("p (k t) -> p k t", t=2), ps_a[:, 0:4 * KB].rearrange("p (k t) -> p k t", t=4)[:, :, 0:2])
                        eng.tensor_copy(a2[:, ds(j, 1), :].rearrange("p a (k t) -> p (a k) t", t=2), ps_a[:, 0:4 * KB].rearrange("p (k t) -> p k t", t=4)[:, :, 2:4]).then_inc(s_rc, 1)
                    eng.sem_inc(s_rc, 1)
                    step(0, 0, None)
                    step(1, 1, None)
                    with eng.Fori(1, NT // 2) as i:
                        for par in range(2):
                            step(i * 2 + par, par, i * 32)
                    step(NT - 1, 0, 32 * (NT // 2))

                @block.scalar
                def _(eng):
                    eng.wait_ge(s_var, 1)
                    eng.activation(std[:, :], std[:, :], ACT.Sqrt).then_inc(s_sqrt, 1)
                    eng.wait_ge(s_ready, 1)

                    def norm(j, par):
                        eng.activation(h2[:, par, :], nodes[:, ds(j, 1), :].rearrange("p a d -> p (a d)"), ACT.Relu, bias=bi[:, ds(j, 1)], scale=std[:, ds(j, 1)]).then_inc(s_h2, 1)

                    def features(j, par, stored):
                        eng.wait_ge(s_f, j + 2)
                        if stored is not None:
                            eng.wait_ge(s_fst[par], stored)
                        eng.activation(ft[:, par, :, :], ps_f[:, :].rearrange("p (k c) -> p k c", c=2 * P)[:, :, 0:P], ACT.Copy).then_inc(s_fc, 1)
                        eng.wait_ge(s_fc, j + 2)
                        eng.dma_start(by_tile(table3)[:, ds(j, 1), :], ft[:, par:par + 1, :, :].rearrange("p a k c -> p a (k c)")).then_inc(s_fst[par], 16)
                    eng.sem_inc(s_fc, 1)
                    norm(0, 0)
                    norm(1, 1)
                    features(0, 0, None)
                    eng.wait_ge(s_t, 2)
                    norm(2, 0)
                    features(1, 1, None)
                    with eng.Fori(1, NT // 2) as i:
                        for par in range(2):
                            eng.wait_ge(s_t, i * 2 + par + 1)
                            norm(i * 2 + par + 1, 1 - par)
                            features(i * 2 + par, par, i * 16)
                    features(NT - 1, 0, 16 * (NT // 2))
                    eng.wait_ge(s_fst[0], 16 * (NT // 2 + 1))
                    eng.wait_ge(s_fst[1], 16 * (NT // 2))

                @block.tensor
                def _(eng):
                    eng.sem_inc(s_t, 1)
                    eng.sem_inc(s_f, 1)
                    eng.wait_ge(s_w, 64)
                    eng.matmul(ps_a[:, 0:2 * H], wfc2[:, :, :].rearrange("p a d -> p (a d)"), attn_t[:, :], start=True, stop=True).then_inc(s_fold, 1)
                    eng.wait_ge(s_blk, 64)
                    eng.wait_ge(s_ready, 1)

                    def step(j, par):
                        eng.wait_ge(s_h2, j + 1)
                        for k in range(KB):
                            last = eng.transpose(ps_t[:, k * P:(k + 1) * P], h2[:, par, k * P:(k + 1) * P], ident[:, :])
                        last.then_inc(s_t, 1)
                        eng.wait_ge(s_tc, j + 1)
                        eng.wait_ge(s_fc, j + 1)
                        eng.wait_ge(s_rc, j + 1)
                        for k in range(KB):
                            eng.matmul(ps_f[:, k * 2 * P:(k + 1) * 2 * P], h2_t[:, k * P:(k + 1) * P], blk[:, :, :].rearrange("p a c -> p (a c)"), start=True, stop=True)
                            last = eng.matmul(ps_a[:, 4 * k:4 * k + 4], h2_t[:, k * P:(k + 1) * P], att_w[:, k, :], start=True, stop=True)
                        last.then_inc(s_f, 1)
                    with eng.Fori(0, NT // 2) as i:
                        for par in range(2):
                            step(i * 2 + par, par)
                    step(NT - 1, 0)

        weights = sb(ctx, "weights", [P, V + 2 * AHEAD, H])
        with ExitStack() as st:
            a2e = sb(st, "a2e", [P, V, H])
            cont = sb(st, "cont", [SPT, SL], BF16)
            ends = sb(st, "ends", [SPT, 3])
            perm = sb(st, "perm", [P, SW, SG, H])

            with ExitStack() as st1:
                a1_slot = sb(st1, "a1_slot", [P, 2, SMALL, H])
                hots = sb(st1, "hots", [P, 2, GROUP, P])
                hots_t = sb(st1, "hots_t", [P, 2, GROUP * P])
                ps_ht = [pb(st1, f"ps_ht{k}", GROUP * P) for k in range(2)]
                ps_e = [pb(st1, f"ps_e{k}") for k in range(2)]
                small_landed = [sem(st1, f"small_landed{k}") for k in range(2)]
                s_used = sem(st1, "s_used")
                idx_ready = sem(st1, "idx_ready_s")
                asked = sem(st1, "asked_s")
                s_hot = sem(st1, "s_hots")
                s_ht = sem(st1, "s_ht")
                s_htc = sem(st1, "s_htc")
                s_e = sem(st1, "s_e")
                s_ec = sem(st1, "s_ec")
                groups = V // GROUP

                with nc.Block() as block:

                    @block.gpsimd
                    def _(eng):
                        with eng.Fori(0, V // (2 * SMALL)) as i:
                            for half in range(2):
                                eng.wait_ge(s_used, i * 2 + half + 1)
                                eng.tensor_copy(idx_slot[half][:, 0:SMALL], idx[:, ds((i * 2 + half) * SMALL, SMALL)]).then_inc(idx_ready, 1)
                                eng.wait_ge(idx_ready, i * 2 + half + 1)
                                eng.sem_inc(asked, 1)
                                for k in range(SMALL):
                                    eng.indirect_dma_start(out=a1_slot[:, half, k, :], out_offset=None, in_=a1_table,
                                                           in_offset=bass.IndirectOffsetOnAxis(ap=idx_slot[half][:, k:k + 1], axis=0)).then_inc(small_landed[half], 16)

                    @block.vector
                    def _(eng):
                        def one_hots(g, par):
                            eng.wait_ge(s_ht, g + 1)
                            eng.tensor_tensor(hots[:, par, :, :], iota1[:, :].unsqueeze(1).to_broadcast([P, GROUP, P]),
                                              dl1[:, ds(g * GROUP, GROUP)].unsqueeze(2).to_broadcast([P, GROUP, P]), ALU.is_equal).then_inc(s_hot, 1)

                        def terms(g, par):
                            eng.wait_ge(s_e, g + 1)
                            eng.tensor_copy(a2e[:, ds(g * GROUP, GROUP), :].rearrange("p v h -> p (v h)"), ps_e[par][:, 0:GROUP * H]).then_inc(s_ec, 1)
                        one_hots(0, 0)
                        with eng.Fori(0, groups // 2 - 1) as i:
                            for par in range(2):
                                one_hots(i * 2 + par + 1, 1 - par)
                                terms(i * 2 + par, par)
                        one_hots(groups - 1, 1)
                        terms(groups - 2, 0)
                        terms(groups - 1, 1)

                    @block.tensor
                    def _(eng):
                        eng.sem_inc(s_ht, 2)

                        def transposes(g, par):
                            eng.wait_ge(s_hot, g + 1)
                            for k in range(GROUP):
                                last = eng.transpose(ps_ht[par][:, k * P:(k + 1) * P], hots[:, par, k, :], ident[:, :])
                            last.then_inc(s_ht, 1)

                        def products(g, par):
                            eng.wait_ge(s_htc, g + 1)
                            for k in range(GROUP):
                                tile = eng.value_load(tile_of[0:1, ds(g * GROUP + k, 1)], min_val=0, max_val=NT - 1)
                                last = eng.matmul(ps_e[par][:, k * H:(k + 1) * H], hots_t[:, par, k * P:(k + 1) * P], a2[:, ds(tile, 1), :], start=True, stop=True)
                            last.then_inc(s_e, 1)
                        transposes(0, 0)
                        with eng.Fori(0, groups // 2 - 1) as i:
                            for par in range(2):
                                transposes(i * 2 + par + 1, 1 - par)
                                products(i * 2 + par, par)
                        transposes(groups - 1, 1)
                        products(groups - 2, 0)
                        products(groups - 1, 1)

                    @block.scalar
                    def _(eng):
                        eng.sem_inc(s_used, 2)
                        with eng.Fori(0, V // (2 * SMALL)) as i:
                            for half in range(2):
                                for par in range(2):
                                    g = i * 4 + half * 2 + par
                                    eng.wait_ge(s_ht, g + 3)
                                    eng.activation(hots_t[:, par, :], ps_ht[par][:, 0:GROUP * P], ACT.Copy).then_inc(s_htc, 1)
                                eng.wait_ge(small_landed[half], (i + 1) * 16 * SMALL)
                                eng.activation(weights[:, ds((i * 2 + half) * SMALL, SMALL), :], a1_slot[:, half, :, :], ACT.Copy).then_inc(s_used, 1)

            with ExitStack() as st1:
                key = sb(st1, "key", [P, V])
                keys = sb(st1, "keys", [SPT, SL])
                ps_k = [pb(st1, f"ps_k{k}") for k in range(4)]
                s_dve = sem(st1, "s_dve_k")
                s_perm = sem(st1, "s_perm_k")
                s_t = sem(st1, "s_t_k")
                s_c = sem(st1, "s_c_k")
                with nc.Block() as block:

                    @block.vector
                    def _(eng):
                        link = chained(eng, s_dve)
                        link(eng.tensor_scalar(key[:, :], dl1[:, 0:V], 1.0, None, ALU.is_ge))
                        link(eng.scalar_tensor_tensor(out=key[:, :], in0=dl1[:, 0:V], scalar=float(P), in1=key[:, :], op0=ALU.is_le, op1=ALU.mult))
                        link(eng.tensor_tensor(key[:, :], key[:, :], d1v[:, :], ALU.mult))
                        eng.tensor_copy(perm[:, :, :, :], key[:, :].rearrange("p (g w) -> p w g", w=SW).unsqueeze(3).to_broadcast([P, SW, SG, H])).then_inc(s_perm, 1)
                        eng.wait_ge(s_c, SW // 4)
                        link(eng.tensor_tensor(cont[:, 1:SL], keys[:, 1:SL], keys[:, 0:SL - 1], ALU.is_equal))
                        link(eng.tensor_scalar(cont[:, 1:SL], cont[:, 1:SL], -1.0, BIG, ALU.add, ALU.mult))
                        link(eng.memset(cont[:, 0:1], -BIG))
                        link(eng.tensor_copy(ends[:, 0:1], keys[:, 0:1]))
                        link(eng.tensor_copy(ends[:, 1:2], keys[:, SL - 1:SL]))

                    @block.tensor
                    def _(eng):
                        eng.wait_ge(s_perm, 1)
                        for q in range(SW // 4):
                            if q >= 4:
                                eng.wait_ge(s_c, q - 3)
                            for k in range(4):
                                last = eng.transpose(ps_k[q % 4][0:SPT, k * P:(k + 1) * P], perm[:, q * 4 + k, :, :].rearrange("p g h -> p (g h)"), ident[:, :])
                            last.then_inc(s_t, 1)

                    @block.scalar
                    def _(eng):
                        for q in range(SW // 4):
                            eng.wait_ge(s_t, q + 1)
                            eng.activation(keys[:, q * 4 * P:(q + 1) * 4 * P], ps_k[q % 4][0:SPT, :], ACT.Copy).then_inc(s_c, 1)

            with ExitStack() as st1:
                run = sb(st1, "run", [SPT, SL])
                row = sb(st1, "row", [1, 14, SPT])
                carry = sb(st1, "carry", [SPT, 2])
                one1 = sb(st1, "one1", [1, 1])
                ps_a = [pb(st1, f"ps_a{k}") for k in range(4)]
                ps_r = pb(st1, "ps_r")
                ps_m = pb(st1, "ps_m")
                s_dve = sem(st1, "s_dve_m")
                s_perm = sem(st1, "s_perm_m")
                s_t = sem(st1, "s_t_m")
                s_c = sem(st1, "s_c_m")
                s_scan = sem(st1, "s_scan")
                s_row = sem(st1, "s_row_m")
                s_car = sem(st1, "s_car")
                s_cc = sem(st1, "s_cc")
                s_mt = sem(st1, "s_mt")
                s_mc = sem(st1, "s_mc")
                s_z = sem(st1, "s_z_m")
                s_d = sem(st1, "s_d_m")
                R_FIRST, R_LAST, R_MAX, R_LINK, R_WHOLE, R_GO, R_ACC, R_IN, R_T = range(9)

                def by_head(r):
                    return row[:, r, :].rearrange("a (h g) -> a h g", g=SG)
                with nc.Block() as block:

                    @block.vector
                    def _(eng):
                        link = chained(eng, s_dve)
                        link(eng.memset(one1[:, :], 1.0))
                        link(eng.memset(weights[:, V:V + 2 * AHEAD, :], 0.0))
                        eng.tensor_copy(perm[:, :, :, :], weights[:, 0:V, :].rearrange("p (g w) h -> p w g h", w=SW)).then_inc(s_perm, 1)
                        eng.wait_ge(s_c, SW // 4)
                        fwd, bwd = slice(None), slice(None, None, -1)

                        def carries(back):
                            lo_, hi_ = (slice(1, SG), slice(0, SG - 1))
                            cur, prev = (hi_, lo_) if back else (lo_, hi_)
                            head_end = slice(SG - 1, SG) if back else slice(0, 1)
                            a, b = (R_LAST, R_FIRST) if back else (R_FIRST, R_LAST)
                            link(eng.memset(row[:, R_LINK, :], -BIG))
                            link(eng.tensor_tensor(by_head(R_LINK)[:, :, cur], by_head(a)[:, :, cur], by_head(b)[:, :, prev], ALU.is_equal))
                            link(eng.tensor_scalar(by_head(R_LINK)[:, :, cur], by_head(R_LINK)[:, :, cur], -1.0, BIG, ALU.add, ALU.mult))
                            link(eng.tensor_tensor(row[:, R_WHOLE, :], row[:, R_FIRST, :], row[:, R_LAST, :], ALU.is_equal))
                            link(eng.tensor_scalar(row[:, R_WHOLE, :], row[:, R_WHOLE, :], -1.0, BIG, ALU.add, ALU.mult))
                            link(eng.tensor_tensor(row[:, R_GO, :], row[:, R_LINK, :], row[:, R_WHOLE, :], ALU.min))
                            d = bwd if back else fwd
                            link(eng.tensor_tensor_scan(row[:, R_ACC, :][:, d], row[:, R_GO, :][:, d], row[:, R_MAX, :][:, d], -BIG, ALU.add, ALU.max))
                            link(eng.memset(row[:, R_IN, :], -BIG))
                            link(eng.tensor_tensor(by_head(R_IN)[:, :, cur], by_head(R_ACC)[:, :, prev], by_head(R_LINK)[:, :, cur], ALU.add))
                            link(eng.tensor_scalar(row[:, R_IN, :], row[:, R_IN, :], -BIG, None, ALU.max))
                            link(eng.tensor_copy(row[:, R_T, :].rearrange("a (g h) -> a g h", h=H), by_head(R_IN).rearrange("a h g -> a g h")))

                        link(eng.tensor_tensor_scan(run[:, :], cont[:, :], run[:, :], -BIG, ALU.add, ALU.max))
                        link(eng.tensor_copy(ends[:, 2:3], run[:, SL - 1:SL]))
                        eng.sem_inc(s_scan, 1)
                        eng.wait_ge(s_row, 1)
                        for r in (R_FIRST, R_LAST, R_MAX):
                            link(eng.tensor_copy(by_head(r).rearrange("a h g -> a g h"), ps_r[0:1, r * P:r * P + SPT].rearrange("a (g h) -> a g h", h=H)))
                        carries(False)
                        eng.sem_inc(s_scan, 1)
                        eng.wait_ge(s_row, 2)
                        link(eng.tensor_copy(carry[:, 0:1], ps_m[0:SPT, 0:1]))
                        link(eng.memset(cont[:, 0:1], 0.0))
                        link(eng.tensor_tensor_scan(run[:, :], cont[:, :], run[:, :], carry[:, 0:1], ALU.add, ALU.max))
                        link(eng.memset(cont[:, 0:1], -BIG))
                        eb = run[:, 0:SL - 1][:, bwd]
                        cb = cont[:, 1:SL][:, bwd]
                        link(eng.tensor_tensor_scan(eb, cb, eb, run[:, SL - 1:SL], ALU.add, ALU.max))
                        link(eng.tensor_copy(ends[:, 2:3], run[:, 0:1]))
                        eng.sem_inc(s_scan, 1)
                        eng.wait_ge(s_row, 3)
                        link(eng.tensor_copy(by_head(R_MAX).rearrange("a h g -> a g h"), ps_r[0:1, R_MAX * P:R_MAX * P + SPT].rearrange("a (g h) -> a g h", h=H)))
                        carries(True)
                        eng.sem_inc(s_scan, 1)
                        eng.wait_ge(s_row, 4)
                        link(eng.tensor_copy(carry[:, 1:2], ps_m[0:SPT, 1:2]))
                        link(eng.tensor_tensor(run[:, SL - 1:SL], run[:, SL - 1:SL], carry[:, 1:2], ALU.max))
                        link(eng.tensor_tensor_scan(eb, cb, eb, run[:, SL - 1:SL], ALU.add, ALU.max))
                        eng.sem_inc(s_scan, 1)
                        def flat(t):
                            return t.rearrange("p v h -> p (v h)")
                        w_, e_ = flat(weights[:, 0:V, :]), flat(a2e[:, :, :])
                        m_ = perm[:, :, :, :].rearrange("p w g h -> p (w g h)")
                        link(eng.tensor_tensor(w_, w_, e_, ALU.add))
                        link(eng.scalar_tensor_tensor(out=w_, in0=w_, scalar=SLOPE, in1=w_, op0=ALU.mult, op1=ALU.max))
                        eng.wait_ge(s_mc, SW // 4)
                        link(eng.tensor_tensor(m_, m_, e_, ALU.add))
                        link(eng.scalar_tensor_tensor(out=m_, in0=m_, scalar=SLOPE, in1=m_, op0=ALU.mult, op1=ALU.max))
                        eng.tensor_tensor(w_, w_, m_, ALU.subtract).then_inc(s_d, 1)

                    @block.tensor
                    def _(eng):
                        eng.wait_ge(s_perm, 1)
                        for q in range(SW // 4):
                            if q >= 4:
                                eng.wait_ge(s_c, q - 3)
                            for k in range(4):
                                last = eng.transpose(ps_a[q % 4][0:SPT, k * P:(k + 1) * P], perm[:, q * 4 + k, :, :].rearrange("p g h -> p (g h)"), ident[:, :])
                            last.then_inc(s_t, 1)
                        for back in range(2):
                            eng.wait_ge(s_scan, 2 * back + 1)
                            for r in range(3) if not back else (2,):
                                last = eng.transpose(ps_r[0:1, r * P:r * P + SPT], ends[:, r:r + 1], ident[0:SPT, 0:SPT])
                            last.then_inc(s_row, 1)
                            eng.wait_ge(s_scan, 2 * back + 2)
                            eng.matmul(ps_m[0:SPT, back:back + 1], row[:, R_T, :], one1[:, :], start=True, stop=True).then_inc(s_row, 1)
                        eng.wait_ge(s_scan, 5)
                        for q in range(SW // 4):
                            eng.wait_ge(s_c, SW // 4) if q < 4 else eng.wait_ge(s_mc, q - 3)
                            for k in range(4):
                                last = eng.transpose(ps_a[q % 4][:, k * P:k * P + SPT], run[:, (q * 4 + k) * P:(q * 4 + k + 1) * P], ident[0:SPT, 0:SPT])
                            last.then_inc(s_mt, 1)

                    @block.scalar
                    def _(eng):
                        for q in range(SW // 4):
                            eng.wait_ge(s_t, q + 1)
                            eng.activation(run[:, q * 4 * P:(q + 1) * 4 * P], ps_a[q % 4][0:SPT, :], ACT.Copy).then_inc(s_c, 1)
                        back = perm[:, :, :, :].rearrange("p w g h -> p (w g h)").rearrange("p (g w h) -> p w g h", g=SG, h=H)
                        for q in range(SW // 4):
                            eng.wait_ge(s_mt, q + 1)
                            for k in range(4):
                                last = eng.activation(back[:, q * 4 + k, :, :], ps_a[q % 4][:, k * P:k * P + SPT].rearrange("p (g h) -> p g h", h=H), ACT.Copy)
                            last.then_inc(s_mc, 1)
                        eng.wait_ge(s_d, 1)
                        w_ = weights[:, 0:V, :].rearrange("p v h -> p (v h)")
                        eng.activation(w_, w_, ACT.Exp).then_inc(s_z, 1)

        with ExitStack() as st:
            HA = 3
            ring = sb(st, "ring_g", [P, RING, D])
            hot = sb(st, "hot_g", [P, 2 * HOTS, P])
            msg = sb(st, "msg", [P, 2 * HOTS, D + H])
            zeros = sb(st, "zeros", [P, 512], BF16)
            rden = sb(st, "rden", [P, H])
            res = sb(st, "res_l", [P, 2, D])
            o = sb(st, "o", [P, 2, D])
            ps_sum = pb(st, "ps_sum_g", 2048)
            rows_landed = sem(st, "rows_landed_g")
            visited = sem(st, "visited_g")
            idx_ready = sem(st, "idx_ready_g")
            asked = sem(st, "asked_g")
            hot_ready = sem(st, "hot_ready_g")
            scaled_a = sem(st, "scaled_a")
            scaled_v = sem(st, "scaled_v")
            s_r = sem(st, "s_r")
            s_out = sem(st, "s_out")
            s_end = sem(st, "s_end")
            s_zero = sem(st, "s_zero_g")
            s_st = sem(st, "s_st_g")
            s_stored = sem(st, "s_stored_g")

            def sums(par, c0, n):
                return ps_sum[:, par * 1024 + c0:par * 1024 + c0 + n]

            def row_at(t, g, k, slots, c0, n):
                return t[:, ds((g * 2) % slots + k, 1), c0:c0 + n].rearrange("p s c -> p (s c)")
            with nc.Block() as block:

                @block.gpsimd
                def _(eng):
                    gather_rows(eng, table3, [scaled_a, scaled_v], idx_ready, asked, lambda k: ring[:, k, :])

                @block.sync
                def _(eng):
                    relay_landed(eng, 2, rows_landed)

                @block.scalar
                def _(eng):
                    eng.sem_inc(scaled_a, RING // 2)

                    def scale(g):
                        eng.wait_ge(rows_landed, g * 2 + 2)
                        eng.wait_ge(visited, g + 1)
                        for k in range(2):
                            for h in range(HA):
                                eng.activation(row_at(msg, g, k, 2 * HOTS, h * DH, DH), row_at(ring, g, k, RING, h * DH, DH), ACT.Copy,
                                               scale=weights[:, ds(g * 2 + k, 1), h:h + 1].rearrange("p a h -> p (a h)"))
                        eng.activation(msg[:, ds((g * 2) % (2 * HOTS), 2), D:D + H], weights[:, ds(g * 2, 2), :], ACT.Copy).then_inc(scaled_a, 1)

                    def step(j, par):
                        if has(j, 1):
                            jj = j - 1
                            if not isinstance(j, int) or jj >= 1:
                                eng.wait_ge(s_r, jj * 16)
                                eng.wait_ge(s_out, jj + 1)
                            eng.dma_start(res[:, 1 - par:2 - par, :], by_tile(res_table)[:, ds(jj, 1), :]).then_inc(s_r, 16)
                        if has(j, 0):
                            visits_of(eng, j, lambda g: scale(g + AHEAD))
                        if has(j, 1):
                            if not isinstance(j, int) or jj >= 1:
                                eng.wait_ge(s_st, jj * 16)
                                eng.sem_inc(s_stored, 1)
                            eng.wait_ge(s_out, jj + 3)
                            if isinstance(j, int) and jj == NT - 1:
                                eng.dma_start(out[jj * P:N, :], o[0:LAST, 1 - par, :]).then_inc(s_st, 16)
                            else:
                                whole = out[0:(NT - 1) * P, :].rearrange("(t p) d -> p t d", p=P)
                                eng.dma_start(whole[:, ds(jj, 1), :], o[:, 1 - par:2 - par, :]).then_inc(s_st, 16)
                    for g in range(AHEAD):
                        scale(g)
                    staged(eng, 3, step)
                    eng.wait_ge(s_st, NT * 16)

                @block.tensor
                def _(eng):
                    eng.sem_inc(visited, HOTS)
                    eng.wait_ge(s_zero, 1)

                    def step(j, par):
                        if has(j, 0):
                            if not isinstance(j, int) or j >= 2:
                                eng.wait_ge(s_out, j + 1)
                            for c0, n in ((0, 512), (512, D + H - 512)):
                                eng.matmul(sums(par, c0, n), zeros[:, 0:P], zeros[:, 0:n], start=True, stop=True)

                            def visit(g):
                                eng.wait_ge(scaled_a, g + RING // 2 + 1)
                                eng.wait_ge(scaled_v, g + RING // 2 + 1)
                                eng.wait_ge(hot_ready, g + 1)

                                def products(at):
                                    for k in range(at * 2, at * 2 + 2):
                                        for c0, n in ((0, 512), (512, D + H - 512)):
                                            last = eng.matmul(sums(par, c0, n), hot[:, k, :], msg[:, k, c0:c0 + n],
                                                              start=False, stop=True, skip_group_check=True)
                                    last.then_inc(visited, 1)
                                by_pair(eng, g, products)
                            visits_of(eng, j, visit)
                    staged(eng, 3, step)

                @block.vector
                def _(eng):
                    eng.memset(zeros[:, :], 0.0).then_inc(s_zero, 1)
                    eng.sem_inc(s_out, 2)

                    eng.sem_inc(scaled_v, RING // 2)

                    def scale_and_hot(g):
                        eng.wait_ge(rows_landed, g * 2 + 2)
                        eng.wait_ge(visited, g + 1)
                        to, of = (t[:, ds((g * 2) % slots, 2), HA * DH:D].rearrange("p a (h d) -> p a h d", d=DH) for t, slots in ((msg, 2 * HOTS), (ring, RING)))
                        eng.tensor_tensor(to, of, weights[:, ds(g * 2, 2), HA:H].unsqueeze(3).to_broadcast([P, 2, H - HA, DH]), ALU.mult).then_inc(scaled_v, 1)
                        one_hots(eng, g, hot).then_inc(hot_ready, 1)

                    def step(j, par):
                        if has(j, 0):
                            visits_of(eng, j, scale_and_hot)
                        if has(j, 1):
                            jj = j - 1
                            end = eng.value_load(pair0[0:1, ds(jj + 1, 1)], min_val=1, max_val=V // 2)
                            eng.wait_ge(visited, end + HOTS)
                            o_ = o[:, 1 - par:2 - par, :].rearrange("p a d -> p (a d)")
                            eng.tensor_scalar(rden[:, :], sums(1 - par, D, H), 0.5, None, ALU.max).then_inc(s_end, 1)
                            eng.wait_ge(s_end, jj * 4 + 1)
                            eng.reciprocal(rden[:, :], rden[:, :]).then_inc(s_end, 1)
                            eng.wait_ge(s_end, jj * 4 + 2)
                            if not isinstance(j, int) or jj >= 2:
                                eng.wait_ge(s_stored, jj - 1)
                            eng.tensor_tensor(o_.rearrange("p (h d) -> p h d", d=DH), sums(1 - par, 0, D).rearrange("p (h d) -> p h d", d=DH),
                                              rden[:, :].unsqueeze(2).to_broadcast([P, H, DH]), ALU.mult).then_inc(s_end, 1)
                            eng.wait_ge(s_end, jj * 4 + 3)
                            eng.wait_ge(s_r, jj * 16 + 16)
                            eng.tensor_tensor(o_, o_, res[:, 1 - par:2 - par, :].rearrange("p a d -> p (a d)"), ALU.add).then_inc(s_end, 1)
                            eng.wait_ge(s_end, jj * 4 + 4)
                            eng.scalar_tensor_tensor(out=o_, in0=o_, scalar=0.0, in1=nodes[:, ds(jj, 1), :].rearrange("p a d -> p (a d)"), op0=ALU.max, op1=ALU.add).then_inc(s_out, 1)
                    staged(eng, 3, step)


def kernel(**inputs):
    import numpy as np
    import concourse.bacc as bacc
    from concourse.bass_utils import run_bass_kernel_spmd

    nc = bacc.Bacc("TRN2", target_bir_lowering=False, num_devices=1)
    given = {k: np.asarray(v) for k, v in inputs.items()}
    laid = {
        "x": given["x"], "src": given["src"], "dst": given["dst"],
        "w1t": given["L0_gnn_W1"].T, "b1": given["L0_gnn_b1"],
        "w2t": given["L0_gnn_W2"].T, "b2": given["L0_gnn_b2"],
        "wfc": given["L1_gnn_W_fc"], "wfct": given["L1_gnn_W_fc"].T,
        "attn_lt": given["L1_gnn_attn_l"].T, "attn_rt": given["L1_gnn_attn_r"].T,
        "wrest": given["L1_gnn_W_res"].T,
    }
    arrays, args = {}, []
    for name, a in laid.items():
        a = np.ascontiguousarray(a)
        arrays[f"in_{name}"] = a
        args.append(nc.dram_tensor(f"in_{name}", a.shape, mybir.dt.from_np(a.dtype), kind="ExternalInput").ap())
    args.append(nc.dram_tensor("out_x", (N, D), F32, kind="ExternalOutput").ap())
    gnn_kernel(nc, *args)
    r = run_bass_kernel_spmd(nc, [arrays], core_ids=[0])
    return r.results[0]["out_x"]
```

```python
from contextlib import ExitStack

import concourse.bass as bass
from concourse import mybir

F32 = mybir.dt.float32
F32R = mybir.dt.float32r
BF16 = mybir.dt.bfloat16
I32 = mybir.dt.int32
ALU = mybir.AluOpType
ACT = mybir.ActivationFunctionType
ds = bass.ds

P = 128
N = 3125
D = 768
E = 50000
H = 12
DH = D // H
NT = -(-N // P)
LAST = N - (NT - 1) * P
NCH = -(-E // P)
V = (NCH + NT + NT) // 2 * 2
RING = 10
AHEAD = 2
GROUP = 10
BYPE = 4
HB = 4
HOTS = 5
KB = D // P
HALVES = [(0, 512), (512, D - 512)]
CB = -(-NCH // P)
EB = E // P // P
EPS = 1e-5
SLOPE = 0.2
BIG = 3.0e38
PH = P // 2
HSTEP = 14
HCOLS = -(-NCH // (2 * HSTEP)) * 2 * HSTEP
HFULL = E // P
HREST = E - HFULL * P
XG = 5
SG = 10
SW = V // SG
SPT = SG * H
SL = SW * P
assert V % (4 * GROUP) == 0 and GROUP % 2 == 0 and RING % 2 == 0 and HCOLS % (2 * HSTEP) == 0 and NT % XG == 0 and V % SG == 0 and SW % 4 == 0


def gnn_kernel(nc, x, src, dst, w1t, b1, w2t, b2, wfc, wfct, attn_lt, attn_rt, wrest, out):
    ctx = ExitStack()

    def sb(stack, name, shape, dt=F32):
        return stack.enter_context(nc.sbuf_tensor(name, shape, dt))

    def pb(stack, name, cols=512, dt=F32):
        return stack.enter_context(nc.psum_tensor(name, [P, cols], dt))

    def sem(stack, name):
        return stack.enter_context(nc.semaphore(name))

    def chained(eng, s):
        n = [0]

        def link(ins):
            n[0] += 1
            ins.then_inc(s, 1)
            eng.wait_ge(s, n[0])
        return link

    with ctx:
        table1 = nc.dram_tensor("table1", (NT * P, D), F32).ap()
        table2 = nc.dram_tensor("table2", (NT * P, D), F32).ap()
        table3 = nc.dram_tensor("table3", (NT * P, D), F32).ap()
        a1_table = nc.dram_tensor("a1_table", (NT * P, H), F32).ap()
        res_table = nc.dram_tensor("res_table", (NT * P, D), F32).ap()

        def by_tile(t):
            return t.rearrange("(t p) d -> p t d", p=P)

        nodes = sb(ctx, "nodes", [P, NT, D])
        ident = sb(ctx, "ident", [P, P])
        iota1 = sb(ctx, "iota1", [P, P])
        dl1 = sb(ctx, "dl1", [P, V])
        d1v = sb(ctx, "d1v", [P, V])
        idx = sb(ctx, "idx", [P, V], I32)
        tile_of = sb(ctx, "tile_of", [1, V], I32)
        pair0 = sb(ctx, "pair0", [1, NT + 1], I32)
        dinv = sb(ctx, "dinv", [P, NT])
        landed = [sem(ctx, f"landed{k}") for k in range(RING)]
        idx_slot = [sb(ctx, f"idx_slot{h}", [P, RING], I32) for h in range(2)]

        with ExitStack() as st:
            hist_dst = sb(st, "hist_dst", [P, HCOLS], I32)
            lo_i = sb(st, "lo_i", [P, HCOLS], I32)
            hi_i = sb(st, "hi_i", [P, HCOLS], I32)
            lo = sb(st, "lo", [P, HCOLS], BF16)
            hi = sb(st, "hi", [P, HCOLS], BF16)
            hi_hot = sb(st, "hi_hot", [P, 2, HSTEP, 2 * NT], BF16)
            lo_hot = sb(st, "lo_hot", [P, 2, HSTEP, PH], BF16)
            iota0b = sb(st, "iota0b", [P, P], BF16)
            iota_v = sb(st, "iota_v", [P, V])
            rowno = sb(st, "rowno", [P, CB])
            zeros_b = sb(st, "zeros_b", [P, P], BF16)
            ones = sb(st, "ones", [P, P])
            tri = sb(st, "tri", [NT, NT])
            src_i = sb(st, "src_i", [P, CB, P], I32)
            dst_i = sb(st, "dst_i", [P, CB, P], I32)
            src_f = sb(st, "src_f", [P, CB, P])
            dst_f = sb(st, "dst_f", [P, CB, P])
            counts = sb(st, "counts", [P, NT])
            c = sb(st, "c", [NT, 16])
            ci = sb(st, "ci", [NT, 4], I32)
            at_least = sb(st, "at_least", [NT, V])
            sel = sb(st, "sel", [NT, V])
            off_b = sb(st, "off_b", [NT, P])
            tile_b = sb(st, "tile_b", [NT, P])
            chunk_v = sb(st, "chunk_v", [P, V])
            chunk_hot = sb(st, "chunk_hot", [P, CB, V])
            stats = sb(st, "stats", [P, NT, 2, 6])
            mv = sb(st, "mv", [P, NT, 2])
            std = sb(st, "std", [P, NT])
            sc = sb(st, "sc", [P, NT])
            bi = sb(st, "bi", [P, NT])
            ps_h = pb(st, "ps_h", NT)
            ps_c = pb(st, "ps_c")
            ps_off = pb(st, "ps_off")
            ps_tile = pb(st, "ps_tile")
            ps_d = pb(st, "ps_d")
            ps_s = pb(st, "ps_s")
            s_fill = sem(st, "s_fill")
            s_hd = sem(st, "s_hd")
            s_ed = sem(st, "s_ed")
            s_x = [sem(st, f"s_x{g}") for g in range(NT // XG)]
            s_pool = sem(st, "s_pool")
            s_dve = sem(st, "s_dve")
            s_lo = sem(st, "s_lo")
            s_hdone = sem(st, "s_hdone")
            s_counts = sem(st, "s_counts")
            s_pe = sem(st, "s_pe")
            s_step = sem(st, "s_step")
            s_sqrt = sem(st, "s_sqrt")
            s_var = sem(st, "s_var")
            s_scale = sem(st, "s_scale")
            s_row = sem(st, "s_row")
            s_st = sem(st, "s_st")
            FILL = 5
            POOL = 9
            with nc.Block() as block:

                @block.sync
                def _(eng):
                    eng.wait_ge(s_fill, FILL)
                    eng.dma_start(hist_dst[:, 0:HFULL], dst[0:HFULL * P].rearrange("(p c) -> p c", p=P)).then_inc(s_hd, 16)
                    eng.dma_start(hist_dst[0:HREST, HFULL:HFULL + 1], dst[HFULL * P:E].rearrange("(p c) -> p c", c=1)).then_inc(s_hd, 16)
                    whole = EB * P * P
                    rows = (E - whole) // P
                    for v, t in ((src, src_i), (dst, dst_i)):
                        eng.dma_start(t[:, 0:EB, :], v[0:whole].rearrange("(b q e) -> q b e", q=P, e=P)).then_inc(s_ed, 16)
                        eng.dma_start(t[0:rows, EB, :], v[whole:whole + rows * P].rearrange("(q e) -> q e", e=P)).then_inc(s_ed, 16)
                        eng.dma_start(t[rows:rows + 1, EB, 0:E - whole - rows * P], v[whole + rows * P:E].rearrange("(a e) -> a e", a=1)).then_inc(s_ed, 16)
                    for g in range(NT // XG):
                        r0, r1 = g * XG * P, min((g + 1) * XG * P, N)
                        full = (r1 - r0) // P
                        eng.dma_start(nodes[:, g * XG:g * XG + full, :], x[r0:r0 + full * P, :].rearrange("(t p) d -> p t d", p=P)).then_inc(s_x[g], 16)
                        if r0 + full * P < r1:
                            eng.dma_start(nodes[0:r1 - r0 - full * P, g * XG + full, :], x[r0 + full * P:r1, :]).then_inc(s_x[g], 16)
                    with eng.Fori(0, NT) as j:
                        eng.wait_ge(s_row, j + 1)
                        eng.dma_start(by_tile(table1)[:, ds(j, 1), :], nodes[:, ds(j, 1), :]).then_inc(s_st, 16)
                    eng.wait_ge(s_st, NT * 16)

                @block.gpsimd
                def _(eng):
                    eng.memset(hist_dst[:, HFULL:HCOLS], -1).then_inc(s_fill, 1)
                    eng.memset(src_i[:, EB, :], 0).then_inc(s_fill, 1)
                    eng.memset(dst_i[:, EB, :], -1).then_inc(s_fill, 1)
                    eng.memset(nodes[:, NT - 1, :], 0.0).then_inc(s_fill, 1)
                    eng.memset(zeros_b[:, :], 0.0).then_inc(s_fill, 1)
                    eng.iota(iota0b[:, :], pattern=[[1, P]], base=0, channel_multiplier=0, allow_small_or_imprecise_dtypes=True).then_inc(s_pool, 1)
                    eng.iota(iota_v[:, :], pattern=[[1, V]], base=0, channel_multiplier=0, allow_small_or_imprecise_dtypes=True).then_inc(s_pool, 1)
                    eng.iota(rowno[:, :], pattern=[[P, CB]], base=0, channel_multiplier=1, allow_small_or_imprecise_dtypes=True).then_inc(s_pool, 1)
                    eng.iota(iota1[:, :], pattern=[[1, P]], base=1, channel_multiplier=0, allow_small_or_imprecise_dtypes=True).then_inc(s_pool, 1)
                    eng.memset(ones[:, :], 1.0).then_inc(s_pool, 1)
                    eng.memset(ident[:, :], 0.0).then_inc(s_pool, 1)
                    eng.memset(tri[:, :], 1.0).then_inc(s_pool, 1)
                    eng.wait_ge(s_pool, 7)
                    eng.affine_select(out=ident[:, :], in_=ident[:, :], compare_op=ALU.not_equal, fill=1.0, base=0,
                                      pattern=[[-1, P]], channel_multiplier=1).then_inc(s_pool, 1)
                    eng.affine_select(out=tri[:, :], in_=tri[:, :], compare_op=ALU.is_gt, fill=0.0, base=0,
                                      pattern=[[1, NT]], channel_multiplier=-1).then_inc(s_pool, 1)

                @block.vector
                def _(eng):
                    link = chained(eng, s_dve)
                    eng.wait_ge(s_pool, POOL)
                    eng.wait_ge(s_hd, 32)
                    link(eng.tensor_single_scalar(lo_i[:, :], hist_dst[:, :], PH - 1, ALU.bitwise_and))
                    link(eng.tensor_single_scalar(hi_i[:, :], hist_dst[:, :], PH.bit_length() - 1, ALU.arith_shift_right))
                    link(eng.tensor_copy(lo[:, :], lo_i[:, :]))
                    link(eng.tensor_copy(hi[:, :], hi_i[:, :]))
                    with eng.Fori(0, HCOLS // HSTEP // 2) as i:
                        for par in range(2):
                            eng.wait_ge(s_hdone, i * 2 + par + 1)
                            for hot_, n, value in ((lo_hot, PH, lo), (hi_hot, 2 * NT, hi)):
                                eng.tensor_tensor(hot_[:, par, :, :], iota0b[:, 0:n].unsqueeze(1).to_broadcast([P, HSTEP, n]),
                                                  value[:, ds((i * 2 + par) * HSTEP, HSTEP)].unsqueeze(2).to_broadcast([P, HSTEP, n]), ALU.is_equal).then_inc(s_lo, 1)
                    for j in range(NT):
                        if j % XG == 0:
                            eng.wait_ge(s_x[j // XG], 32 if j == NT - XG else 16)
                        for h in range(2):
                            last = eng.bn_stats(stats[:, j, h, :], nodes[:, j, h * D // 2:(h + 1) * D // 2])
                    link(last)
                    for j in range(NT):
                        last = eng.bn_aggr(mv[:, j, :], stats[:, j, :, :])
                    link(last)
                    eng.tensor_scalar(std[:, :], mv[:, :, 1], EPS, None, ALU.add).then_inc(s_var, 1)
                    eng.wait_ge(s_hdone, 3 + HCOLS // HSTEP)
                    link(eng.tensor_copy(counts[:, :], ps_h[:, 0:NT]))
                    eng.tensor_scalar(dinv[:, :], counts[:, :], 1.0, None, ALU.add).then_inc(s_var, 1)
                    eng.sem_inc(s_counts, 1)
                    eng.wait_ge(s_sqrt, 2)
                    link(eng.reciprocal(dinv[:, :], dinv[:, :]))
                    link(eng.reciprocal(std[:, :], std[:, :]))
                    link(eng.tensor_tensor(sc[:, :], std[:, :], dinv[:, :], ALU.mult))
                    link(eng.scalar_tensor_tensor(out=bi[:, :], in0=mv[:, :, 0], scalar=-1.0, in1=sc[:, :], op0=ALU.mult, op1=ALU.mult))
                    eng.sem_inc(s_scale, 1)
                    CNT, T0, T1, CS, CE, NV, M0, M1, LASTV, OFF, V0, V1 = range(12)

                    def col(k):
                        return c[:, k:k + 1]
                    eng.wait_ge(s_pe, 1)
                    link(eng.tensor_copy(col(CNT), ps_c[0:NT, 0:1]))
                    eng.sem_inc(s_step, 1)
                    eng.wait_ge(s_pe, 2)
                    link(eng.tensor_copy(col(T0), ps_c[0:NT, 1:2]))
                    link(eng.tensor_tensor(col(T1), col(T0), col(CNT), ALU.add))
                    link(eng.tensor_scalar(col(T1), col(T1), float(P - 1), None, ALU.add))
                    link(eng.tensor_copy(ci[:, 0:2], c[:, T0:T1 + 1]))
                    link(eng.tensor_single_scalar(ci[:, 2:4], ci[:, 0:2], P.bit_length() - 1, ALU.arith_shift_right))
                    link(eng.tensor_copy(c[:, CS:CE + 1], ci[:, 2:4]))
                    link(eng.tensor_tensor(col(NV), col(CE), col(CS), ALU.subtract))
                    link(eng.tensor_scalar(ci[:, 0:1], col(NV), 1.0, 1.0, ALU.max, ALU.add))
                    link(eng.tensor_single_scalar(ci[:, 1:2], ci[:, 0:1], 1, ALU.arith_shift_right))
                    link(eng.tensor_copy(col(NV), ci[:, 1:2]))
                    eng.sem_inc(s_step, 1)
                    eng.wait_ge(s_pe, 3)
                    link(eng.tensor_copy(col(M0), ps_c[0:NT, 2:3]))
                    link(eng.tensor_tensor(col(M1), col(M0), col(NV), ALU.add))
                    link(eng.tensor_scalar(col(LASTV), rowno[0:NT, 0:1], float(NT - 1), float(V // 2), ALU.is_equal, ALU.mult))
                    link(eng.tensor_tensor(col(M1), col(M1), col(LASTV), ALU.max))
                    link(eng.tensor_scalar(c[:, V0:V1 + 1], c[:, M0:M1 + 1], 2.0, None, ALU.mult))
                    link(eng.tensor_tensor(col(OFF), col(CS), col(V0), ALU.subtract))
                    link(eng.tensor_scalar(at_least[:, :], iota_v[0:NT, :], col(V0), None, ALU.is_ge))
                    link(eng.scalar_tensor_tensor(out=sel[:, :], in0=iota_v[0:NT, :], scalar=col(V1), in1=at_least[:, :],
                                                  op0=ALU.is_lt, op1=ALU.mult))
                    link(eng.tensor_scalar(off_b[:, :], ones[0:NT, :], col(OFF), None, ALU.mult))
                    link(eng.tensor_scalar(tile_b[:, :], ones[0:NT, :], rowno[0:NT, 0:1], float(P), ALU.mult, ALU.mult))
                    eng.sem_inc(s_step, 1)
                    eng.wait_ge(s_pe, 4)
                    link(eng.tensor_tensor(chunk_v[:, :], ps_off[:, 0:V], iota_v[:, :], ALU.add))
                    for b in range(CB):
                        link(eng.tensor_scalar(chunk_hot[:, b, :], chunk_v[:, :], rowno[:, b:b + 1], None, ALU.is_equal))
                    eng.wait_ge(s_ed, 6 * 16)
                    link(eng.tensor_scalar(dst_f[:, :, :], dst_i[:, :, :], 1.0, None, ALU.add))
                    link(eng.tensor_copy(src_f[:, :, :], src_i[:, :, :]))
                    eng.sem_inc(s_step, 1)
                    eng.wait_ge(s_pe, 5)
                    link(eng.tensor_copy(pair0[:, 0:NT], ps_c[0:1, 4:4 + NT]))
                    link(eng.memset(pair0[:, NT:NT + 1], V // 2))
                    link(eng.tensor_copy(d1v[:, :], ps_d[:, 0:V]))
                    link(eng.tensor_tensor(dl1[:, 0:V], d1v[:, :], ps_tile[:, 0:V], ALU.subtract))
                    link(eng.tensor_copy(idx[:, :], ps_s[:, 0:V]))
                    link(eng.tensor_scalar(tile_of[:, :], ps_tile[0:1, 0:V], 1.0 / P, None, ALU.mult))

                @block.tensor
                def _(eng):
                    eng.wait_ge(s_pool, POOL)
                    eng.wait_ge(s_fill, FILL)
                    eng.sem_inc(s_hdone, 1)
                    eng.matmul(ps_h[:, 0:NT], zeros_b[:, :], zeros_b[:, 0:NT], start=True, stop=True).then_inc(s_hdone, 1)
                    with eng.Fori(0, HCOLS // HSTEP // 2) as i:
                        for par in range(2):
                            eng.wait_ge(s_lo, (i * 2 + par) * 2 + 2)
                            for k in range(HSTEP):
                                for u in range(2):
                                    last = eng.matmul(ps_h[u * PH:(u + 1) * PH, 0:NT], lo_hot[:, par, k, :], hi_hot[:, par, k, :].rearrange("p (t u) -> p t u", u=2)[:, :, u],
                                                      start=False, stop=True, skip_group_check=True)
                            last.then_inc(s_hdone, 1)
                    eng.matmul(ps_h[:, 0:NT], zeros_b[:, :], zeros_b[:, 0:NT], start=False, stop=True,
                               skip_group_check=True).then_inc(s_hdone, 1)
                    eng.wait_ge(s_counts, 1)
                    eng.matmul(ps_c[0:NT, 0:1], counts[:, :], ones[:, 0:1], start=True, stop=True).then_inc(s_pe, 1)
                    eng.wait_ge(s_step, 1)
                    eng.matmul(ps_c[0:NT, 1:2], tri[:, :], c[:, 0:1], start=True, stop=True).then_inc(s_pe, 1)
                    eng.wait_ge(s_step, 2)
                    eng.matmul(ps_c[0:NT, 2:3], tri[:, :], c[:, 5:6], start=True, stop=True).then_inc(s_pe, 1)
                    eng.wait_ge(s_step, 3)
                    eng.transpose(ps_c[0:1, 4:4 + NT], c[:, 6:7], ident[0:NT, 0:NT])
                    eng.matmul(ps_off[:, 0:V], off_b[:, :], sel[:, :], start=True, stop=True)
                    eng.matmul(ps_tile[:, 0:V], tile_b[:, :], sel[:, :], start=True, stop=True).then_inc(s_pe, 1)
                    eng.wait_ge(s_step, 4)
                    for t, ps in ((dst_f, ps_d), (src_f, ps_s)):
                        for b in range(CB):
                            last = eng.matmul(ps[:, 0:V], t[:, b, :], chunk_hot[:, b, :], start=(b == 0), stop=(b == CB - 1))
                    last.then_inc(s_pe, 1)

                @block.scalar
                def _(eng):
                    eng.wait_ge(s_var, 1)
                    eng.activation(std[:, :], std[:, :], ACT.Sqrt).then_inc(s_sqrt, 1)
                    eng.wait_ge(s_var, 2)
                    eng.activation(dinv[:, :], dinv[:, :], ACT.Sqrt).then_inc(s_sqrt, 1)
                    eng.wait_ge(s_scale, 1)
                    with eng.Fori(0, NT) as j:
                        eng.activation(nodes[:, ds(j, 1), :], nodes[:, ds(j, 1), :], ACT.Relu, bias=bi[:, ds(j, 1)],
                                       scale=sc[:, ds(j, 1)]).then_inc(s_row, 1)

        def gather_rows(eng, table, freed, idx_ready, asked, dest):
            def half(n, h, count):
                eng.wait_ge(freed[0], n * (RING // 2) + 1)
                eng.tensor_copy(idx_slot[h][:, 0:count], idx[:, ds(n * RING, count)]).then_inc(idx_ready, 1)
                eng.wait_ge(idx_ready, n + 1)
                for k in range(count):
                    if k % 2 == 0:
                        for f in freed:
                            eng.wait_ge(f, n * (RING // 2) + k // 2 + 1)
                        eng.sem_inc(asked, 1)
                    eng.indirect_dma_start(out=dest(k), out_offset=None, in_=table,
                                           in_offset=bass.IndirectOffsetOnAxis(ap=idx_slot[h][:, k:k + 1], axis=0)).then_inc(landed[k], 16)
            with eng.Fori(0, V // RING // 2) as i:
                for h in range(2):
                    half(i * 2 + h, h, RING)
            for n in range(V // RING // 2 * 2, -(-V // RING)):
                half(n, n % 2, min(RING, V - n * RING))

        def slot_uses(k):
            return -(-(V - k) // RING)

        def relay_landed(eng, earlier, rows_landed):
            with eng.Fori(0, V // RING) as i:
                for k in range(RING):
                    eng.wait_ge(landed[k], i * 16 + (slot_uses(k) * earlier + 1) * 16)
                    eng.sem_inc(rows_landed, 1)
            for k in range(V % RING):
                eng.wait_ge(landed[k], slot_uses(k) * (earlier + 1) * 16)
                eng.sem_inc(rows_landed, 1)
            eng.sem_inc(rows_landed, 2 * AHEAD)

        def visits_of(eng, j, body):
            first = eng.value_load(pair0[0:1, ds(j, 1)], min_val=0, max_val=V // 2 - 1)
            end = eng.value_load(pair0[0:1, ds(j + 1, 1)], min_val=1, max_val=V // 2)
            with eng.Fori(first, end) as g:
                body(g)

        def one_hots(eng, g, hot):
            return eng.tensor_tensor(hot[:, ds((g * 2) % (2 * HOTS), 2), :], iota1[:, :].unsqueeze(1).to_broadcast([P, 2, P]),
                                     dl1[:, ds(g * 2, 2)].unsqueeze(2).to_broadcast([P, 2, P]), ALU.is_equal)

        def by_pair(eng, g, body):
            which = eng.snap(g % HOTS)

            def choose(lo_, hi_):
                if hi_ - lo_ == 1:
                    body(lo_)
                    return
                mid = (lo_ + hi_) // 2
                with eng.If(which < mid):
                    choose(lo_, mid)
                with eng.Else():
                    choose(mid, hi_)
            choose(0, HOTS)

        def staged(eng, lag, step):
            assert (NT - lag) % 2 == 0
            for j in range(lag):
                step(j, j % 2)
            with eng.Fori(0, (NT - lag) // 2) as i:
                for b in range(2):
                    step(i * 2 + lag + b, (lag + b) % 2)
            for j in range(NT, NT + lag):
                step(j, j % 2)

        def has(j, back):
            return not isinstance(j, int) or 0 <= j - back < NT

        def convolution(tag, table, wt, bias, first):
            with ExitStack() as st:
                ring = sb(st, f"ring{tag}", [P, RING, D])
                hot = sb(st, f"hot{tag}", [P, 2 * HOTS, P], F32R)
                parts = sb(st, f"parts{tag}", [P, 2, 2 * HOTS, D], F32R)
                w = sb(st, f"w{tag}", [P, KB, D])
                bias_b = sb(st, f"bias_b{tag}", [P, D])
                summed = sb(st, f"summed{tag}", [P, D])
                sum_t = sb(st, f"sum_t{tag}", [P, D])
                zeros = sb(st, f"zeros{tag}", [P, P], BF16)
                ps_sum = pb(st, f"ps_sum{tag}", 2048)
                ps_t = pb(st, f"ps_t{tag}", 1024)
                ps_y = pb(st, f"ps_y{tag}", 1024)
                rows_landed = sem(st, f"rows_landed{tag}")
                visited = sem(st, f"visited{tag}")
                idx_ready = sem(st, f"idx_ready{tag}")
                asked = sem(st, f"asked{tag}")
                high = sem(st, f"high{tag}")
                low = sem(st, f"low{tag}")
                hot_ready = sem(st, f"hot_ready{tag}")
                s_w = sem(st, f"s_w{tag}")
                s_zero = sem(st, f"s_zero{tag}")
                s_summed = sem(st, f"s_summed{tag}")
                s_t = sem(st, f"s_t{tag}")
                s_tc = sem(st, f"s_tc{tag}")
                s_y = sem(st, f"s_y{tag}")
                s_b = sem(st, f"s_b{tag}")
                s_o = sem(st, f"s_o{tag}")
                s_st = sem(st, f"s_st{tag}")
                s_xl = sem(st, f"s_xl{tag}")

                def sums(par, c0, n):
                    return ps_sum[:, par * 1024 + c0:par * 1024 + c0 + n]

                def pair_of(t, g, slots):
                    return t[:, ds((g * 2) % slots, 2), :]
                with nc.Block() as block:

                    @block.gpsimd
                    def _(eng):
                        gather_rows(eng, table, [low], idx_ready, asked, lambda k: ring[:, k, :])

                    @block.sync
                    def _(eng):
                        eng.dma_start(w[:, :, :], wt.rearrange("(k p) n -> p k n", p=P)).then_inc(s_w, 16)
                        eng.dma_start(bias_b[:, :], bias.rearrange("(a n) -> a n", a=1).to_broadcast([P, D])).then_inc(s_w, 16)
                        relay_landed(eng, 0 if first else 1, rows_landed)

                    @block.scalar
                    def _(eng):
                        if first:
                            eng.sem_inc(s_o, 1)

                        def round_high(g):
                            eng.wait_ge(rows_landed, g * 2 + 2)
                            eng.wait_ge(visited, g + 1)
                            eng.activation(pair_of(parts[:, 0, :, :], g, 2 * HOTS), pair_of(ring, g, RING), ACT.Copy).then_inc(high, 1)

                        def step(j, par):
                            if not first and has(j, 3):
                                jj = j - 3
                                if not isinstance(j, int) or jj >= 1:
                                    eng.wait_ge(s_xl, jj * 16)
                                eng.wait_ge(s_summed, jj + 1)
                                if isinstance(j, int) and jj == NT - 1:
                                    eng.dma_start(nodes[0:LAST, jj, :], x[jj * P:N, :]).then_inc(s_xl, 16)
                                else:
                                    whole = x[0:(NT - 1) * P, :].rearrange("(t p) d -> p t d", p=P)
                                    eng.dma_start(nodes[:, ds(jj, 1), :], whole[:, ds(jj, 1), :]).then_inc(s_xl, 16)
                            if has(j, 0):
                                visits_of(eng, j, lambda g: round_high(g + AHEAD))
                            if has(j, 2):
                                eng.wait_ge(s_y, j - 2 + 1)
                                eng.wait_ge(s_t, j - 2 + 2)
                                eng.activation(sum_t[:, :], ps_t[:, 0:D], ACT.Copy).then_inc(s_tc, 1)
                            if first and has(j, 3):
                                jj = j - 3
                                eng.wait_ge(s_b, jj + 2)
                                eng.activation(nodes[:, ds(jj, 1), :].rearrange("p a d -> p (a d)"), nodes[:, ds(jj, 1), :].rearrange("p a d -> p (a d)"), ACT.Relu, scale=dinv[:, ds(jj, 1)]).then_inc(s_o, 1)
                                eng.wait_ge(s_o, jj + 2)
                                eng.dma_start(by_tile(table2)[:, ds(jj, 1), :], nodes[:, ds(jj, 1), :]).then_inc(s_st, 16)
                        for g in range(AHEAD):
                            round_high(g)
                        staged(eng, 5, step)
                        if first:
                            eng.wait_ge(s_st, NT * 16)

                    @block.tensor
                    def _(eng):
                        eng.sem_inc(visited, HOTS)
                        eng.sem_inc(s_t, 1)
                        eng.sem_inc(s_y, 1)
                        eng.wait_ge(s_w, 32)
                        eng.wait_ge(s_zero, 1)

                        def step(j, par):
                            if has(j, 0):
                                if not isinstance(j, int) or j >= 2:
                                    eng.wait_ge(s_summed, j - 1)
                                for c0, n in HALVES:
                                    eng.matmul(sums(par, c0, n), zeros[:, :], zeros[:, 0:1].to_broadcast([P, n]), start=True, stop=True)

                                def visit(g):
                                    eng.wait_ge(low, g + RING // 2 + 1)
                                    eng.wait_ge(hot_ready, g + 1)

                                    def products(at):
                                        for k in range(at * 2, at * 2 + 2):
                                            for c0, n in HALVES:
                                                for t in range(2):
                                                    last = eng.matmul(sums(par, c0, n), hot[:, k, :], parts[:, t, k, c0:c0 + n],
                                                                      start=False, stop=True, skip_group_check=True)
                                        last.then_inc(visited, 1)
                                    by_pair(eng, g, products)
                                visits_of(eng, j, visit)
                            if has(j, 2):
                                jj = j - 2
                                eng.wait_ge(s_tc, jj + 1)
                                eng.wait_ge(s_b, jj + 1)
                                for c0, n in HALVES:
                                    for k in range(KB):
                                        last = eng.matmul(ps_y[:, c0:c0 + n], sum_t[:, k * P:(k + 1) * P], w[:, k, c0:c0 + n],
                                                          start=(k == 0), stop=(k == KB - 1))
                                last.then_inc(s_y, 1)
                            if has(j, 1):
                                eng.wait_ge(s_summed, j)
                                for k in range(KB):
                                    last = eng.transpose(ps_t[:, k * P:(k + 1) * P], summed[:, k * P:(k + 1) * P], ident[:, :])
                                last.then_inc(s_t, 1)
                        staged(eng, 3, step)

                    @block.vector
                    def _(eng):
                        eng.memset(zeros[:, :], 0.0).then_inc(s_zero, 1)
                        eng.sem_inc(low, RING // 2)
                        eng.sem_inc(s_b, 1)
                        if not first:
                            eng.sem_inc(s_o, 1)
                        eng.wait_ge(s_w, 32)

                        def low_and_hot(g):
                            eng.wait_ge(high, g + 1)
                            eng.tensor_tensor(pair_of(parts[:, 1, :, :], g, 2 * HOTS), pair_of(ring, g, RING),
                                              pair_of(parts[:, 0, :, :], g, 2 * HOTS).bitcast(F32), ALU.subtract).then_inc(low, 1)
                            one_hots(eng, g, hot).then_inc(hot_ready, 1)

                        def step(j, par):
                            if has(j, 0):
                                visits_of(eng, j, low_and_hot)
                            if has(j, 1):
                                end = eng.value_load(pair0[0:1, ds(j, 1)], min_val=1, max_val=V // 2)
                                eng.wait_ge(visited, end + HOTS)
                                eng.wait_ge(s_t, j)
                                eng.tensor_tensor(summed[:, :], sums(1 - par, 0, D), nodes[:, ds(j - 1, 1), :].rearrange("p a d -> p (a d)"), ALU.add).then_inc(s_summed, 1)
                            if has(j, 3):
                                jj = j - 3
                                eng.wait_ge(s_y, jj + 2)
                                node = nodes[:, ds(jj, 1), :].rearrange("p a d -> p (a d)")
                                if first:
                                    eng.scalar_tensor_tensor(out=node, in0=ps_y[:, 0:D], scalar=dinv[:, ds(jj, 1)], in1=bias_b[:, :], op0=ALU.mult, op1=ALU.add).then_inc(s_b, 1)
                                else:
                                    eng.wait_ge(s_xl, jj * 16 + 16)
                                    eng.scalar_tensor_tensor(out=node, in0=ps_y[:, 0:D], scalar=dinv[:, ds(jj, 1)], in1=node, op0=ALU.mult, op1=ALU.add).then_inc(s_b, 1)
                                    eng.wait_ge(s_b, jj + 2)
                                    eng.tensor_tensor(node, node, bias_b[:, :], ALU.add).then_inc(s_o, 1)
                                    eng.wait_ge(s_o, jj + 2)
                                    for h in range(2):
                                        eng.bn_stats(stats2[:, ds(jj, 1), h, :].rearrange("p a s -> p (a s)"),
                                                     nodes[:, ds(jj, 1), h * D // 2:(h + 1) * D // 2].rearrange("p a d -> p (a d)"))
                        staged(eng, 3, step)

        stats2 = sb(ctx, "stats2", [P, NT, 2, 6])
        convolution("a", table1, w1t, b1, True)
        convolution("b", table2, w2t, b2, False)

        a1 = sb(ctx, "a1", [P, NT, H])
        a2 = sb(ctx, "a2", [P, NT, H])
        with ExitStack() as st:
            mv = sb(st, "mv2", [P, NT, 2])
            std = sb(st, "std2", [P, NT])
            bi = sb(st, "bi2", [P, NT])
            wfc2 = sb(st, "wfc2", [DH, 2, DH])
            attn_t = sb(st, "attn_t", [DH, 2 * H])
            maps = sb(st, "maps", [P, KB, 2 * P + 4])
            blk = sb(st, "blk", [P, 4, DH])
            h2 = sb(st, "h2", [P, 2, D])
            h2_t = sb(st, "h2_t", [P, 2, D])
            ft = sb(st, "ft", [P, 2, KB, P])
            res = sb(st, "res", [P, 2, KB, P])
            ps_t = pb(st, "ps_t2", 1024)
            ps_f = [pb(st, f"ps_f{k}", 1536) for k in range(2)]
            s_w = sem(st, "s_w2")
            s_z = sem(st, "s_z2")
            s_var = sem(st, "s_var2")
            s_sqrt = sem(st, "s_sqrt2")
            s_dve = sem(st, "s_dve2")
            s_blk = sem(st, "s_blk2")
            s_fold = sem(st, "s_fold2")
            s_ready = sem(st, "s_ready2")
            s_h2 = sem(st, "s_h2")
            s_t = sem(st, "s_t2")
            s_tc = sem(st, "s_tc2")
            s_f = sem(st, "s_f2")
            s_fc = sem(st, "s_fc2")
            s_r = sem(st, "s_r2")
            s_fst = [sem(st, f"s_fst2{k}") for k in range(2)]
            s_rst = [sem(st, f"s_rst2{k}") for k in range(2)]
            HK = KB // 2

            def products_of(half):
                return ps_f[half][:, :].rearrange("p (k c) -> p k c", c=512)
            with nc.Block() as block:

                @block.sync
                def _(eng):
                    eng.dma_start(wfc2[:, 0, :], wfc).then_inc(s_w, 16)
                    eng.dma_start(wfc2[:, 1, :], wfc).then_inc(s_w, 16)
                    eng.dma_start(attn_t[:, 0:H], attn_lt).then_inc(s_w, 16)
                    eng.dma_start(attn_t[:, H:2 * H], attn_rt).then_inc(s_w, 16)
                    eng.wait_ge(s_z, 1)
                    for q, w in ((0, wfct), (2, wrest)):
                        eng.dma_start(blk[0:DH, q, :], w).then_inc(s_blk, 16)
                        eng.dma_start(blk[DH:P, q + 1, :], w).then_inc(s_blk, 16)
                    with eng.Fori(0, NT // 2) as i:
                        for par in range(2):
                            eng.wait_ge(s_r, (i * 2 + par) * 2 + 4)
                            eng.dma_start(by_tile(res_table)[:, ds(i * 2 + par, 1), :], res[:, par:par + 1, :, :].rearrange("p a k c -> p a (k c)")).then_inc(s_rst[par], 16)
                            eng.dma_start(by_tile(a1_table)[:, ds(i * 2 + par, 1), :], a1[:, ds(i * 2 + par, 1), :]).then_inc(s_rst[par], 16)
                    eng.wait_ge(s_r, 2 * NT + 2)
                    eng.dma_start(by_tile(res_table)[:, NT - 1:NT, :], res[:, 0:1, :, :].rearrange("p a k c -> p a (k c)")).then_inc(s_rst[0], 16)
                    eng.dma_start(by_tile(a1_table)[:, NT - 1:NT, :], a1[:, NT - 1:NT, :]).then_inc(s_rst[0], 16)
                    eng.wait_ge(s_rst[0], 32 * (NT // 2 + 1))
                    eng.wait_ge(s_rst[1], 32 * (NT // 2))

                @block.vector
                def _(eng):
                    link = chained(eng, s_dve)
                    eng.memset(maps[:, :, 2 * P:2 * P + 4], 0.0)
                    eng.memset(blk[:, :, :], 0.0).then_inc(s_z, 1)
                    eng.wait_ge(s_z, 1)
                    for j in range(NT):
                        last = eng.bn_aggr(mv[:, j, :], stats2[:, j, :, :])
                    link(last)
                    eng.tensor_scalar(std[:, :], mv[:, :, 1], EPS, None, ALU.add).then_inc(s_var, 1)
                    eng.wait_ge(s_fold, 1)
                    for half, which in ((0, 0), (1, 1)):
                        rows = slice(half * DH, half * DH + DH)
                        for side in range(2):
                            v = ps_f[0][rows, side * H:(side + 1) * H].rearrange("p (k t) -> p k t", t=2)
                            last = eng.tensor_copy(maps[rows, :, 2 * P + 2 * side + which], v[:, :, which])
                    link(last)
                    eng.wait_ge(s_blk, 64)
                    link(eng.tensor_copy(maps[:, :, 0:2 * P], blk[:, :, :].rearrange("p a c -> p (a c)").unsqueeze(1).to_broadcast([P, KB, 2 * P])))
                    eng.wait_ge(s_sqrt, 1)
                    link(eng.reciprocal(std[:, :], std[:, :]))
                    link(eng.scalar_tensor_tensor(out=bi[:, :], in0=mv[:, :, 0], scalar=-1.0, in1=std[:, :], op0=ALU.mult, op1=ALU.mult))
                    eng.sem_inc(s_ready, 1)

                    def transposed(j, par):
                        eng.wait_ge(s_t, j + 1)
                        eng.tensor_copy(h2_t[:, par, :], ps_t[:, 0:D]).then_inc(s_tc, 1)

                    def rest(j, par, half, stored):
                        eng.wait_ge(s_fc, j * 2 + half + 1)
                        if stored is not None:
                            eng.wait_ge(s_rst[par], stored)
                        eng.tensor_copy(res[:, par, half * HK:(half + 1) * HK, :], products_of(half)[:, :, P:2 * P])
                        terms = products_of(half)[:, :, 2 * P:2 * P + 4]
                        heads = slice(half * 2 * HK, (half + 1) * 2 * HK)
                        for a, c0 in ((a1, 0), (a2, 2)):
                            last = eng.tensor_copy(a[:, ds(j, 1), heads].rearrange("p a (k t) -> p (a k) t", t=2), terms[:, :, c0:c0 + 2])
                        last.then_inc(s_r, 1)

                    def step(j, par, stored, more=True):
                        rest(j, par, 0, stored)
                        if more:
                            transposed(j + 1, 1 - par)
                        rest(j, par, 1, None)
                    eng.sem_inc(s_r, 2)
                    transposed(0, 0)
                    step(0, 0, None)
                    step(1, 1, None)
                    with eng.Fori(1, NT // 2) as i:
                        for par in range(2):
                            step(i * 2 + par, par, i * 32)
                    step(NT - 1, 0, 32 * (NT // 2), False)

                @block.scalar
                def _(eng):
                    eng.wait_ge(s_var, 1)
                    eng.activation(std[:, :], std[:, :], ACT.Sqrt).then_inc(s_sqrt, 1)
                    eng.wait_ge(s_ready, 1)

                    def norm(j, par):
                        eng.activation(h2[:, par, :], nodes[:, ds(j, 1), :].rearrange("p a d -> p (a d)"), ACT.Relu, bias=bi[:, ds(j, 1)], scale=std[:, ds(j, 1)]).then_inc(s_h2, 1)

                    def features(j, par, stored):
                        for half in range(2):
                            eng.wait_ge(s_f, j * 2 + half + 1)
                            if stored is not None and half == 0:
                                eng.wait_ge(s_fst[par], stored)
                            eng.activation(ft[:, par, half * HK:(half + 1) * HK, :], products_of(half)[:, :, 0:P], ACT.Copy).then_inc(s_fc, 1)
                        eng.wait_ge(s_fc, j * 2 + 2)
                        eng.dma_start(by_tile(table3)[:, ds(j, 1), :], ft[:, par:par + 1, :, :].rearrange("p a k c -> p a (k c)")).then_inc(s_fst[par], 16)

                    def step(j, par, stored, more=True):
                        if more:
                            eng.wait_ge(s_t, j + 1)
                            norm(j + 2, par)
                        features(j, par, stored)
                    norm(0, 0)
                    norm(1, 1)
                    step(0, 0, None)
                    step(1, 1, None)
                    with eng.Fori(1, NT // 2 - 1) as i:
                        for par in range(2):
                            step(i * 2 + par, par, i * 16)
                    for j in range(NT - 3, NT):
                        step(j, j % 2, 16 * (j // 2), j + 2 < NT)
                    eng.wait_ge(s_fst[0], 16 * (NT // 2 + 1))
                    eng.wait_ge(s_fst[1], 16 * (NT // 2))

                @block.tensor
                def _(eng):
                    eng.wait_ge(s_w, 64)
                    eng.matmul(ps_f[0][:, 0:2 * H], wfc2[:, :, :].rearrange("p a d -> p (a d)"), attn_t[:, :], start=True, stop=True).then_inc(s_fold, 1)
                    eng.wait_ge(s_ready, 1)

                    def transposes(j, par):
                        eng.wait_ge(s_h2, j + 1)
                        for k in range(KB):
                            last = eng.transpose(ps_t[:, k * P:(k + 1) * P], h2[:, par, k * P:(k + 1) * P], ident[:, :])
                        last.then_inc(s_t, 1)

                    def products(j, par, half):
                        eng.wait_ge(s_r, j * 2 + half + 1)
                        for k in range(HK):
                            kk = half * HK + k
                            last = eng.matmul(ps_f[half][:, k * 512:k * 512 + 2 * P + 4], h2_t[:, par, kk * P:(kk + 1) * P], maps[:, kk, :], start=True, stop=True)
                        last.then_inc(s_f, 1)

                    def step(j, par, more=True):
                        eng.wait_ge(s_tc, j + 1)
                        products(j, par, 0)
                        if more:
                            transposes(j + 1, 1 - par)
                        products(j, par, 1)
                    transposes(0, 0)
                    with eng.Fori(0, NT // 2) as i:
                        for par in range(2):
                            step(i * 2 + par, par)
                    step(NT - 1, 0, False)

        weights = sb(ctx, "weights", [P, V + 2 * AHEAD, H])
        with ExitStack() as st:
            a2e = sb(st, "a2e", [P, V, H])
            cont = sb(st, "cont", [SPT, SL], BF16)
            ends = sb(st, "ends", [SPT, 3])
            perm = sb(st, "perm", [P, SW, SG, H])

            with ExitStack() as st1:
                ROWS = GROUP - BYPE
                HOTN = GROUP + BYPE
                STEPS = -(-HOTN // HB)
                idx_group = sb(st1, "idx_group", [P, 4, ROWS], I32)
                a1_slot = sb(st1, "a1_slot", [P, 4, ROWS, H])
                key = sb(st1, "key", [P, V])
                keys = sb(st1, "keys", [SPT, SL])
                half_i = sb(st1, "half_i", [P, V], I32)
                lo1 = key
                hi1 = sb(st1, "hi1", [P, V])
                a1_parts = sb(st1, "a1_parts", [P, 2, NT * H], F32R)
                a2_pair = sb(st1, "a2_pair", [P, 2, GROUP // 2, H])
                hi_hot = sb(st1, "hi_hot_s", [P, BYPE, NT])
                hots = perm[:, :, :, :].rearrange("p w g h -> p (w g h)")[:, 0:2 * HOTN * P].rearrange("p (a v c) -> p a v c", a=2, c=P)
                picked = perm[:, :, :, :].rearrange("p w g h -> p (w g h)")[:, 2 * HOTN * P:2 * HOTN * P + BYPE * NT * H].rearrange("p (v c) -> p v c", v=BYPE)
                hots_t = sb(st1, "hots_t", [P, 2, HOTN * P], F32R)
                ps_ht = [pb(st1, f"ps_ht{k}") for k in range(2)]
                ps_e = [pb(st1, f"ps_e{k}") for k in range(2)]
                ps_s = pb(st1, "ps_s2", 2048)
                small_landed = [sem(st1, f"small_landed{k}") for k in range(4)]
                s_used = sem(st1, "s_used")
                idx_ready = sem(st1, "idx_ready_s")
                asked = sem(st1, "asked_s")
                s_dve = sem(st1, "s_dve_s")
                s_perm = sem(st1, "s_perm_k")
                s_t = sem(st1, "s_t_k")
                s_c = sem(st1, "s_c_k")
                s_split = sem(st1, "s_split")
                s_hot = sem(st1, "s_hots")
                s_tb = sem(st1, "s_tb")
                s_htc = sem(st1, "s_htc")
                s_e = sem(st1, "s_e")
                s_ec = sem(st1, "s_ec")
                s_a2 = sem(st1, "s_a2")
                s_s = sem(st1, "s_s")
                s_m = sem(st1, "s_m")
                groups = V // GROUP
                key_bank = [ps_s[:, b * 512:(b + 1) * 512] for b in range(4)]
                with nc.Block() as block:

                    @block.gpsimd
                    def _(eng):
                        with eng.Fori(0, groups // 4) as i:
                            for q in range(4):
                                eng.wait_ge(s_used, i * 4 + q + 1)
                                eng.tensor_copy(idx_group[:, q, :], idx[:, ds((i * 4 + q) * GROUP, ROWS)]).then_inc(idx_ready, 1)
                                eng.wait_ge(idx_ready, i * 4 + q + 1)
                                eng.sem_inc(asked, 1)
                                for k in range(ROWS):
                                    eng.indirect_dma_start(out=a1_slot[:, q, k, :], out_offset=None, in_=a1_table,
                                                           in_offset=bass.IndirectOffsetOnAxis(ap=idx_group[:, q, k:k + 1], axis=0)).then_inc(small_landed[q], 16)

                    @block.vector
                    def _(eng):
                        link = chained(eng, s_dve)
                        link(eng.tensor_scalar(key[:, :], dl1[:, 0:V], 1.0, None, ALU.is_ge))
                        link(eng.scalar_tensor_tensor(out=key[:, :], in0=dl1[:, 0:V], scalar=float(P), in1=key[:, :], op0=ALU.is_le, op1=ALU.mult))
                        link(eng.tensor_tensor(key[:, :], key[:, :], d1v[:, :], ALU.mult))
                        eng.tensor_copy(perm[:, :, :, :], key[:, :].rearrange("p (g w) -> p w g", w=SW).unsqueeze(3).to_broadcast([P, SW, SG, H])).then_inc(s_perm, 1)
                        link(eng.tensor_single_scalar(half_i[:, :], idx[:, :], P - 1, ALU.bitwise_and))
                        eng.wait_ge(s_perm, 1)
                        link(eng.tensor_scalar(lo1[:, :], half_i[:, :], 1.0, None, ALU.add))
                        link(eng.tensor_single_scalar(half_i[:, :], idx[:, :], P.bit_length() - 1, ALU.arith_shift_right))
                        link(eng.tensor_scalar(hi1[:, :], half_i[:, :], 1.0, None, ALU.add))
                        eng.wait_ge(s_split, 1)
                        eng.tensor_tensor(a1_parts[:, 1, :], a1[:, :, :].rearrange("p t h -> p (t h)"), a1_parts[:, 0, :].bitcast(F32), ALU.subtract).then_inc(s_split, 1)
                        eng.wait_ge(s_c, SW // 4)
                        link(eng.tensor_tensor(cont[:, 1:SL], keys[:, 1:SL], keys[:, 0:SL - 1], ALU.is_equal))
                        link(eng.tensor_scalar(cont[:, 1:SL], cont[:, 1:SL], -1.0, BIG, ALU.add, ALU.mult))
                        link(eng.memset(cont[:, 0:1], -BIG))
                        link(eng.tensor_copy(ends[:, 0:1], keys[:, 0:1]))
                        link(eng.tensor_copy(ends[:, 1:2], keys[:, SL - 1:SL]))

                        def one_hots_of(g, par):
                            eng.wait_ge(s_tb, g * STEPS + 1)
                            for first, count, value, v0 in ((0, GROUP, dl1, 0), (GROUP, BYPE, lo1, ROWS)):
                                eng.tensor_tensor(hots[:, par, first:first + count, :], iota1[:, :].unsqueeze(1).to_broadcast([P, count, P]),
                                                  value[:, ds(g * GROUP + v0, count)].unsqueeze(2).to_broadcast([P, count, P]), ALU.is_equal).then_inc(s_hot, 1)

                        def terms(g, par):
                            eng.tensor_tensor(hi_hot[:, :, :], iota1[:, 0:NT].unsqueeze(1).to_broadcast([P, BYPE, NT]),
                                              hi1[:, ds(g * GROUP + ROWS, BYPE)].unsqueeze(2).to_broadcast([P, BYPE, NT]), ALU.is_equal).then_inc(s_ec, 1)
                            eng.wait_ge(s_e, g + 1)
                            eng.tensor_copy(a2e[:, ds(g * GROUP, GROUP), :].rearrange("p v h -> p (v h)"), ps_e[par][:, 0:GROUP * H])
                            eng.wait_ge(s_ec, g + 1)
                            eng.wait_ge(s_s, g + 1)
                            eng.tensor_tensor(picked[:, :, :].rearrange("p v (t h) -> p v t h", h=H),
                                              ps_s[:, :].rearrange("p (v c) -> p v c", v=BYPE)[:, :, 0:NT * H].rearrange("p v (t h) -> p v t h", h=H),
                                              hi_hot[:, :, :].unsqueeze(3).to_broadcast([P, BYPE, NT, H]), ALU.mult).then_inc(s_m, 1)
                            eng.wait_ge(s_m, g + 2)
                            eng.tensor_reduce(weights[:, ds(g * GROUP + ROWS, BYPE), :], picked[:, :, :].rearrange("p v (t h) -> p v h t", h=H), mybir.AxisListType.X, ALU.add)
                        eng.sem_inc(s_m, 1)
                        one_hots_of(0, 0)
                        one_hots_of(1, 1)
                        with eng.Fori(0, groups // 2 - 1) as i:
                            for par in range(2):
                                one_hots_of(i * 2 + par + 2, par)
                                terms(i * 2 + par, par)
                        terms(groups - 2, 0)
                        terms(groups - 1, 1)

                    @block.tensor
                    def _(eng):
                        eng.wait_ge(s_perm, 1)
                        for q in range(SW // 4):
                            if q >= 4:
                                eng.wait_ge(s_c, q - 3)
                            for k in range(4):
                                last = eng.transpose(key_bank[q % 4][0:SPT, k * P:(k + 1) * P], perm[:, q * 4 + k, :, :].rearrange("p g h -> p (g h)"), ident[:, :])
                            last.then_inc(s_t, 1)
                        eng.sem_inc(s_tb, STEPS + 1)
                        eng.wait_ge(s_c, SW // 4)
                        eng.wait_ge(s_split, 2)

                        def transposes(g, par):
                            for b in range(STEPS):
                                if b == 0:
                                    eng.wait_ge(s_hot, g * 2 + 2)
                                eng.wait_ge(s_htc, g * STEPS + b + 1)
                                for k in range(b * HB, min((b + 1) * HB, HOTN)):
                                    last = eng.transpose(ps_ht[b % 2][:, (k % HB) * P:(k % HB + 1) * P], hots[:, par, k, :], ident[:, :])
                                last.then_inc(s_tb, 1)

                        def products(g, par):
                            eng.wait_ge(s_a2, g + 1)
                            for k in range(GROUP):
                                last = eng.matmul(ps_e[par][:, k * H:(k + 1) * H], hots_t[:, par, k * P:(k + 1) * P].bitcast(F32), a2_pair[:, par, k // 2, :], start=True, stop=True)
                            last.then_inc(s_e, 1)
                            eng.wait_ge(s_m, g + 1)
                            for k in range(BYPE):
                                for t in range(2):
                                    last = eng.matmul(ps_s[:, k * 512:k * 512 + NT * H], hots_t[:, par, (GROUP + k) * P:(GROUP + k + 1) * P], a1_parts[:, t, :],
                                                      start=(t == 0), stop=(t == 1))
                            last.then_inc(s_s, 1)
                        transposes(0, 0)
                        with eng.Fori(0, groups // 2 - 1) as i:
                            for par in range(2):
                                transposes(i * 2 + par + 1, 1 - par)
                                products(i * 2 + par, par)
                        transposes(groups - 1, 1)
                        products(groups - 2, 0)
                        products(groups - 1, 1)

                    @block.scalar
                    def _(eng):
                        eng.sem_inc(s_used, 4)
                        eng.activation(a1_parts[:, 0, :], a1[:, :, :].rearrange("p t h -> p (t h)"), ACT.Copy).then_inc(s_split, 1)
                        for q in range(SW // 4):
                            eng.wait_ge(s_t, q + 1)
                            eng.activation(keys[:, q * 4 * P:(q + 1) * 4 * P], key_bank[q % 4][0:SPT, :], ACT.Copy).then_inc(s_c, 1)
                        eng.sem_inc(s_htc, 2)
                        with eng.Fori(0, groups // 4) as i:
                            for q in range(4):
                                g = i * 4 + q
                                for b in range(STEPS):
                                    eng.wait_ge(s_tb, g * STEPS + b + STEPS + 2)
                                    n = (min((b + 1) * HB, HOTN) - b * HB) * P
                                    eng.activation(hots_t[:, q % 2, b * HB * P:b * HB * P + n], ps_ht[b % 2][:, 0:n], ACT.Copy).then_inc(s_htc, 1)
                                for k in range(GROUP // 2):
                                    tile = eng.value_load(tile_of[0:1, ds(g * GROUP + k * 2, 1)], min_val=0, max_val=NT - 1)
                                    last = eng.activation(a2_pair[:, q % 2, k, :], a2[:, ds(tile, 1), :].rearrange("p a h -> p (a h)"), ACT.Copy)
                                last.then_inc(s_a2, 1)
                                eng.wait_ge(small_landed[q], (i + 1) * 16 * ROWS)
                                eng.activation(weights[:, ds(g * GROUP, ROWS), :], a1_slot[:, q, :, :], ACT.Copy).then_inc(s_used, 1)

            with ExitStack() as st1:
                run = sb(st1, "run", [SPT, SL])
                row = sb(st1, "row", [1, 14, SPT])
                carry = sb(st1, "carry", [SPT, 2])
                one1 = sb(st1, "one1", [1, 1])
                ps_a = [pb(st1, f"ps_a{k}") for k in range(4)]
                ps_r = pb(st1, "ps_r")
                ps_m = pb(st1, "ps_m")
                s_dve = sem(st1, "s_dve_m")
                s_perm = sem(st1, "s_perm_m")
                s_t = sem(st1, "s_t_m")
                s_c = sem(st1, "s_c_m")
                s_scan = sem(st1, "s_scan")
                s_row = sem(st1, "s_row_m")
                s_mt = sem(st1, "s_mt")
                s_mc = sem(st1, "s_mc")
                s_d = sem(st1, "s_d_m")
                R_FIRST, R_LAST, R_MAX, R_LINK, R_WHOLE, R_GO, R_ACC, R_IN, R_T = range(9)

                def columns(t, q):
                    return t[:, 0:V, :].rearrange("p (g w) h -> p w g h", w=SW)[:, q * 4:q * 4 + 4, :, :]

                def by_head(r):
                    return row[:, r, :].rearrange("a (h g) -> a h g", g=SG)
                with nc.Block() as block:

                    @block.vector
                    def _(eng):
                        link = chained(eng, s_dve)
                        link(eng.memset(one1[:, :], 1.0))
                        link(eng.memset(weights[:, V:V + 2 * AHEAD, :], 0.0))
                        eng.tensor_copy(perm[:, :, :, :], weights[:, 0:V, :].rearrange("p (g w) h -> p w g h", w=SW)).then_inc(s_perm, 1)
                        w_, e_ = (t[:, 0:V, :].rearrange("p v h -> p (v h)") for t in (weights, a2e))
                        eng.wait_ge(s_perm, 1)
                        link(eng.tensor_tensor(w_, w_, e_, ALU.add))
                        link(eng.scalar_tensor_tensor(out=w_, in0=w_, scalar=SLOPE, in1=w_, op0=ALU.mult, op1=ALU.max))
                        eng.wait_ge(s_c, SW // 4)
                        fwd, bwd = slice(None), slice(None, None, -1)

                        def carries(back):
                            lo_, hi_ = (slice(1, SG), slice(0, SG - 1))
                            cur, prev = (hi_, lo_) if back else (lo_, hi_)
                            a, b = (R_LAST, R_FIRST) if back else (R_FIRST, R_LAST)
                            link(eng.memset(row[:, R_LINK, :], -BIG))
                            link(eng.tensor_tensor(by_head(R_LINK)[:, :, cur], by_head(a)[:, :, cur], by_head(b)[:, :, prev], ALU.is_equal))
                            link(eng.tensor_scalar(by_head(R_LINK)[:, :, cur], by_head(R_LINK)[:, :, cur], -1.0, BIG, ALU.add, ALU.mult))
                            link(eng.tensor_tensor(row[:, R_WHOLE, :], row[:, R_FIRST, :], row[:, R_LAST, :], ALU.is_equal))
                            link(eng.tensor_scalar(row[:, R_WHOLE, :], row[:, R_WHOLE, :], -1.0, BIG, ALU.add, ALU.mult))
                            link(eng.tensor_tensor(row[:, R_GO, :], row[:, R_LINK, :], row[:, R_WHOLE, :], ALU.min))
                            d = bwd if back else fwd
                            link(eng.tensor_tensor_scan(row[:, R_ACC, :][:, d], row[:, R_GO, :][:, d], row[:, R_MAX, :][:, d], -BIG, ALU.add, ALU.max))
                            link(eng.memset(row[:, R_IN, :], -BIG))
                            link(eng.tensor_tensor(by_head(R_IN)[:, :, cur], by_head(R_ACC)[:, :, prev], by_head(R_LINK)[:, :, cur], ALU.add))
                            link(eng.tensor_scalar(row[:, R_IN, :], row[:, R_IN, :], -BIG, None, ALU.max))
                            link(eng.tensor_copy(row[:, R_T, :].rearrange("a (g h) -> a g h", h=H), by_head(R_IN).rearrange("a h g -> a g h")))

                        link(eng.tensor_tensor_scan(run[:, :], cont[:, :], run[:, :], -BIG, ALU.add, ALU.max))
                        link(eng.tensor_copy(ends[:, 2:3], run[:, SL - 1:SL]))
                        eng.sem_inc(s_scan, 1)
                        eng.wait_ge(s_row, 1)
                        for r in (R_FIRST, R_LAST, R_MAX):
                            link(eng.tensor_copy(by_head(r).rearrange("a h g -> a g h"), ps_r[0:1, r * P:r * P + SPT].rearrange("a (g h) -> a g h", h=H)))
                        carries(False)
                        eng.sem_inc(s_scan, 1)
                        eng.wait_ge(s_row, 2)
                        link(eng.tensor_copy(carry[:, 0:1], ps_m[0:SPT, 0:1]))
                        link(eng.memset(cont[:, 0:1], 0.0))
                        link(eng.tensor_tensor_scan(run[:, :], cont[:, :], run[:, :], carry[:, 0:1], ALU.add, ALU.max))
                        link(eng.memset(cont[:, 0:1], -BIG))
                        eb = run[:, 0:SL - 1][:, bwd]
                        cb = cont[:, 1:SL][:, bwd]
                        link(eng.tensor_tensor_scan(eb, cb, eb, run[:, SL - 1:SL], ALU.add, ALU.max))
                        link(eng.tensor_copy(ends[:, 2:3], run[:, 0:1]))
                        eng.sem_inc(s_scan, 1)
                        eng.wait_ge(s_row, 3)
                        link(eng.tensor_copy(by_head(R_MAX).rearrange("a h g -> a g h"), ps_r[0:1, R_MAX * P:R_MAX * P + SPT].rearrange("a (g h) -> a g h", h=H)))
                        carries(True)
                        eng.sem_inc(s_scan, 1)
                        eng.wait_ge(s_row, 4)
                        link(eng.tensor_copy(carry[:, 1:2], ps_m[0:SPT, 1:2]))
                        link(eng.tensor_tensor(run[:, SL - 1:SL], run[:, SL - 1:SL], carry[:, 1:2], ALU.max))
                        link(eng.tensor_tensor_scan(eb, cb, eb, run[:, SL - 1:SL], ALU.add, ALU.max))
                        eng.sem_inc(s_scan, 1)
                        for q in range(SW // 4):
                            eng.wait_ge(s_mt, q + 1)
                            m_ = perm[:, q * 4:q * 4 + 4, :, :]
                            maxima = ps_a[q % 4][:, :].rearrange("p (k c) -> p k c", c=P)[:, :, 0:SPT].rearrange("p k (g h) -> p k g h", h=H)
                            eng.tensor_tensor(m_, maxima, columns(a2e, q), ALU.add).then_inc(s_mc, 1)
                            eng.wait_ge(s_mc, q + 1)
                            link(eng.scalar_tensor_tensor(out=m_, in0=m_, scalar=SLOPE, in1=m_, op0=ALU.mult, op1=ALU.max))
                            eng.tensor_tensor(columns(weights, q), columns(weights, q), m_, ALU.subtract).then_inc(s_d, 1)

                    @block.tensor
                    def _(eng):
                        eng.wait_ge(s_perm, 1)
                        for q in range(SW // 4):
                            if q >= 4:
                                eng.wait_ge(s_c, q - 3)
                            for k in range(4):
                                last = eng.transpose(ps_a[q % 4][0:SPT, k * P:(k + 1) * P], perm[:, q * 4 + k, :, :].rearrange("p g h -> p (g h)"), ident[:, :])
                            last.then_inc(s_t, 1)
                        for back in range(2):
                            eng.wait_ge(s_scan, 2 * back + 1)
                            for r in range(3) if not back else (2,):
                                last = eng.transpose(ps_r[0:1, r * P:r * P + SPT], ends[:, r:r + 1], ident[0:SPT, 0:SPT])
                            last.then_inc(s_row, 1)
                            eng.wait_ge(s_scan, 2 * back + 2)
                            eng.matmul(ps_m[0:SPT, back:back + 1], row[:, R_T, :], one1[:, :], start=True, stop=True).then_inc(s_row, 1)
                        eng.wait_ge(s_scan, 5)
                        for q in range(SW // 4):
                            eng.wait_ge(s_c, SW // 4) if q < 4 else eng.wait_ge(s_mc, q - 3)
                            for k in range(4):
                                last = eng.transpose(ps_a[q % 4][:, k * P:k * P + SPT], run[:, (q * 4 + k) * P:(q * 4 + k + 1) * P], ident[0:SPT, 0:SPT])
                            last.then_inc(s_mt, 1)

                    @block.scalar
                    def _(eng):
                        for q in range(SW // 4):
                            eng.wait_ge(s_t, q + 1)
                            eng.activation(run[:, q * 4 * P:(q + 1) * 4 * P], ps_a[q % 4][0:SPT, :], ACT.Copy).then_inc(s_c, 1)
                        for q in range(SW // 4):
                            eng.wait_ge(s_d, q + 1)
                            eng.activation(columns(weights, q), columns(weights, q), ACT.Exp)

        with ExitStack() as st:
            HA = 3
            ring = sb(st, "ring_g", [P, RING, D])
            hot = sb(st, "hot_g", [P, 2 * HOTS, P])
            msg = sb(st, "msg", [P, 2 * HOTS, D + H])
            zeros = sb(st, "zeros", [P, 512], BF16)
            rden = sb(st, "rden", [P, H])
            res = sb(st, "res_l", [P, 2, D])
            o = sb(st, "o", [P, 2, D])
            ps_sum = pb(st, "ps_sum_g", 2048)
            rows_landed = sem(st, "rows_landed_g")
            visited = sem(st, "visited_g")
            idx_ready = sem(st, "idx_ready_g")
            asked = sem(st, "asked_g")
            hot_ready = sem(st, "hot_ready_g")
            scaled_a = sem(st, "scaled_a")
            scaled_v = sem(st, "scaled_v")
            s_r = sem(st, "s_r")
            s_out = sem(st, "s_out")
            s_end = sem(st, "s_end")
            s_zero = sem(st, "s_zero_g")
            s_st = sem(st, "s_st_g")
            s_stored = sem(st, "s_stored_g")

            def sums(par, c0, n):
                return ps_sum[:, par * 1024 + c0:par * 1024 + c0 + n]

            def row_at(t, g, k, slots, c0, n):
                return t[:, ds((g * 2) % slots + k, 1), c0:c0 + n].rearrange("p s c -> p (s c)")
            with nc.Block() as block:

                @block.gpsimd
                def _(eng):
                    gather_rows(eng, table3, [scaled_a, scaled_v], idx_ready, asked, lambda k: ring[:, k, :])

                @block.sync
                def _(eng):
                    relay_landed(eng, 2, rows_landed)

                @block.scalar
                def _(eng):
                    eng.sem_inc(scaled_a, RING // 2)

                    def scale(g):
                        eng.wait_ge(rows_landed, g * 2 + 2)
                        eng.wait_ge(visited, g + 1)
                        for k in range(2):
                            for h in range(HA):
                                eng.activation(row_at(msg, g, k, 2 * HOTS, h * DH, DH), row_at(ring, g, k, RING, h * DH, DH), ACT.Copy,
                                               scale=weights[:, ds(g * 2 + k, 1), h:h + 1].rearrange("p a h -> p (a h)"))
                        eng.activation(msg[:, ds((g * 2) % (2 * HOTS), 2), D:D + H], weights[:, ds(g * 2, 2), :], ACT.Copy).then_inc(scaled_a, 1)

                    def step(j, par):
                        if has(j, 1):
                            jj = j - 1
                            if not isinstance(j, int) or jj >= 1:
                                eng.wait_ge(s_r, jj * 16)
                                eng.wait_ge(s_out, jj + 1)
                            eng.dma_start(res[:, 1 - par:2 - par, :], by_tile(res_table)[:, ds(jj, 1), :]).then_inc(s_r, 16)
                        if has(j, 0):
                            visits_of(eng, j, lambda g: scale(g + AHEAD))
                        if has(j, 1):
                            if not isinstance(j, int) or jj >= 1:
                                eng.wait_ge(s_st, jj * 16)
                                eng.sem_inc(s_stored, 1)
                            eng.wait_ge(s_out, jj + 3)
                            if isinstance(j, int) and jj == NT - 1:
                                eng.dma_start(out[jj * P:N, :], o[0:LAST, 1 - par, :]).then_inc(s_st, 16)
                            else:
                                whole = out[0:(NT - 1) * P, :].rearrange("(t p) d -> p t d", p=P)
                                eng.dma_start(whole[:, ds(jj, 1), :], o[:, 1 - par:2 - par, :]).then_inc(s_st, 16)
                    for g in range(AHEAD):
                        scale(g)
                    staged(eng, 3, step)
                    eng.wait_ge(s_st, NT * 16)

                @block.tensor
                def _(eng):
                    eng.sem_inc(visited, HOTS)
                    eng.wait_ge(s_zero, 1)

                    def step(j, par):
                        if has(j, 0):
                            if not isinstance(j, int) or j >= 2:
                                eng.wait_ge(s_out, j + 1)
                            for c0, n in ((0, 512), (512, D + H - 512)):
                                eng.matmul(sums(par, c0, n), zeros[:, 0:P], zeros[:, 0:n], start=True, stop=True)

                            def visit(g):
                                eng.wait_ge(scaled_a, g + RING // 2 + 1)
                                eng.wait_ge(scaled_v, g + RING // 2 + 1)
                                eng.wait_ge(hot_ready, g + 1)

                                def products(at):
                                    for k in range(at * 2, at * 2 + 2):
                                        for c0, n in ((0, 512), (512, D + H - 512)):
                                            last = eng.matmul(sums(par, c0, n), hot[:, k, :], msg[:, k, c0:c0 + n],
                                                              start=False, stop=True, skip_group_check=True)
                                    last.then_inc(visited, 1)
                                by_pair(eng, g, products)
                            visits_of(eng, j, visit)
                    staged(eng, 3, step)

                @block.vector
                def _(eng):
                    eng.memset(zeros[:, :], 0.0).then_inc(s_zero, 1)
                    eng.sem_inc(s_out, 2)

                    eng.sem_inc(scaled_v, RING // 2)

                    def scale_and_hot(g):
                        eng.wait_ge(rows_landed, g * 2 + 2)
                        eng.wait_ge(visited, g + 1)
                        to, of = (t[:, ds((g * 2) % slots, 2), HA * DH:D].rearrange("p a (h d) -> p a h d", d=DH) for t, slots in ((msg, 2 * HOTS), (ring, RING)))
                        eng.tensor_tensor(to, of, weights[:, ds(g * 2, 2), HA:H].unsqueeze(3).to_broadcast([P, 2, H - HA, DH]), ALU.mult).then_inc(scaled_v, 1)
                        one_hots(eng, g, hot).then_inc(hot_ready, 1)

                    def step(j, par):
                        if has(j, 0):
                            visits_of(eng, j, scale_and_hot)
                        if has(j, 1):
                            jj = j - 1
                            end = eng.value_load(pair0[0:1, ds(jj + 1, 1)], min_val=1, max_val=V // 2)
                            eng.wait_ge(visited, end + HOTS)
                            o_ = o[:, 1 - par:2 - par, :].rearrange("p a d -> p (a d)")
                            eng.tensor_scalar(rden[:, :], sums(1 - par, D, H), 0.5, None, ALU.max).then_inc(s_end, 1)
                            eng.wait_ge(s_end, jj * 4 + 1)
                            eng.reciprocal(rden[:, :], rden[:, :]).then_inc(s_end, 1)
                            eng.wait_ge(s_end, jj * 4 + 2)
                            if not isinstance(j, int) or jj >= 2:
                                eng.wait_ge(s_stored, jj - 1)
                            eng.tensor_tensor(o_.rearrange("p (h d) -> p h d", d=DH), sums(1 - par, 0, D).rearrange("p (h d) -> p h d", d=DH),
                                              rden[:, :].unsqueeze(2).to_broadcast([P, H, DH]), ALU.mult).then_inc(s_end, 1)
                            eng.wait_ge(s_end, jj * 4 + 3)
                            eng.wait_ge(s_r, jj * 16 + 16)
                            eng.tensor_tensor(o_, o_, res[:, 1 - par:2 - par, :].rearrange("p a d -> p (a d)"), ALU.add).then_inc(s_end, 1)
                            eng.wait_ge(s_end, jj * 4 + 4)
                            eng.scalar_tensor_tensor(out=o_, in0=o_, scalar=0.0, in1=nodes[:, ds(jj, 1), :].rearrange("p a d -> p (a d)"), op0=ALU.max, op1=ALU.add).then_inc(s_out, 1)
                    staged(eng, 3, step)


def kernel(**inputs):
    import numpy as np
    import concourse.bacc as bacc
    from concourse.bass_utils import run_bass_kernel_spmd

    nc = bacc.Bacc("TRN2", target_bir_lowering=False, num_devices=1)
    given = {k: np.asarray(v) for k, v in inputs.items()}
    laid = {
        "x": given["x"], "src": given["src"], "dst": given["dst"],
        "w1t": given["L0_gnn_W1"].T, "b1": given["L0_gnn_b1"],
        "w2t": given["L0_gnn_W2"].T, "b2": given["L0_gnn_b2"],
        "wfc": given["L1_gnn_W_fc"], "wfct": given["L1_gnn_W_fc"].T,
        "attn_lt": given["L1_gnn_attn_l"].T, "attn_rt": given["L1_gnn_attn_r"].T,
        "wrest": given["L1_gnn_W_res"].T,
    }
    arrays, args = {}, []
    for name, a in laid.items():
        a = np.ascontiguousarray(a)
        arrays[f"in_{name}"] = a
        args.append(nc.dram_tensor(f"in_{name}", a.shape, mybir.dt.from_np(a.dtype), kind="ExternalInput").ap())
    args.append(nc.dram_tensor("out_x", (N, D), F32, kind="ExternalOutput").ap())
    gnn_kernel(nc, *args)
    r = run_bass_kernel_spmd(nc, [arrays], core_ids=[0])
    return r.results[0]["out_x"]
```
